# Optimizing a Trainium2 kernel written in Bass

```python
import numpy as np
import jax
import jax.numpy as jnp

def _softmax(x, axis=-1):
    return jax.nn.softmax(x, axis=axis)

def _gelu(x):
    return jax.nn.gelu(x, approximate=True)

def _silu(x):
    return jax.nn.silu(x)

def _sigmoid(x):
    return jax.nn.sigmoid(x)

def _layernorm(x, axis=-1, eps=1e-05):
    m = jnp.mean(x, axis=axis, keepdims=True)
    v = jnp.var(x, axis=axis, keepdims=True)
    return (x - m) / jnp.sqrt(v + eps)

def _scatter_add(tgt, idx, src, axis=0):
    return tgt.at[idx].add(src)

def _segment_sum(src, seg, n):
    return jax.ops.segment_sum(src, seg, n)
kernel_name = 'mk_xattn_seq_d2_seqx_r4_5b1a90'

def setup_inputs(seed: int=0):
    np.random.seed(seed)
    _w = jnp.asarray

    def _rec_inputs():
        import jax
        import jax.numpy as jnp
        _rk = jax.random.key(seed)
        x = -0.0001108 + 0.9999 * jax.random.normal(jax.random.fold_in(_rk, 1), (4, 1024, 320), jnp.float32)
        _lenS = 1024 - jax.random.randint(jax.random.fold_in(_rk, 7), (4,), 0, max(1, 1024 // 4) + 1, jnp.int32)
        _lenS2 = 64 - jax.random.randint(jax.random.fold_in(_rk, 8), (4,), 0, max(1, 64 // 4) + 1, jnp.int32)
        _ctx_768P = jax.random.normal(jax.random.fold_in(_rk, 11), (4, 16, 192), jnp.float32)
        _ctx_768c = jax.random.dirichlet(jax.random.fold_in(_rk, 511), 0.3 * jnp.ones((16,), jnp.float32), (4, 64))
        _ctx_768t = jnp.einsum('bsk,bkd->bsd', _ctx_768c, _ctx_768P)
        _ctx_768t = _ctx_768t * jax.lax.rsqrt(jnp.mean(jnp.square(_ctx_768t)) + 1e-12) * 0.953939
        ctx_768 = 0.00114861 + 0.999593 * (_ctx_768t + 0.3 * jax.random.normal(jax.random.fold_in(_rk, 611), (4, 64, 192), jnp.float32))
        return (x, ctx_768)
    x, ctx_768 = _rec_inputs()

    def _L0_xattn_setup():
        import jax, jax.numpy as jnp
        import numpy as np
        HEADS = 20
        NUM_AOE = 16
        NUM_IP = 16
        key = jax.random.key(seed)
        ks = jax.random.split(key, 7)
        B, Sq, H = (8, 1024, 320)
        Skv, C = (109, 192)
        scale = 0.02
        return {'hidden_states': jax.random.normal(ks[0], (B, Sq, H), jnp.float32), 'encoder_hidden_states': jax.random.normal(ks[1], (B, Skv, C), jnp.float32), 'Wq': jax.random.normal(ks[2], (H, H), jnp.float32) * scale, 'Wk': jax.random.normal(ks[3], (C, H), jnp.float32) * scale, 'Wv': jax.random.normal(ks[4], (C, H), jnp.float32) * scale, 'Wo': jax.random.normal(ks[5], (H, H), jnp.float32) * scale, 'bo': jnp.zeros((H,), jnp.float32)}
    _L0_xattn_all = _L0_xattn_setup()
    _L0_xattn_in = {k: v for k, v in _L0_xattn_all.items() if k in ('Wq', 'Wk', 'Wv', 'Wo', 'bo')}
    del _L0_xattn_all

    def _L1_xattn_setup():
        import jax, jax.numpy as jnp
        import numpy as np
        HEADS = 8
        NUM_TOKENS = 4
        CROSS_ATTENTION_DIM = 192

        def _mha(q, k, v, heads=HEADS):
            B, Sq, H = q.shape
            Sk = k.shape[1]
            d = H // heads
            qh = q.reshape(B, Sq, heads, d).transpose(0, 2, 1, 3)
            kh = k.reshape(B, Sk, heads, d).transpose(0, 2, 1, 3)
            vh = v.reshape(B, Sk, heads, d).transpose(0, 2, 1, 3)
            scores = jnp.einsum('bhqd,bhkd->bhqk', qh, kh) * jnp.asarray(d, q.dtype) ** (-0.5)
            probs = jax.nn.softmax(scores, axis=-1)
            out = jnp.einsum('bhqk,bhkd->bhqd', probs, vh)
            return out.transpose(0, 2, 1, 3).reshape(B, Sq, H)
        key = jax.random.key(seed)
        ks = jax.random.split(key, 10)
        B, S, H, CAD, T = (4, 256, 320, CROSS_ATTENTION_DIM, NUM_TOKENS)
        sc = 0.02
        return {'hidden_states': jax.random.normal(ks[0], (B, S, H), jnp.float32), 'encoder_hidden_states': jax.random.normal(ks[1], (B, 77 + T, CAD), jnp.float32), 'Wq': jax.random.normal(ks[2], (H, H), jnp.float32) * sc, 'Wk': jax.random.normal(ks[3], (CAD, H), jnp.float32) * sc, 'Wv': jax.random.normal(ks[4], (CAD, H), jnp.float32) * sc, 'Wq_ca': jax.random.normal(ks[5], (T, H), jnp.float32) * sc, 'Wk_ca': jax.random.normal(ks[6], (CAD, H), jnp.float32) * sc, 'Wv_ca': jax.random.normal(ks[7], (CAD, H), jnp.float32) * sc, 'Wout': jax.random.normal(ks[8], (H, H), jnp.float32) * sc, 'b_out': jnp.zeros((H,), jnp.float32)}
    _L1_xattn_all = _L1_xattn_setup()
    _L1_xattn_in = {k: v for k, v in _L1_xattn_all.items() if k in ('Wq', 'Wk', 'Wv', 'Wq_ca', 'Wk_ca', 'Wv_ca', 'Wout', 'b_out')}
    del _L1_xattn_all
    return {'x': x, 'ctx_768': ctx_768, 'L0_xattn_Wq': _L0_xattn_in['Wq'], 'L0_xattn_Wk': _L0_xattn_in['Wk'], 'L0_xattn_Wv': _L0_xattn_in['Wv'], 'L0_xattn_Wo': _L0_xattn_in['Wo'], 'L0_xattn_bo': _L0_xattn_in['bo'], 'L1_xattn_Wq': _L1_xattn_in['Wq'], 'L1_xattn_Wk': _L1_xattn_in['Wk'], 'L1_xattn_Wv': _L1_xattn_in['Wv'], 'L1_xattn_Wq_ca': _L1_xattn_in['Wq_ca'], 'L1_xattn_Wk_ca': _L1_xattn_in['Wk_ca'], 'L1_xattn_Wv_ca': _L1_xattn_in['Wv_ca'], 'L1_xattn_Wout': _L1_xattn_in['Wout'], 'L1_xattn_b_out': _L1_xattn_in['b_out']}

def reference(x, ctx_768, L0_xattn_Wq, L0_xattn_Wk, L0_xattn_Wv, L0_xattn_Wo, L0_xattn_bo, L1_xattn_Wq, L1_xattn_Wk, L1_xattn_Wv, L1_xattn_Wq_ca, L1_xattn_Wk_ca, L1_xattn_Wv_ca, L1_xattn_Wout, L1_xattn_b_out):
    import jax
    import jax.numpy as jnp

    def _L0_xattn_ref(hidden_states, encoder_hidden_states, Wq, Wk, Wv, Wo, bo):
        import jax, jax.numpy as jnp
        import numpy as np
        HEADS = 20
        NUM_AOE = 16
        NUM_IP = 16
        B, Sq, H = hidden_states.shape
        Skv = encoder_hidden_states.shape[1]
        head_dim = H // HEADS
        residual = hidden_states
        q = (hidden_states @ Wq).reshape(B, Sq, HEADS, head_dim).transpose(0, 2, 1, 3)
        k = (encoder_hidden_states @ Wk).reshape(B, Skv, HEADS, head_dim).transpose(0, 2, 1, 3)
        v = (encoder_hidden_states @ Wv).reshape(B, Skv, HEADS, head_dim).transpose(0, 2, 1, 3)
        scores = jnp.einsum('bhqd,bhkd->bhqk', q, k) / jnp.sqrt(jnp.asarray(head_dim, q.dtype))
        probs = jax.nn.softmax(scores, axis=-1)
        scale_aoe = jnp.asarray(1.0, probs.dtype)
        scale_ip = jnp.asarray(1.0, probs.dtype)
        idx = jnp.arange(Skv)
        scale_vector = jnp.where(idx < NUM_AOE, scale_aoe, 1.0)
        scale_vector = jnp.where(idx >= Skv - NUM_IP, scale_vector * scale_ip, scale_vector)
        probs = probs * scale_vector
        probs = probs / probs.sum(axis=-1, keepdims=True)
        out = jnp.einsum('bhqk,bhkd->bhqd', probs, v)
        out = out.transpose(0, 2, 1, 3).reshape(B, Sq, H)
        out = out @ Wo + bo
        return out + residual

    def _L1_xattn_ref(hidden_states, encoder_hidden_states, Wq, Wk, Wv, Wq_ca, Wk_ca, Wv_ca, Wout, b_out):
        import jax, jax.numpy as jnp
        import numpy as np
        HEADS = 8
        NUM_TOKENS = 4
        CROSS_ATTENTION_DIM = 192

        def _mha(q, k, v, heads=HEADS):
            B, Sq, H = q.shape
            Sk = k.shape[1]
            d = H // heads
            qh = q.reshape(B, Sq, heads, d).transpose(0, 2, 1, 3)
            kh = k.reshape(B, Sk, heads, d).transpose(0, 2, 1, 3)
            vh = v.reshape(B, Sk, heads, d).transpose(0, 2, 1, 3)
            scores = jnp.einsum('bhqd,bhkd->bhqk', qh, kh) * jnp.asarray(d, q.dtype) ** (-0.5)
            probs = jax.nn.softmax(scores, axis=-1)
            out = jnp.einsum('bhqk,bhkd->bhqd', probs, vh)
            return out.transpose(0, 2, 1, 3).reshape(B, Sq, H)
        residual = hidden_states
        unet_size = residual.shape[1]
        end_pos = encoder_hidden_states.shape[1] - NUM_TOKENS
        enc = encoder_hidden_states[:, :end_pos, :]
        ca = encoder_hidden_states[:, end_pos:, :]
        query = hidden_states @ Wq
        keyt = enc @ Wk
        valt = enc @ Wv
        hs = _mha(query, keyt, valt)
        ca_q1 = jnp.einsum('btc,th->bch', ca, Wq_ca)
        indices = np.linspace(0, CROSS_ATTENTION_DIM - 1, unet_size).astype(np.int64)
        ca_q1 = ca_q1[:, indices, :]
        ca_hs1 = _mha(ca_q1, residual, residual)
        ca_q2 = ca_hs1 @ Wq
        ca_k2 = ca @ Wk_ca
        ca_v2 = ca @ Wv_ca
        ca_hs2 = _mha(ca_q2, ca_k2, ca_v2)
        out = hs + ca_hs2
        out = out @ Wout + b_out
        out = out + residual
        return out
    x = _L0_xattn_ref(x, ctx_768, L0_xattn_Wq, L0_xattn_Wk, L0_xattn_Wv, L0_xattn_Wo, L0_xattn_bo)
    x = _L1_xattn_ref(x, ctx_768, L1_xattn_Wq, L1_xattn_Wk, L1_xattn_Wv, L1_xattn_Wq_ca, L1_xattn_Wk_ca, L1_xattn_Wv_ca, L1_xattn_Wout, L1_xattn_b_out)
    return x

_drawn_inputs = setup_inputs


def setup_inputs(seed=0):
    import zlib

    import numpy as np

    out = dict(_drawn_inputs(seed))
    spreads = {'L0_xattn_bo': (0.0, 0.1), 'L1_xattn_b_out': (0.0, 0.1)}
    factors = {'L0_xattn_Wq': 8.0,
     'L0_xattn_Wk': 8.0,
     'L1_xattn_Wq': 8.0,
     'L1_xattn_Wk': 8.0,
     'L1_xattn_Wq_ca': 39.426,
     'L1_xattn_Wk_ca': 8.0}
    for name, (base, spread) in spreads.items():
        noise = np.random.default_rng([zlib.crc32(name.encode()), seed]).standard_normal(out[name].shape)
        drawn = base * np.exp(spread * noise) if base else spread * noise
        out[name] = jnp.asarray(drawn.astype(out[name].dtype))
    for name, factor in factors.items():
        out[name] = (out[name] * factor).astype(out[name].dtype)
    return out
```

```python
from contextlib import ExitStack

import concourse.bass as bass
from concourse import mybir

F32 = mybir.dt.float32
F32R = mybir.dt.float32r
ALU = mybir.AluOpType
ACT = mybir.ActivationFunctionType
AX = mybir.AxisListType

B, S, F, C, NK = 4, 1024, 320, 192, 64
P = 128
HALF = 512
H0, D0 = 20, 16
H1, D1 = 8, 40
T = 4
K1 = NK - T
PAIRS0, PAIRS1 = H0 // 2, H1 // 2
GROUP = 4
QT = HALF // P
KT = S // P
SCALE0 = float(D0) ** -0.5
SCALE1 = float(D1) ** -0.5
KC = C // 2
HC = H1 * C
PC = 2 * C
HT = H1 * T
CH = C // 2 + 1
CH0 = [0, C - CH]
ROWS1 = [3 * D1, 3 * D1, 2 * D1]
HEADS1 = [3, 3, 2]
COMBOS = [(0, 0), (0, 1), (1, 1), (1, 2), (2, 3)]
FT = [P, P, F - 2 * P]
QS0_ROWS = 3 * 32 + H0
SLOTS = 4


class Ring:

    def __init__(self, names, banks, full, free):
        self.banks, self.full, self.free = banks, full, free
        self.names = list(names)
        assert len(self.names) % len(banks) == 0, len(self.names)
        self.per = len(self.names) // len(banks)
        self.at = {n: i for i, n in enumerate(self.names)}

    def bank(self, *name):
        return self.banks[self.at[name] % len(self.banks)]

    def wait_free(self, eng, b, *name):
        i = self.at[name]
        eng.wait_ge(self.free[i % len(self.banks)], b * self.per + (i // len(self.banks) + 1))

    def filled(self, ins, *name):
        ins.then_inc(self.full[self.at[name] % len(self.banks)], 1)

    def wait_full(self, eng, b, *name):
        i = self.at[name]
        eng.wait_ge(self.full[i % len(self.banks)], b * self.per + (i // len(self.banks) + 1))

    def read(self, ins, *name):
        ins.then_inc(self.free[self.at[name] % len(self.banks)], 1)

    def wait_read(self, eng, b, *name):
        i = self.at[name]
        eng.wait_ge(self.free[i % len(self.banks)], b * self.per + (i // len(self.banks) + 2))

    def wait_before(self, eng, b, s, *name):
        if s:
            self.wait_read(eng, b, *name)
        else:
            eng.wait_ge(self.free[(len(self.names) - 1) % len(self.banks)], b * self.per + 1)


def ring0_order():
    for s in range(2):
        yield from (("q", s, t) for t in range(3))
        for qp in range(QT // 2):
            yield from (("max", s, 2 * qp + i, t) for i in range(2) for t in range(2))
            yield ("max2", s, qp)
        yield ("maxT", s)
        for t in range(3):
            yield from (("sT", s, p) for p in range(GROUP * t, min(GROUP * t + GROUP, PAIRS0)))
            yield ("pv", s, t)
        yield from (("rec", s, t) for t in range(3))
        yield from (("wo", s, t) for t in range(3))


def ring1_order():
    for s in range(2):
        yield from (("q", s, t) for t in range(3))
        yield from (("xn", s, qt) for qt in range(QT))
        yield from (("max", s, qt) for qt in range(QT))
        yield ("maxT", s)
        yield from (("sT", s, p) for p in range(PAIRS1))
        yield from (("pv", s, t) for t in range(3))
        yield from (("rec", s, t) for t in range(3))
        yield from (("wo", s, t) for t in range(3))
    yield from (("cmax", m, s) for m in range(HC // P) for s in range(2))
    yield ("cmaxT",)
    yield from (("csT", p, kt) for p in range(PAIRS1) for kt in range(KT))
    yield from (("cnat", c) for c in range(2))
    yield from (("cnT", c) for c in range(2))
    yield ("cs3",)
    yield from (("cexp", s) for s in range(2))
    yield from (("fin", s, t) for s in range(2) for t in range(3))


def prologue(nc, a, scr, w):
    with ExitStack() as ctx:
        def sb(name, shape, dt=F32):
            return ctx.enter_context(nc.sbuf_tensor(name, shape, dt))

        def sem(name):
            return ctx.enter_context(nc.semaphore(name))

        raw = {k: sb(f"pro_{k}", list(a[k].shape)) for k in
               ("ctxD", "Wk0", "Wk1", "Wv0", "Wv1", "Wkca", "Wvca", "Wq1T", "W2", "mKB0", "mKB1", "m8", "mV0",
                "mV1", "ones0", "ones1", "car", "Wq0", "Wo0", "W1", "EX")}
        CAS = sb("pCAS", [96, HC], F32R)
        kT0H, kT0L = sb("kT0H", [P, 3, B, NK], F32R), sb("kT0L", [P, 3, B, NK], F32R)
        kT1H, kT1L = sb("kT1H", [P, 3, B, NK], F32R), sb("kT1L", [P, 3, B, NK], F32R)
        k3bd, v3bd = sb("k3bd", [P, 3, B, H1, T]), sb("v3bd", [P, 3, B, H1, T])
        KB0H, KB0L = sb("pKB0H", [P, 3, 8, NK], F32R), sb("pKB0L", [P, 3, 8, NK], F32R)
        KB1H, KB1L = sb("pKB1H", [P, 3, 3, NK], F32R), sb("pKB1L", [P, 3, 3, NK], F32R)
        V0, V1 = sb("pV0", [P, F]), sb("pV1", [P, len(COMBOS), P])
        A3 = sb("pA3", [P, 3, B, HT])
        VWH, VWL = sb("pVWH", [HT, F], F32R), sb("pVWL", [HT, F], F32R)
        onesr0, onesr1 = sb("onesr0", [H0, PAIRS0, P], F32R), sb("onesr1", [H1, PAIRS1, 2, P], F32R)
        zero1 = sb("zero1", [P, PAIRS1, 2, P])
        bank = [ctx.enter_context(nc.psum_tensor(f"pbank{i}", [P, HALF], F32)) for i in range(4)]
        loaded, filled, read = sem("pro_loaded"), sem("pro_filled"), sem("pro_read")
        own, const_ready, zeroed = sem("pro_dve_done"), sem("pro_const_ready"), sem("pro_zeroed")
        weights_hi = sem("pro_weights_hi")
        stored, blocks_out = sem("pro_stored"), sem("pro_blocks_out")
        stores = 1 + 3 * PAIRS0 + 1 + 3 * H1 + 3 + 3 + 1
        MK1 = (3 * D1, 3 * D1, P)
        block = ctx.enter_context(nc.Block())

        @block.sync
        def _(sp):
            for k in raw:
                sp.dma_start(raw[k][:], a[k]).then_inc(loaded, 16)
            sp.wait_ge(zeroed, 1)
            for b in range(B):
                sp.dma_start(scr["KS1"][b], zero1[:]).then_inc(stored, 16)
            sp.wait_ge(const_ready, 2)
            for b in range(B):
                sp.dma_start(scr["KS0"][b, 96:96 + H0], onesr0[:].bitcast(F32)).then_inc(stored, 16)
            sp.wait_ge(stored, 16 * 2 * B)
            for b in range(B):
                sp.dma_start(scr["KS1"][b, 3 * D1:P], onesr1[:].bitcast(F32)).then_inc(stored, 16)
            for b in range(B):
                sp.wait_ge(read, 15 + 3 * (b + 1))
                sp.dma_start(scr["KB0"][b], KB0H[:].bitcast(F32)).then_inc(blocks_out, 16)
                for seg, src in enumerate((KB0H, KB0H, KB0L)):
                    for p in range(PAIRS0):
                        t, j = p // GROUP, p % GROUP
                        sp.dma_start(scr["KS0"][b, 32 * seg:32 * seg + 32, p, :],
                                     src[32 * j:32 * j + 32, t, 2 * j:2 * j + 2, :].bitcast(F32)
                                     .rearrange("p a k -> p (a k)")).then_inc(blocks_out, 16)
                sp.dma_start(scr["KB1"][b], KB1H[:].bitcast(F32)).then_inc(blocks_out, 16)
                for seg, src in enumerate((KB1H, KB1H, KB1L)):
                    for h in range(H1):
                        t, j = h // 3, h % 3
                        sp.dma_start(scr["KS1"][b, D1 * seg:D1 * seg + D1, h // 2, h % 2,
                                                NK * (h % 2):NK * (h % 2) + NK],
                                     src[D1 * j:D1 * j + D1, t, j, :].bitcast(F32)).then_inc(blocks_out, 16)
                sp.dma_start(scr["V0"][b], V0[:]).then_inc(blocks_out, 16)
                sp.dma_start(scr["V1"][b], V1[:]).then_inc(blocks_out, 16)
                sp.dma_start(scr["A3"][b], A3[:, :, b, :]).then_inc(blocks_out, 16)
                for seg, src in enumerate((VWH, VWH, VWL)):
                    sp.dma_start(scr["VW"][b, HT * seg:HT * seg + HT], src[:].bitcast(F32)).then_inc(blocks_out, 16)
                sp.dma_start(scr["CAS"][b], CAS[:].bitcast(F32)).then_inc(blocks_out, 16)
                sp.wait_ge(blocks_out, 16 * stores * (b + 1))
            sp.wait_ge(stored, 16 * 3 * B)

        @block.gpsimd
        def _(pool):
            nc.gpsimd.memset(zero1[:], 0.0).then_inc(zeroed, 1)

        @block.scalar
        def _(act):
            act.wait_ge(loaded, 16 * len(raw))
            for k in ("Wq0", "Wo0", "W1", "W2"):
                nc.scalar.copy(w[k + "H"][:], raw[k][:]).then_inc(weights_hi, 1)
            nc.scalar.copy(w["EX"][:], raw["EX"][:])

        @block.tensor
        def _(pe):
            pe.wait_ge(loaded, 16 * len(raw))
            fills = [0]

            def fill(rows, cols, parts):
                n = fills[0]
                if n >= 4:
                    pe.wait_ge(read, n - 3)
                for i, (lhsT, rhs) in enumerate(parts):
                    last = nc.tensor.matmul(bank[n % 4][0:rows, 0:cols], lhsT, rhs, start=(i == 0),
                                            stop=(i == len(parts) - 1))
                last.then_inc(filled, 1)
                fills[0] += 1

            keys = [raw["ctxD"][:, k, :, 0:NK] for k in range(2)]
            toks = [raw["ctxD"][:, k, :, K1:NK] for k in range(2)]
            for t in range(3):
                fill(FT[t], B * NK, [(raw["Wk0"][:, k, P * t:P * t + FT[t]], keys[k]) for k in range(2)])
            for t in range(3):
                fill(MK1[t], B * NK, [(raw["Wk1"][:, k, 120 * t:120 * t + MK1[t]], keys[k]) for k in range(2)])
            for name in ("Wkca", "Wvca"):
                for t in range(3):
                    fill(ROWS1[t], B * T, [(raw[name][:, k, 120 * t:120 * t + ROWS1[t]], toks[k]) for k in range(2)])
            pe.wait_ge(read, 12)
            for t in range(3):
                fill(FT[t], B * HT, [(raw["Wq1T"][0:ROWS1[k], k, P * t:P * t + FT[t]],
                                      k3bd[0:ROWS1[k], k].rearrange("p b h t -> p (b h t)")) for k in range(3)])
            for b in range(B):
                for name in ("Wv0", "Wv1"):
                    fill(P, F, [(raw["ctxD"][:, k, b, :], raw[name][:, k, :]) for k in range(2)])
                fill(HT, F, [(v3bd[0:ROWS1[k], k, b].rearrange("p h t -> p (h t)"), raw["W2"][0:ROWS1[k], k, :])
                             for k in range(3)])

        @block.vector
        def _(dve):
            done = [0]
            fills = [0]

            def link(ins):
                ins.then_inc(own, 1)
                done[0] += 1
                dve.wait_ge(own, done[0])

            def next_fill():
                fills[0] += 1
                dve.wait_ge(filled, fills[0])
                return bank[(fills[0] - 1) % 4]

            for x in (kT0H, kT0L, kT1H, kT1L):
                link(nc.vector.memset(x[:].bitcast(F32), 0.0))
            link(nc.vector.memset(V1[:], 0.0))
            link(nc.vector.memset(A3[:], 0.0))
            dve.wait_ge(loaded, 16 * len(raw))
            for i, k in enumerate(("Wq0", "Wo0", "W1", "W2")):
                dve.wait_ge(weights_hi, i + 1)
                nc.vector.tensor_tensor(w[k + "L"][:], raw[k][:], w[k + "H"][:].bitcast(F32), ALU.subtract)
            nc.vector.tensor_copy(onesr0[:], raw["ones0"][:]).then_inc(const_ready, 1)
            nc.vector.tensor_copy(onesr1[:], raw["ones1"][:]).then_inc(const_ready, 1)
            for hi, lo, rows in ((kT0H, kT0L, FT), (kT1H, kT1L, MK1)):
                for t in range(3):
                    r = rows[t]
                    ps = next_fill()[0:r, 0:B * NK]
                    h = hi[0:r, t].rearrange("p b k -> p (b k)")
                    link(nc.vector.tensor_copy(h, ps))
                    nc.vector.tensor_tensor(lo[0:r, t].rearrange("p b k -> p (b k)"), ps, h.bitcast(F32),
                                            ALU.subtract).then_inc(read, 1)
            for dst in (k3bd, v3bd):
                for t in range(3):
                    r = ROWS1[t]
                    bk = next_fill()[0:r, 0:B * T].rearrange("p (b t) -> p b t", b=B)
                    for b in range(B):
                        last = nc.vector.tensor_tensor(
                            dst[0:r, t, b], bk[:, b].unsqueeze(1).to_broadcast([r, H1, T]),
                            raw["m8"][0:r, t].unsqueeze(2).to_broadcast([r, H1, T]), ALU.mult)
                    last.then_inc(read, 1)
            for t in range(3):
                r = FT[t]
                ps = next_fill()[0:r, 0:B * HT].rearrange("p (b h) -> p b h", b=B)
                nc.vector.tensor_copy(A3[0:r, t], ps).then_inc(read, 1)
            dve.wait_ge(read, 15)
            for b in range(B):
                if b >= 1:
                    dve.wait_ge(blocks_out, 16 * stores * b)
                link(nc.vector.tensor_copy(CAS[:], raw["car"][:, b]))
                nc.vector.tensor_tensor(CAS[64:96], raw["car"][64:96, b], CAS[64:96].bitcast(F32), ALU.subtract)
                for dst, src in ((KB0H, kT0H), (KB0L, kT0L)):
                    for t in range(3):
                        nc.vector.tensor_tensor(dst[:, t], src[:, t, b].bitcast(F32).unsqueeze(1).to_broadcast([P, 8, NK]),
                                                raw["mKB0"][:], ALU.mult)
                for dst, src in ((KB1H, kT1H), (KB1L, kT1L)):
                    for t in range(3):
                        nc.vector.tensor_tensor(dst[:, t], src[:, t, b].bitcast(F32).unsqueeze(1).to_broadcast([P, 3, NK]),
                                                raw["mKB1"][:, t], ALU.mult)
                nc.vector.tensor_tensor(V0[:], next_fill()[:, 0:F], raw["mV0"][:], ALU.mult).then_inc(read, 1)
                bk = next_fill()
                for i, (t, _) in enumerate(COMBOS):
                    n = ROWS1[t]
                    last = nc.vector.tensor_tensor(V1[:, i, 0:n], bk[:, 120 * t:120 * t + n], raw["mV1"][:, i, 0:n],
                                                   ALU.mult)
                last.then_inc(read, 1)
                bk = next_fill()
                link(nc.vector.tensor_copy(VWH[:], bk[0:HT, 0:F]))
                nc.vector.tensor_tensor(VWL[:], bk[0:HT, 0:F], VWH[:].bitcast(F32), ALU.subtract).then_inc(read, 1)


def layers(nc, a, scr, w, out):
    with ExitStack() as ctx:
        def sb(name, shape, dt=F32):
            return ctx.enter_context(nc.sbuf_tensor(name, shape, dt))

        def sem(name):
            return ctx.enter_context(nc.semaphore(name))

        bank = [ctx.enter_context(nc.psum_tensor(f"bank{i}", [P, HALF], F32)) for i in range(8)]
        R0 = Ring(ring0_order(), bank[0:3], [sem(f"l0_bank{i}_full") for i in range(3)],
                  [sem(f"l0_bank{i}_read") for i in range(3)])
        R1 = Ring(ring1_order(), bank[4:7], [sem(f"l1_bank{i}_full") for i in range(3)],
                  [sem(f"l1_bank{i}_read") for i in range(3)])
        sums0, sums1 = bank[3], bank[7]

        WqH, WqL, WoH, WoL, W1H, W1L, W2H, W2L, EX = (
            w[k] for k in ("Wq0H", "Wq0L", "Wo0H", "Wo0L", "W1H", "W1L", "W2H", "W2L", "EX"))
        bo0, bo1 = sb("bo0_sb", [P, 3]), sb("bo1_sb", [P, 3])
        ident = sb("ident_sb", [P, P])
        OH0, OH1 = sb("OH0_sb", [P, PAIRS0, 32]), sb("OH1_sb", [P, PAIRS1, 32])
        E0, E1 = sb("E0_sb", [P, 3 * P]), sb("E1_sb", [P, 3 * P])
        KB0 = sb("KB0_sb", [P, 3, 8, NK], F32R)
        KS0 = sb("KS0_sb", [QS0_ROWS, PAIRS0, P], F32R)
        V0 = sb("V0_sb", [P, F])
        KB1 = sb("KB1_sb", [P, 3, 3, NK], F32R)
        KS1 = sb("KS1_sb", [P, PAIRS1, 2, P], F32R)
        V1 = sb("V1_sb", [P, len(COMBOS), P])
        A3 = sb("A3_sb", [P, 3, HT])
        VW = sb("VW_sb", [96, F], F32R)
        CAS = sb("CAS_sb", [97, HC], F32R)
        XH, XL = sb("XH", [P, 3, HALF], F32R), sb("XL", [P, 2, HALF], F32R)
        q0H, q0L = sb("q0H", [P, 3, HALF], F32R), sb("q0L", [P, 3, HALF])
        o0 = q0L
        QS0 = sb("QS0", [QS0_ROWS, 2 * GROUP, HALF], F32R)
        nmax0 = sb("nmax0", [P, QT, H0])
        nmaxT0 = sb("nmaxT0", [H0, HALF], F32R)
        P0 = sb("P0", [P, SLOTS, HALF])
        rec0 = sb("rec0", [P, P])
        x1T = sb("x1T", [P, 3, S])
        X1H, X1L = sb("X1H", [P, 3, HALF], F32R), sb("X1L", [P, 3, HALF], F32R)
        q1H, q1L = sb("q1H", [P, 3, HALF], F32R), sb("q1L", [P, 3, HALF])
        o1 = q1L
        QS1 = sb("QS1", [P, 2, 2, HALF], F32R)
        nmax1 = sb("nmax1", [P, QT, H1])
        nmaxT1 = sb("nmaxT1", [H1, HALF], F32R)
        P1 = sb("P1", [P, PAIRS1, HALF])
        rec1 = sb("rec1", [P, P])
        GS = sb("GS", [97, S], F32R)
        X1N = sb("X1N", [P, KT, H1, D1 + 1])
        cmax2, cmax = sb("cmax2", [P, HC // P, 2]), sb("cmax", [P, HC // P])
        cmaxT = sb("cmaxT", [HC // P, P], F32R)
        PCA = P1
        CO = sb("CO", [P, PAIRS1, C])
        crec = sb("crec", [CH, 2, H1])
        hs = sb("hs", [CH, 2, H1, D1])
        hsT = sb("hsT", [P, 2, 3, CH])
        m3, s3, r3 = sb("m3", [CH, 2, H1]), sb("s3", [CH, 2, H1]), sb("r3", [CH, 2, H1])
        d3, e3, p3 = sb("d3", [CH, 2, H1, T]), sb("e3", [CH, 2, H1, T]), sb("p3", [CH, 2, H1, T])
        P3 = sb("P3", [CH, 2, 3, HT], F32R)
        P3S = X1H

        const_here, const_set = sem("const_here"), sem("const_set")
        pack0_here, pack1_here, x_here = sem("pack0_here"), sem("pack1_here"), [sem(f"x_here{s}") for s in range(2)]
        x_hi, x_lo, q0_hi = sem("x_hi"), sem("x_lo"), sem("q0_hi")
        qs0_here = [sem(f"qs0_here{t}") for t in range(3)]
        sums0_done, sums0_read, o0_hi, o0_lo = sem("sums0_done"), sem("sums0_read"), sem("o0_hi"), sem("o0_lo")
        x1_hi, x1_lo, q1_hi = sem("x1_hi"), sem("x1_lo"), sem("q1_hi")
        gs_here, qs1_here = sem("gs_here"), [sem(f"qs1_here{i}") for i in range(PAIRS1)]
        sums1_done, sums1_read = sem("sums1_done"), sem("sums1_read")
        o1_hi, o1_lo = sem("o1_hi"), sem("o1_lo")
        cmax_ready, cas_here, pca_used = sem("cmax_ready"), sem("cas_here"), sem("pca_used")
        dve_ca, act_ca, out_done = sem("dve_ca"), sem("act_ca"), sem("out_done")

        consts = [(bo0, "bo0"), (bo1, "bo1"), (ident, "ident"), (OH0, "OH0"), (OH1, "OH1"), (E0, "E0"), (E1, "E1")]
        QG0 = [3 * GROUP + 1, 3 * GROUP + 1, 3 * (PAIRS0 - 2 * GROUP) + 1]
        QG1 = 3 * 2 + 1
        MQ1 = (3 * D1, 3 * D1, P)
        USES1 = 4 + PAIRS1
        DVE_CA = 2 + 1 + 3 + 3
        ACT_CA = PAIRS1 + 2 + 1
        with nc.Block() as first:
            @first.sync
            def _(sp):
                for x in R0.free + R1.free + qs0_here + qs1_here + [gs_here, sums0_read, sums0_done, sums1_read,
                                                                    pca_used, out_done]:
                    sp.sem_inc(x, 1)

        block = ctx.enter_context(nc.Block())

        def pairs_of(t):
            return range(GROUP * t, min(GROUP * t + GROUP, PAIRS0))

        def half(s):
            return slice(s * HALF, (s + 1) * HALF)

        @block.sync
        def _(sp):
            for dst, k in consts:
                sp.dma_start(dst[:], a[k]).then_inc(const_here, 16)

            def load_queries0(b, s, t):
                if t == 2:
                    R0.wait_read(sp, b, "sT", s, GROUP - 1)
                else:
                    R0.wait_read(sp, b, "q", s, t)
                for p in pairs_of(t):
                    j = p - GROUP * t
                    for seg, src in enumerate((q0H, q0L, q0H)):
                        sp.dma_start(QS0[32 * seg:32 * seg + 32, GROUP * (t % 2) + j].bitcast(F32),
                                     src[32 * j:32 * j + 32, t].bitcast(F32)).then_inc(qs0_here[t], 16)

            def load_maxima0(t):
                n, g = len(pairs_of(t)), GROUP * (t % 2)
                sp.dma_start(QS0[96:96 + H0, g:g + n].bitcast(F32),
                             nmaxT0[:].bitcast(F32).unsqueeze(1).to_broadcast([H0, n, HALF])).then_inc(qs0_here[t], 16)

            def load_queries1(b, s, p):
                if p >= 2:
                    R1.wait_read(sp, b, "sT", s, p - 2)
                for i in range(2):
                    t, j = (2 * p + i) // 3, (2 * p + i) % 3
                    for seg, src in enumerate((q1H, q1L, q1H)):
                        sp.dma_start(QS1[D1 * seg:D1 * seg + D1, p % 2, i].bitcast(F32),
                                     src[D1 * j:D1 * j + D1, t].bitcast(F32)).then_inc(qs1_here[p], 16)

            def load_maxima1(p):
                sp.dma_start(QS1[3 * D1:P, p % 2].bitcast(F32),
                             nmaxT1[:].bitcast(F32).unsqueeze(1).to_broadcast([H1, 2, HALF])).then_inc(qs1_here[p], 16)

            with sp.Fori(0, B) as b:
                for s in range(2):
                    load_queries0(b, s, 0)
                    load_queries0(b, s, 1)
                    R0.wait_read(sp, b, "maxT", s)
                    load_maxima0(0)
                    load_maxima0(1)
                    load_queries0(b, s, 2)
                    load_maxima0(2)
                R1.wait_before(sp, b, 0)
                for dst, k in ((KB1, "KB1"), (KS1, "KS1"), (V1, "V1"), (A3, "A3"), (VW, "VW")):
                    d = dst[:] if k in ("V1", "A3") else dst[:].bitcast(F32)
                    sp.dma_start(d, scr[k][bass.ds(b, 1)].squeeze(0)).then_inc(pack1_here, 16)
                sp.dma_start(CAS[0:96].bitcast(F32), scr["CAS"][bass.ds(b, 1)].squeeze(0)).then_inc(pack1_here, 16)
                for s in range(2):
                    R1.wait_read(sp, b, "q", s, 2)
                    for seg, src in enumerate((q1H, q1L, q1H)):
                        sp.dma_start(GS[HT * seg:HT * seg + HT, half(s)].bitcast(F32),
                                     src[96:P, 2].bitcast(F32)).then_inc(gs_here, 16)
                    load_queries1(b, s, 0)
                    load_queries1(b, s, 1)
                    R1.wait_read(sp, b, "maxT", s)
                    load_maxima1(0)
                    load_maxima1(1)
                    for p in range(2, PAIRS1):
                        load_queries1(b, s, p)
                        load_maxima1(p)
                R1.wait_read(sp, b, "cmaxT")
                sp.dma_start(CAS[96:97].bitcast(F32), cmaxT[:].bitcast(F32)).then_inc(cas_here, 16)
                for s in range(2):
                    R1.wait_read(sp, b, "fin", s, 2)
                    cols = bass.ds(b * S + s * HALF, HALF)
                    sp.dma_start(out[:, 0:2, cols], x1T[:, 0:2, half(s)]).then_inc(out_done, 16)
                    sp.dma_start(out[0:FT[2], 2, cols], x1T[0:FT[2], 2, half(s)]).then_inc(out_done, 16)
            sp.wait_ge(out_done, B * 16 * 4 + 1)

        @block.gpsimd
        def _(pool):
            nc.gpsimd.memset(GS[96:97].bitcast(F32), 1.0).then_inc(const_set, 1)
            pool.wait_ge(const_set, 1)
            nc.gpsimd.memset(X1N[:], 1.0).then_inc(const_set, 1)
            pool.wait_ge(const_set, 2)
            nc.gpsimd.memset(CO[:], 0.0).then_inc(const_set, 1)
            pool.wait_ge(const_set, 3)
            with pool.Fori(0, B) as b:
                R0.wait_before(pool, b, 0)
                pool.wait_ge(out_done, b * (16 * 4) + 1)
                for s in range(2):
                    pool.dma_start(x1T[:, :, half(s)], a["xT"][:, :, bass.ds(b * S + s * HALF, HALF)]).then_inc(x_here[s], 16)
                for dst, k in ((KB0, "KB0"), (KS0, "KS0")):
                    pool.dma_start(dst[:].bitcast(F32), scr[k][bass.ds(b, 1)].squeeze(0)).then_inc(pack0_here, 16)
                pool.dma_start(V0[:], scr["V0"][bass.ds(b, 1)].squeeze(0)).then_inc(pack0_here, 16)
                for s in range(2):
                    if s:
                        pool.wait_ge(x_lo, b * 4 + 2)
                    pool.wait_ge(x_hi, b * 2 + (s + 1))
                    nc.gpsimd.tensor_tensor(XL[:], x1T[:, 0:2, half(s)], XH[:, 0:2].bitcast(F32), ALU.subtract)\
                        .then_inc(x_lo, 1)
                    pool.wait_ge(x_lo, b * 4 + (2 * s + 1))
                    nc.gpsimd.tensor_tensor(XH[64:P, 2], x1T[64:P, 2, half(s)], XH[64:P, 2].bitcast(F32), ALU.subtract)\
                        .then_inc(x_lo, 1)

        @block.scalar
        def _(act):
            act.wait_ge(const_set, 3)

            def queries0(b, s):
                u = b * 2 + s
                act.wait_ge(x_here[s], b * 16 + 16)
                R0.wait_before(act, b, s, "wo", 0, 2)
                nc.scalar.copy(XH[:], x1T[:, :, half(s)]).then_inc(x_hi, 1)
                for t in range(3):
                    act.wait_ge(qs0_here[t], u * (16 * QG0[t]) + 1)
                    R0.wait_full(act, b, "q", s, t)
                    nc.scalar.copy(q0H[0:FT[t], t], R0.bank("q", s, t)[0:FT[t]]).then_inc(q0_hi, 1)
                R0.wait_full(act, b, "maxT", s)
                R0.read(nc.scalar.copy(nmaxT0[:], R0.bank("maxT", s)[0:H0]), "maxT", s)

            def attend0(b, s):
                u = b * 2 + s
                for t in range(3):
                    act.wait_ge(sums0_done, u * 4 + t + 1)
                    for p in pairs_of(t):
                        R0.wait_full(act, b, "sT", s, p)
                        R0.read(nc.scalar.activation(P0[:, p % SLOTS], R0.bank("sT", s, p)[:], ACT.Exp, scale=SCALE0),
                                "sT", s, p)
                    R0.wait_full(act, b, "pv", s, t)
                    R0.read(nc.scalar.copy(o0[:, t], R0.bank("pv", s, t)[:]), "pv", s, t)

            def split0(b, s):
                act.wait_ge(sums0_read, (b * 2 + s) * 2 + 2 + 1)
                for t in range(3):
                    nc.scalar.copy(XH[:, t], o0[:, t]).then_inc(o0_hi, 1)

            def queries1(b, s):
                u = b * 2 + s
                for t in range(3):
                    R0.wait_read(act, b, "wo", s, t)
                R1.wait_before(act, b, s, "wo", 0, 2)
                nc.scalar.copy(X1H[:], x1T[:, :, half(s)]).then_inc(x1_hi, 1)
                for p in range(PAIRS1):
                    act.wait_ge(qs1_here[p], u * (16 * QG1) + 1)
                act.wait_ge(gs_here, u * 48 + 1)
                for t in range(3):
                    R1.wait_full(act, b, "q", s, t)
                    nc.scalar.copy(q1H[0:MQ1[t], t], R1.bank("q", s, t)[0:MQ1[t]]).then_inc(q1_hi, 1)
                for qt in range(QT):
                    R1.wait_full(act, b, "xn", s, qt)
                    R1.read(nc.scalar.copy(X1N[:, s * QT + qt, :, 0:D1],
                                           R1.bank("xn", s, qt)[:, 0:F].rearrange("p (h d) -> p h d", h=H1)),
                            "xn", s, qt)
                R1.wait_full(act, b, "maxT", s)
                R1.read(nc.scalar.copy(nmaxT1[:], R1.bank("maxT", s)[0:H1]), "maxT", s)

            def attend1(b, s):
                u = b * 2 + s
                R1.wait_before(act, b, s, "wo", 0, 2)
                for p in range(PAIRS1):
                    R1.wait_full(act, b, "sT", s, p)
                    R1.read(nc.scalar.activation(P1[:, p], R1.bank("sT", s, p)[:], ACT.Exp, scale=SCALE1), "sT", s, p)
                act.wait_ge(gs_here, u * 48 + 48 + 1)
                for t in range(3):
                    R1.wait_full(act, b, "pv", s, t)
                    R1.read(nc.scalar.copy(o1[0:ROWS1[t], t], R1.bank("pv", s, t)[0:ROWS1[t]]), "pv", s, t)
                act.wait_ge(sums1_read, b * USES1 + (2 * s + 2) + 1)
                for t in range(3):
                    nc.scalar.copy(X1H[0:ROWS1[t], t], o1[0:ROWS1[t], t]).then_inc(o1_hi, 1)

            def channels(b):
                R1.wait_full(act, b, "cmaxT")
                R1.read(nc.scalar.copy(cmaxT[:], R1.bank("cmaxT")[0:HC // P, 0:P]), "cmaxT")
                for p in range(PAIRS1):
                    for kt in range(KT):
                        n = p * KT + kt
                        act.wait_ge(pca_used, b * (PAIRS1 * KT) + max(n - SLOTS + 1, 0) + 1)
                        R1.wait_full(act, b, "csT", p, kt)
                        R1.read(nc.scalar.activation(PCA[:, n % SLOTS, 0:PC], R1.bank("csT", p, kt)[:, 0:PC], ACT.Exp,
                                                     scale=SCALE1), "csT", p, kt)
                    act.wait_ge(pca_used, b * (PAIRS1 * KT) + KT * (p + 1) + 1)
                    nc.scalar.copy(CO[0:D1 + 1, p], sums1[0:D1 + 1, 0:C]).then_inc(act_ca, 1)
                    nc.scalar.copy(CO[64:64 + D1 + 1, p], sums1[64:64 + D1 + 1, 0:C]).then_inc(sums1_read, 1)
                for c in range(2):
                    R1.wait_full(act, b, "cnT", c)
                    bk = R1.bank("cnT", c)[:, 0:3 * CH].rearrange("p (t c) -> p t c", t=3)
                    nc.scalar.copy(hsT[:, c, 0:2], bk[:, 0:2]).then_inc(act_ca, 1)
                    R1.read(nc.scalar.copy(hsT[0:FT[2], c, 2], bk[0:FT[2], 2]), "cnT", c)
                R1.wait_read(act, b, "cs3")
                nc.scalar.activation(e3[:], d3[:], ACT.Exp, scale=SCALE1).then_inc(act_ca, 1)
                for s in range(2):
                    R1.wait_full(act, b, "cexp", s)
                    R1.read(nc.scalar.copy(P3S[0:96, s], R1.bank("cexp", s)[0:96]), "cexp", s)

            with act.Fori(0, B) as b:
                for s in range(2):
                    queries0(b, s)
                    attend0(b, s)
                    split0(b, s)
                for s in range(2):
                    queries1(b, s)
                    attend1(b, s)
                channels(b)

        @block.vector
        def _(dve):
            dve.wait_ge(const_here, 16 * len(consts))
            dve.wait_ge(const_set, 3)

            def queries0(b, s):
                u = b * 2 + s
                for t in range(3):
                    dve.wait_ge(q0_hi, u * 3 + (t + 1))
                    r = FT[t]
                    R0.read(nc.vector.tensor_tensor(q0L[0:r, t].bitcast(F32R), R0.bank("q", s, t)[0:r], q0H[0:r, t].bitcast(F32),
                                                    ALU.subtract), "q", s, t)
                R0.wait_before(dve, b, s, "maxT", 0)
                for qp in range(QT // 2):
                    for i in range(2):
                        for t in range(2):
                            qt = 2 * qp + i
                            R0.wait_full(dve, b, "max", s, qt, t)
                            R0.read(nc.vector.tensor_reduce(
                                nmax0[:, qt, 8 * t:8 * t + 8],
                                R0.bank("max", s, qt, t)[:].rearrange("p (h k) -> p h k", k=NK), axis=AX.X, op=ALU.max,
                                negate=True), "max", s, qt, t)
                    R0.wait_full(dve, b, "max2", s, qp)
                    R0.read(nc.vector.tensor_reduce(
                        nmax0[:, 2 * qp:2 * qp + 2, 16:H0],
                        R0.bank("max2", s, qp)[:].rearrange("p (q h k) -> p q h k", q=2, k=NK), axis=AX.X, op=ALU.max,
                        negate=True), "max2", s, qp)

            def normalize0(b, s):
                u = b * 2 + s
                dve.wait_ge(sums0_done, u * 4 + 3 + 1)
                nc.vector.reciprocal(rec0[:], sums0[:, 0:P]).then_inc(sums0_read, 1)
                R0.wait_read(dve, b, "pv", s, 2)
                for c in range(QT):
                    o = o0[:, :, P * c:P * c + P]
                    if c < QT - 1:
                        R0.wait_full(dve, b, "rec", s, c)
                        rec = R0.bank("rec", s, c)[:, 0:3 * P]
                    else:
                        dve.wait_ge(sums0_done, u * 4 + 4 + 1)
                        rec = sums0[:, P:4 * P]
                    ins = nc.vector.tensor_tensor(o, o, rec.rearrange("p (t c) -> p t c", t=3), ALU.mult)
                    if c < QT - 1:
                        R0.read(ins, "rec", s, c)
                    else:
                        ins.then_inc(sums0_read, 1)
                for t in range(3):
                    dve.wait_ge(o0_hi, u * 3 + (t + 1))
                    dst = XL[:, t] if t < 2 else XH[64:P, 2]
                    r = slice(0, P) if t < 2 else slice(64, P)
                    nc.vector.tensor_tensor(dst, o0[r, t], XH[r, t].bitcast(F32), ALU.subtract).then_inc(o0_lo, 1)
                for t in range(3):
                    R0.wait_full(dve, b, "wo", s, t)
                    R0.read(nc.vector.scalar_tensor_tensor(x1T[:, t, half(s)], R0.bank("wo", s, t)[:], bo0[:, t:t + 1],
                                                           x1T[:, t, half(s)], ALU.add, ALU.add), "wo", s, t)

            def queries1(b, s):
                u = b * 2 + s
                dve.wait_ge(x1_hi, u + 1)
                nc.vector.tensor_tensor(X1L[:, 0:2], x1T[:, 0:2, half(s)], X1H[:, 0:2].bitcast(F32), ALU.subtract)\
                    .then_inc(x1_lo, 1)
                nc.vector.tensor_tensor(X1H[64:P, 2], x1T[64:P, 2, half(s)], X1H[64:P, 2].bitcast(F32), ALU.subtract)\
                    .then_inc(x1_lo, 1)
                for t in range(3):
                    dve.wait_ge(q1_hi, u * 3 + (t + 1))
                    r = MQ1[t]
                    R1.read(nc.vector.tensor_tensor(q1L[0:r, t].bitcast(F32R), R1.bank("q", s, t)[0:r], q1H[0:r, t].bitcast(F32),
                                                    ALU.subtract), "q", s, t)
                R1.wait_before(dve, b, s, "maxT", 0)
                for qt in range(QT):
                    R1.wait_full(dve, b, "max", s, qt)
                    R1.read(nc.vector.tensor_reduce(
                        nmax1[:, qt], R1.bank("max", s, qt)[:].rearrange("p (h k) -> p h k", k=NK)[:, :, 0:K1],
                        axis=AX.X, op=ALU.max, negate=True), "max", s, qt)

            def attend1(b, s):
                u = b * 2 + s
                dve.wait_ge(sums1_done, u * 2 + 1)
                nc.vector.reciprocal(rec1[:], sums1[:, 0:P]).then_inc(sums1_read, 1)
                R1.wait_read(dve, b, "pv", s, 2)
                r = ROWS1[0]
                for c in range(QT):
                    o = o1[0:r, :, P * c:P * c + P]
                    if c < QT - 1:
                        R1.wait_full(dve, b, "rec", s, c)
                        rec = R1.bank("rec", s, c)[0:r, 0:3 * P]
                    else:
                        dve.wait_ge(sums1_done, u * 2 + 2)
                        rec = sums1[0:r, P:4 * P]
                    ins = nc.vector.tensor_tensor(o, o, rec.rearrange("p (t c) -> p t c", t=3), ALU.mult)
                    if c < QT - 1:
                        R1.read(ins, "rec", s, c)
                    else:
                        ins.then_inc(sums1_read, 1)
                for t in range(3):
                    r = ROWS1[t]
                    dve.wait_ge(o1_hi, u * 3 + (t + 1))
                    nc.vector.tensor_tensor(X1L[0:r, t], o1[0:r, t], X1H[0:r, t].bitcast(F32), ALU.subtract)\
                        .then_inc(o1_lo, 1)
                for t in range(3):
                    r = FT[t]
                    R1.wait_full(dve, b, "wo", s, t)
                    x = x1T[0:r, t, half(s)]
                    R1.read(nc.vector.scalar_tensor_tensor(x, R1.bank("wo", s, t)[0:r], bo1[0:r, t:t + 1], x, ALU.add,
                                                           ALU.add), "wo", s, t)

            def channels(b):
                for m in range(HC // P):
                    for s in range(2):
                        R1.wait_full(dve, b, "cmax", m, s)
                        R1.read(nc.vector.tensor_reduce(cmax2[:, m, s:s + 1], R1.bank("cmax", m, s)[:], axis=AX.X,
                                                        op=ALU.max), "cmax", m, s)
                R1.wait_read(dve, b, "cmax", HC // P - 1, 1)
                nc.vector.tensor_reduce(cmax[:], cmax2[:], axis=AX.X, op=ALU.max, negate=True).then_inc(cmax_ready, 1)

                done = [0]

                def link(ins):
                    ins.then_inc(dve_ca, 1)
                    done[0] += 1
                    dve.wait_ge(dve_ca, b * DVE_CA + done[0])

                for c in range(2):
                    R1.wait_full(dve, b, "cnat", c)
                    bk = R1.bank("cnat", c)[0:CH].rearrange("p (h d) -> p h d", h=H1)
                    link(nc.vector.reciprocal(crec[:, c].unsqueeze(2), bk[:, :, D1:D1 + 1]))
                    R1.read(nc.vector.tensor_tensor(hs[:, c], bk[:, :, 0:D1],
                                                    crec[:, c].unsqueeze(2).to_broadcast([CH, H1, D1]), ALU.mult),
                            "cnat", c)
                R1.wait_full(dve, b, "cs3")
                sc = R1.bank("cs3")[0:CH, 0:2 * HT].rearrange("p (c h t) -> p c h t", c=2, t=T)
                link(nc.vector.tensor_reduce(m3[:], sc, axis=AX.X, op=ALU.max))
                R1.read(nc.vector.tensor_tensor(d3[:], sc, m3[:].unsqueeze(3).to_broadcast([CH, 2, H1, T]),
                                                ALU.subtract), "cs3")
                dve.wait_ge(act_ca, b * ACT_CA + ACT_CA)
                link(nc.vector.tensor_reduce(s3[:], e3[:], axis=AX.X, op=ALU.add))
                link(nc.vector.reciprocal(r3[:], s3[:]))
                link(nc.vector.tensor_tensor(p3[:], e3[:], r3[:].unsqueeze(3).to_broadcast([CH, 2, H1, T]), ALU.mult))
                pf = p3[:].rearrange("p c h t -> p c (h t)")
                link(nc.vector.tensor_copy(P3[:, :, 0], pf))
                link(nc.vector.tensor_copy(P3[:, :, 2], pf))
                link(nc.vector.tensor_tensor(P3[:, :, 1], pf, P3[:, :, 0].bitcast(F32), ALU.subtract))
                assert done[0] == DVE_CA
                for s in range(2):
                    for t in range(3):
                        r = FT[t]
                        x = x1T[0:r, t, half(s)]
                        R1.wait_full(dve, b, "fin", s, t)
                        R1.read(nc.vector.tensor_tensor(x, R1.bank("fin", s, t)[0:r], x, ALU.add), "fin", s, t)

            with dve.Fori(0, B) as b:
                for s in range(2):
                    queries0(b, s)
                    normalize0(b, s)
                for s in range(2):
                    queries1(b, s)
                    attend1(b, s)
                channels(b)

        @block.tensor
        def _(pe):
            pe.wait_ge(const_here, 16 * len(consts))
            pe.wait_ge(const_set, 3)

            def products(ring, b, name, rows, parts, cols=HALF):
                ring.wait_free(pe, b, *name)
                for i, (lhsT, rhs) in enumerate(parts):
                    last = nc.tensor.matmul(ring.bank(*name)[0:rows, 0:cols], lhsT, rhs, start=(i == 0),
                                            stop=(i == len(parts) - 1))
                ring.filled(last, *name)

            def split_parts(WH, WL, XH, XL, m):
                return ([(WH[:, k, m], XH[:, k]) for k in range(3)] + [(WH[:, k, m], XL[:, k]) for k in range(2)]
                        + [(WL[:, k, m], XH[:, k]) for k in range(2)] + [(WL[0:64, 2, m], XH[0:64, 2])])

            def scores0(b, s):
                u = b * 2 + s
                pe.wait_ge(x_lo, u * 2 + 2)
                for t in range(3):
                    products(R0, b, ("q", s, t), FT[t], split_parts(WqH, WqL, XH, XL, slice(P * t, P * t + FT[t])))
                pe.wait_ge(q0_hi, u * 3 + 3)
                pe.wait_ge(pack0_here, b * 48 + 48)
                for qp in range(QT // 2):
                    for i in range(2):
                        qt = 2 * qp + i
                        for t in range(2):
                            products(R0, b, ("max", s, qt, t), P,
                                     [(q0H[:, t, P * qt:P * qt + P], KB0[:, t].rearrange("p h k -> p (h k)"))])
                    R0.wait_free(pe, b, "max2", s, qp)
                    for i in range(2):
                        qt = 2 * qp + i
                        last = nc.tensor.matmul(R0.bank("max2", s, qp)[:, 256 * i:256 * i + 256],
                                                q0H[0:64, 2, P * qt:P * qt + P],
                                                KB0[0:64, 2, 0:4].rearrange("p h k -> p (h k)"), start=True, stop=True)
                    R0.filled(last, "max2", s, qp)
                R0.wait_read(pe, b, "max2", s, QT // 2 - 1)
                R0.wait_free(pe, b, "maxT", s)
                for qt in range(QT):
                    last = nc.tensor.transpose(R0.bank("maxT", s)[0:H0, P * qt:P * qt + P], nmax0[:, qt], ident[:])
                R0.filled(last, "maxT", s)

            def attend0(b, s):
                u = b * 2 + s
                pe.wait_ge(sums0_read, u * 2 + 1)
                for t in range(3):
                    pe.wait_ge(qs0_here[t], u * (16 * QG0[t]) + 16 * QG0[t] + 1)
                    for p in pairs_of(t):
                        products(R0, b, ("sT", s, p), P, [(KS0[:, p], QS0[:, GROUP * (t % 2) + p - GROUP * t])])
                    for p in pairs_of(t):
                        R0.wait_read(pe, b, "sT", s, p)
                    R0.wait_free(pe, b, "pv", s, t)
                    for j in range(GROUP):
                        p = GROUP * t + j % len(pairs_of(t))
                        last = nc.tensor.matmul(R0.bank("pv", s, t)[32 * j:32 * j + 32], V0[:, 32 * p:32 * p + 32],
                                                P0[:, p % SLOTS], start=True, stop=True)
                    R0.filled(last, "pv", s, t)
                    for p in pairs_of(t):
                        for c in range(QT):
                            last = nc.tensor.matmul(sums0[32 * c:32 * c + 32, 0:P], OH0[:, p],
                                                    P0[:, p % SLOTS, P * c:P * c + P], start=(p == 0),
                                                    stop=(p == PAIRS0 - 1))
                    last.then_inc(sums0_done, 1)

            def output0(b, s):
                u = b * 2 + s
                pe.wait_ge(sums0_read, u * 2 + 1 + 1)
                for c in range(QT):
                    if c < QT - 1:
                        R0.wait_free(pe, b, "rec", s, c)
                        dst = R0.bank("rec", s, c)[:, 0:3 * P]
                    else:
                        dst = sums0[:, P:4 * P]
                    for t in range(3):
                        last = nc.tensor.matmul(dst[:, P * t:P * t + P], E0[32 * c:32 * c + H0, P * t:P * t + P],
                                                rec0[32 * c:32 * c + H0], start=True, stop=True)
                    if c < QT - 1:
                        R0.filled(last, "rec", s, c)
                    else:
                        last.then_inc(sums0_done, 1)
                pe.wait_ge(o0_lo, u * 3 + 3)
                for t in range(3):
                    products(R0, b, ("wo", s, t), P, split_parts(WoH, WoL, XH, XL, slice(P * t, P * t + P)))

            def scores1(b, s):
                u = b * 2 + s
                pe.wait_ge(x1_lo, u * 2 + 2)
                for t in range(3):
                    products(R1, b, ("q", s, t), MQ1[t],
                             split_parts(W1H, W1L, X1H, X1L, slice(120 * t, 120 * t + MQ1[t])))
                for qt in range(QT):
                    R1.wait_free(pe, b, "xn", s, qt)
                    for t in range(3):
                        r = FT[t]
                        last = nc.tensor.transpose(R1.bank("xn", s, qt)[:, P * t:P * t + r],
                                                   x1T[0:r, t, s * HALF + P * qt:s * HALF + P * qt + P], ident[0:r, 0:r])
                    R1.filled(last, "xn", s, qt)
                pe.wait_ge(q1_hi, u * 3 + 3)
                pe.wait_ge(pack1_here, b * 96 + 96)
                for qt in range(QT):
                    R1.wait_free(pe, b, "max", s, qt)
                    for t in range(3):
                        n, r = HEADS1[t] * NK, MQ1[t]
                        last = nc.tensor.matmul(R1.bank("max", s, qt)[:, 192 * t:192 * t + n],
                                                q1H[0:r, t, P * qt:P * qt + P],
                                                KB1[0:r, t, 0:HEADS1[t]].rearrange("p h k -> p (h k)"), start=True,
                                                stop=True)
                    R1.filled(last, "max", s, qt)
                R1.wait_read(pe, b, "max", s, QT - 1)
                R1.wait_free(pe, b, "maxT", s)
                for qt in range(QT):
                    last = nc.tensor.transpose(R1.bank("maxT", s)[0:H1, P * qt:P * qt + P], nmax1[:, qt], ident[:])
                R1.filled(last, "maxT", s)

            def attend1(b, s):
                u = b * 2 + s
                for p in range(PAIRS1):
                    pe.wait_ge(qs1_here[p], u * (16 * QG1) + 16 * QG1 + 1)
                    products(R1, b, ("sT", s, p), P, [(KS1[:, p, i], QS1[:, p % 2, i]) for i in range(2)])
                for p in range(PAIRS1):
                    R1.wait_read(pe, b, "sT", s, p)
                for t in range(3):
                    r = ROWS1[t]
                    products(R1, b, ("pv", s, t), r, [(V1[:, i, 0:r], P1[:, p]) for i, (tt, p) in enumerate(COMBOS)
                                                      if tt == t])
                pe.wait_ge(sums1_read, b * USES1 + 2 * s + 1)
                for p in range(PAIRS1):
                    for c in range(QT):
                        last = nc.tensor.matmul(sums1[32 * c:32 * c + 32, 0:P], OH1[:, p], P1[:, p, P * c:P * c + P],
                                                start=(p == 0), stop=(p == PAIRS1 - 1))
                last.then_inc(sums1_done, 1)
                pe.wait_ge(sums1_read, b * USES1 + (2 * s + 1) + 1)
                r = ROWS1[0]
                for c in range(QT):
                    if c < QT - 1:
                        R1.wait_free(pe, b, "rec", s, c)
                        dst = R1.bank("rec", s, c)[0:r, 0:3 * P]
                    else:
                        dst = sums1[0:r, P:4 * P]
                    for t in range(3):
                        last = nc.tensor.matmul(dst[:, P * t:P * t + P], E1[32 * c:32 * c + H1, P * t:P * t + r],
                                                rec1[32 * c:32 * c + H1], start=True, stop=True)
                    if c < QT - 1:
                        R1.filled(last, "rec", s, c)
                    else:
                        last.then_inc(sums1_done, 1)
                pe.wait_ge(o1_lo, u * 3 + 3)
                for t in range(3):
                    m = slice(P * t, P * t + FT[t])
                    parts = [(W[0:ROWS1[k], k, m], X[0:ROWS1[k], k]) for W, X in
                             ((W2H, X1H), (W2H, X1L), (W2L, X1H)) for k in range(3)]
                    products(R1, b, ("wo", s, t), FT[t], parts)

            def channels(b):
                pe.wait_ge(gs_here, b * 96 + 96 + 1)
                for m in range(HC // P):
                    for s in range(2):
                        products(R1, b, ("cmax", m, s), P, [(CAS[0:HT, P * m:P * m + P], GS[0:HT, half(s)])])
                pe.wait_ge(cmax_ready, b + 1)
                R1.wait_free(pe, b, "cmaxT")
                R1.filled(nc.tensor.transpose(R1.bank("cmaxT")[0:HC // P, 0:P], cmax[:], ident[:]), "cmaxT")
                pe.wait_ge(cas_here, b * 16 + 16)

                def values(p, kt):
                    n = p * KT + kt
                    if kt == 0:
                        pe.wait_ge(sums1_read, b * USES1 + (4 + p) + 1)
                    R1.wait_read(pe, b, "csT", p, kt)
                    for i in range(2):
                        last = nc.tensor.matmul(sums1[64 * i:64 * i + D1 + 1, 0:C], X1N[:, kt, 2 * p + i],
                                                PCA[:, n % SLOTS, C * i:C * i + C], start=(kt == 0),
                                                stop=(kt == KT - 1))
                    last.then_inc(pca_used, 1)

                steps = [(p, kt) for p in range(PAIRS1) for kt in range(KT)]
                for n, (p, kt) in enumerate(steps):
                    products(R1, b, ("csT", p, kt), P, [(GS[:, P * kt:P * kt + P], CAS[:, PC * p:PC * p + PC])], PC)
                    if n >= 2:
                        values(*steps[n - 2])
                values(*steps[-2])
                values(*steps[-1])
                pe.wait_ge(sums1_read, b * USES1 + USES1 + 1)
                for c in range(2):
                    R1.wait_free(pe, b, "cnat", c)
                    for p in range(PAIRS1):
                        last = nc.tensor.transpose(R1.bank("cnat", c)[0:CH, P * p:P * p + P],
                                                   CO[:, p, CH0[c]:CH0[c] + CH], ident[:])
                    R1.filled(last, "cnat", c)
                for c in range(2):
                    R1.wait_read(pe, b, "cnat", c)
                    R1.wait_free(pe, b, "cnT", c)
                    for t in range(3):
                        r = FT[t]
                        last = nc.tensor.transpose(R1.bank("cnT", c)[0:r, CH * t:CH * t + CH],
                                                   hs[:, c].rearrange("p h d -> p (h d)")[:, P * t:P * t + r],
                                                   ident[0:CH, 0:CH])
                    R1.filled(last, "cnT", c)
                R1.wait_free(pe, b, "cs3")
                for c in range(2):
                    R1.wait_read(pe, b, "cnT", c)
                    for t in range(3):
                        r = FT[t]
                        last = nc.tensor.matmul(R1.bank("cs3")[0:CH, HT * c:HT * c + HT], hsT[0:r, c, t], A3[0:r, t],
                                                start=(t == 0), stop=(t == 2))
                R1.filled(last, "cs3")
                pe.wait_ge(dve_ca, b * DVE_CA + DVE_CA)
                for s in range(2):
                    products(R1, b, ("cexp", s), 96, [(P3[:, s].rearrange("p g k -> p (g k)"), EX[:, s])])
                for s in range(2):
                    R1.wait_read(pe, b, "cexp", s)
                    for t in range(3):
                        products(R1, b, ("fin", s, t), FT[t], [(VW[:, P * t:P * t + FT[t]], P3S[0:96, s])])

            with pe.Fori(0, B) as b:
                for s in range(2):
                    scores0(b, s)
                    attend0(b, s)
                    output0(b, s)
                for s in range(2):
                    scores1(b, s)
                    attend1(b, s)
                channels(b)


def program(nc, a, out):
    shapes = {"KB0": [P, 3, 8, NK], "KS0": [QS0_ROWS, PAIRS0, P], "V0": [P, F], "KB1": [P, 3, 3, NK],
              "KS1": [P, PAIRS1, 2, P], "V1": [P, len(COMBOS), P], "A3": [P, 3, HT], "VW": [96, F], "CAS": [96, HC]}
    scr = {k: nc.dram_tensor(f"scratch_{k}", [B] + s, F32, kind="Internal").ap() for k, s in shapes.items()}
    with ExitStack() as ctx:
        w = {}
        for k, n in (("Wq0", F), ("Wo0", 3 * P), ("W1", 368), ("W2", F)):
            for part in "HL":
                w[k + part] = ctx.enter_context(nc.sbuf_tensor(f"{k}{part}", [P, 3, n], F32R))
        w["EX"] = ctx.enter_context(nc.sbuf_tensor("EX_split", [CH, 2, HALF], F32R))
        prologue(nc, a, scr, w)
        layers(nc, a, scr, w, out)



def tiles(x, sizes, rows=P, at=None):
    import numpy as np
    out = np.zeros((rows, len(sizes)) + x.shape[1:], np.float32)
    r = 0
    for t, n in enumerate(sizes):
        out[0:n, t] = x[r:r + n]
        r += n
    return out


def doubled(x):
    import numpy as np
    return tiles(np.concatenate([x, x[2 * P:]], 0), [P, P, P])


def shape_constants():
    import numpy as np
    f = np.float32
    c = {}
    part = np.arange(P)
    c["ident"] = np.eye(P, dtype=f)
    c["mKB0"] = np.repeat((part[:, None] // D0 == np.arange(8)[None]).astype(f)[:, :, None], NK, 2)
    k1 = np.zeros((P, 3, 3, NK), f)
    m8 = np.zeros((P, 3, H1), f)
    for t in range(3):
        for j in range(HEADS1[t]):
            k1[D1 * j:D1 * j + D1, t, j, 0:K1] = 1
            m8[D1 * j:D1 * j + D1, t, 3 * t + j] = 1
    c["mKB1"], c["m8"] = k1, m8
    feat = np.arange(F)
    c["mV0"] = ((feat[None] // D0) % 2 == part[:, None] // NK).astype(f)
    v1 = np.zeros((P, len(COMBOS), P), f)
    for i, (t, p) in enumerate(COMBOS):
        for m in range(ROWS1[t]):
            h = 3 * t + m // D1
            if h // 2 == p:
                v1[NK * (h % 2):NK * (h % 2) + K1, i, m] = 1
    c["mV1"] = v1
    ones0 = np.zeros((H0, PAIRS0, 2, NK), f)
    for h in range(H0):
        ones0[h, h // 2, h % 2] = 1
    c["ones0"] = ones0.reshape(H0, PAIRS0, P)
    ones1 = np.zeros((H1, PAIRS1, 2, 2, NK), f)
    for h in range(H1):
        ones1[h, h // 2, h % 2, h % 2, 0:K1] = 1
    c["ones1"] = ones1.reshape(H1, PAIRS1, 2, P)
    oh0 = np.ones((P, PAIRS0, 32), f)
    oh0[:, :, 0:H0] = 0
    oh1 = np.ones((P, PAIRS1, 32), f)
    oh1[:, :, 0:H1] = 0
    for i in range(2):
        for p in range(PAIRS0):
            oh0[NK * i:NK * i + NK, p, 2 * p + i] = 1
        for p in range(PAIRS1):
            oh1[NK * i:NK * i + K1, p, 2 * p + i] = 1
    c["OH0"], c["OH1"] = oh0, oh1
    e0, e1 = np.zeros((P, 3 * P), f), np.zeros((P, 3 * P), f)
    doubled_feature = np.concatenate([feat, feat[2 * P:]])
    for q in range(QT):
        for m, ft in enumerate(doubled_feature):
            e0[32 * q + ft // D0, m] = 1
        for t in range(3):
            for m in range(ROWS1[t]):
                e1[32 * q + 3 * t + m // D1, P * t + m] = 1
    c["E0"], c["E1"] = e0, e1
    channel = np.linspace(0, C - 1, S).astype(np.int64)
    ex = np.zeros((CH, 2, HALF), f)
    for i in range(S):
        ex[channel[i] - CH0[i // HALF], i // HALF, i % HALF] = 1
    c["EX"] = ex
    return c


def kernel(x, ctx_768, L0_xattn_Wq, L0_xattn_Wk, L0_xattn_Wv, L0_xattn_Wo, L0_xattn_bo, L1_xattn_Wq, L1_xattn_Wk,
           L1_xattn_Wv, L1_xattn_Wq_ca, L1_xattn_Wk_ca, L1_xattn_Wv_ca, L1_xattn_Wout, L1_xattn_b_out):
    import numpy as np
    import concourse.bacc as bacc
    from concourse.bass_utils import run_bass_kernel_spmd

    def host(v):
        return np.asarray(v)

    x, ctx = host(x), host(ctx_768)
    Wq1 = host(L1_xattn_Wq)
    arrays = shape_constants()
    arrays["xT"] = doubled(x.reshape(B * S, F).T)
    ctxT = ctx.transpose(2, 0, 1).reshape(2, KC, B, NK).transpose(1, 0, 2, 3)
    arrays["ctxD"] = np.concatenate([ctxT, ctxT], 3)

    def context_rows(w):
        return w.reshape(2, KC, w.shape[1]).transpose(1, 0, 2)

    arrays["Wk0"] = context_rows(host(L0_xattn_Wk))
    wk1 = np.zeros((C, 368), np.float32)
    wk1[:, 0:F] = host(L1_xattn_Wk)
    arrays["Wk1"] = context_rows(wk1)
    arrays["Wv0"], arrays["Wv1"] = context_rows(host(L0_xattn_Wv)), context_rows(host(L1_xattn_Wv))
    arrays["Wkca"], arrays["Wvca"] = context_rows(host(L1_xattn_Wk_ca)), context_rows(host(L1_xattn_Wv_ca))
    arrays["Wq0"] = doubled(host(L0_xattn_Wq))
    wo = host(L0_xattn_Wo)
    arrays["Wo0"] = doubled(np.concatenate([wo, wo[:, 2 * P:]], 1))
    w1 = np.zeros((F, 368), np.float32)
    w1[:, 0:F] = Wq1
    wca = host(L1_xattn_Wq_ca)
    for h in range(H1):
        for t in range(T):
            w1[D1 * h:D1 * h + D1, 336 + T * h + t] = wca[t, D1 * h:D1 * h + D1]
    arrays["W1"] = doubled(w1)
    arrays["Wq1T"] = tiles(Wq1.T, ROWS1)
    arrays["W2"] = tiles(host(L1_xattn_Wout), ROWS1)
    car = np.zeros((3, H1, T, B, H1, C), np.float32)
    for h in range(H1):
        car[:, h, :, :, h] = ctx[:, K1:].transpose(1, 0, 2)
    arrays["car"] = car.reshape(3 * HT, B, HC)
    for name, bias in (("bo0", L0_xattn_bo), ("bo1", L1_xattn_b_out)):
        arrays[name] = doubled(host(bias).reshape(F, 1))[:, :, 0]

    nc = bacc.Bacc("TRN2", target_bir_lowering=False, num_devices=1)
    arrays = {k: np.ascontiguousarray(v) for k, v in arrays.items()}
    a = {k: nc.dram_tensor(f"in_{k}", v.shape, mybir.dt.from_np(v.dtype), kind="ExternalInput").ap()
         for k, v in arrays.items()}
    out = nc.dram_tensor("out_T", (P, 3, B * S), F32, kind="ExternalOutput").ap()
    program(nc, a, out)
    r = run_bass_kernel_spmd(nc, [{f"in_{k}": v for k, v in arrays.items()}], core_ids=[0])
    y = r.results[0]["out_T"].reshape(P, 3, B * S)
    y = np.concatenate([y[:, 0], y[:, 1], y[0:FT[2], 2]], 0)
    return np.ascontiguousarray(y.T).reshape(B, S, F)
```

```python
from contextlib import ExitStack

import concourse.bass as bass
from concourse import mybir

F32 = mybir.dt.float32
F32R = mybir.dt.float32r
ALU = mybir.AluOpType
ACT = mybir.ActivationFunctionType
AX = mybir.AxisListType

B, S, F, C, NK = 4, 1024, 320, 192, 64
P = 128
HALF = 512
H0, D0 = 20, 16
H1, D1 = 8, 40
T = 4
K1 = NK - T
PAIRS0, PAIRS1 = H0 // 2, H1 // 2
GROUP = 4
QT = HALF // P
KT = S // P
SCALE0 = float(D0) ** -0.5
SCALE1 = float(D1) ** -0.5
KC = C // 2
HC = H1 * C
PC = 2 * C
HT = H1 * T
CH = C // 2 + 1
CH0 = [0, C - CH]
ROWS1 = [3 * D1, 3 * D1, 2 * D1]
HEADS1 = [3, 3, 2]
COMBOS = [(0, 0), (0, 1), (1, 1), (1, 2), (2, 3)]
HEAD1 = [0, 3, 6]
SLOTS1 = [(t, 2 * p + i if 2 * p + i in range(HEAD1[t], HEAD1[t] + HEADS1[t]) else None) for t, p in COMBOS
          for i in range(2)]
FT = [P, P, F - 2 * P]
SLOTS = 4


class Ring:

    def __init__(self, names, banks, full, free):
        self.banks, self.full, self.free = banks, full, free
        self.names = list(names)
        assert len(self.names) % len(banks) == 0, len(self.names)
        self.per = len(self.names) // len(banks)
        self.at = {n: i for i, n in enumerate(self.names)}

    def bank(self, *name):
        return self.banks[self.at[name] % len(self.banks)]

    def wait_free(self, eng, b, *name):
        i = self.at[name]
        eng.wait_ge(self.free[i % len(self.banks)], b * self.per + (i // len(self.banks) + 1))

    def filled(self, ins, *name):
        ins.then_inc(self.full[self.at[name] % len(self.banks)], 1)

    def wait_full(self, eng, b, *name):
        i = self.at[name]
        eng.wait_ge(self.full[i % len(self.banks)], b * self.per + (i // len(self.banks) + 1))

    def read(self, ins, *name):
        ins.then_inc(self.free[self.at[name] % len(self.banks)], 1)

    def wait_read(self, eng, b, *name):
        i = self.at[name]
        eng.wait_ge(self.free[i % len(self.banks)], b * self.per + (i // len(self.banks) + 2))

    def wait_last(self, eng, b, *name):
        i = self.at[name]
        if isinstance(b, int) and b == 0:
            return
        eng.wait_ge(self.free[i % len(self.banks)], b * self.per + (i // len(self.banks) + 2 - self.per))

    def wait_before(self, eng, b, s, *name):
        if s:
            self.wait_read(eng, b, *name)
        else:
            eng.wait_ge(self.free[(len(self.names) - 1) % len(self.banks)], b * self.per + 1)


def ring0_order():
    for s in range(2):
        yield from (("q", s, t) for t in range(3))
        for qp in range(QT // 2):
            yield from (("max", s, 2 * qp + i, t) for i in range(2) for t in range(2))
            yield ("max2", s, qp)
        yield ("maxT", s)
        for t in range(3):
            yield from (("sT", s, p) for p in range(GROUP * t, min(GROUP * t + GROUP, PAIRS0)))
            yield ("pv", s, t)
        yield from (("rec", s, t) for t in range(3))
        yield from (("wo", s, t) for t in range(3))


def ring1_order():
    for s in range(2):
        yield from (("q", s, t) for t in range(3))
        yield from (("xn", s, qt) for qt in range(QT))
        yield from (("max", s, qt) for qt in range(QT))
        yield ("maxT", s)
        for part, names in enumerate((["sT"], ["pv", "rec"], ["wo"])):
            if s == 1:
                n = HC // P // CMAX_PARTS
                yield from (("cmax", m, i) for m in range(n * part, n * part + n) for i in range(2))
            yield from ((k, s, i) for k in names for i in range(PAIRS1 if k == "sT" else 3))
    yield ("cmaxT",)
    yield from (("csT", p, kt) for p in range(PAIRS1) for kt in range(KT))
    yield from (("cnat", c) for c in range(2))
    yield from (("cnT", c) for c in range(2))
    yield ("cs3",)
    yield from (("cexp", s) for s in range(2))
    yield from (("fin", s, t) for s in range(2) for t in range(3))


PRELUDE = [("load_x", 0, 0), ("load_x", 0, 1), ("load0", 0, 0), ("split0", 0, 0), ("load1", 0, 0),
           ("project0", 0, 0), ("split0", 0, 1), ("maxima0", 0, 0), ("attend0", 0, 0), ("normalize0", 0, 0),
           ("output0", 0, 0), ("project0", 0, 1), ("maxima0", 0, 1), ("attend0", 0, 1), ("split1", 0, 0),
           ("normalize0", 0, 1), ("output0", 0, 1)]
STEADY = [("handover", 0, 0), ("load_x", 1, 0), ("load0", 1, 0), ("project1", 0, 0), ("naturals", 0, 0),
          ("maxima1", 0, 0), ("handover", 0, 1), ("split0", 1, 0), ("split1", 0, 1), ("load_x", 1, 1),
          ("scores1", 0, 0), ("project0", 1, 0), ("values1", 0, 0), ("maxima0", 1, 0), ("normalize1", 0, 0),
          ("attend0", 1, 0), ("output1", 0, 0), ("normalize0", 1, 0), ("project1", 0, 1), ("naturals", 0, 1),
          ("output0", 1, 0), ("split0", 1, 1), ("maxima1", 0, 1), ("channel_maxima", 0, 0), ("project0", 1, 1),
          ("scores1", 0, 1), ("channel_maxima", 0, 1), ("values1", 0, 1), ("maxima0", 1, 1),
          ("normalize1", 0, 1), ("channel_maxima", 0, 2), ("output1", 0, 1), ("channel_shift", 0, 0),
          ("attend0", 1, 1), ("channel_values", 0, 0), ("normalize0", 1, 1), ("channel_values", 0, 1),
          ("split1", 1, 0), ("tokens", 0, 0), ("output0", 1, 1), ("spread", 0, 0), ("final", 0, 0), ("final", 0, 1),
          ("load1", 1, 0)]
CMAX_PARTS = 3


def prologue(nc, a, scr, w):
    with ExitStack() as ctx:
        def sb(name, shape, dt=F32):
            return ctx.enter_context(nc.sbuf_tensor(name, shape, dt))

        def sem(name):
            return ctx.enter_context(nc.semaphore(name))

        raw = {k: sb(f"pro_{k}", list(a[k].shape)) for k in
               ("ctxD", "Wk0", "Wk1", "Wv0", "Wv1", "Wkca", "Wvca", "Wq1T", "W2", "mKB0", "mKB1", "m8", "mV0",
                "mV1", "ones0", "ones1", "car", "Wq0", "Wo0", "W1", "EX")}
        CAS = sb("pCAS", [96, HC], F32R)
        kT0H, kT0L = sb("kT0H", [P, 3, B, NK], F32R), sb("kT0L", [P, 3, B, NK], F32R)
        kT1H, kT1L = sb("kT1H", [P, 3, B, NK], F32R), sb("kT1L", [P, 3, B, NK], F32R)
        k3bd, v3bd = sb("k3bd", [P, 3, B, H1, T]), sb("v3bd", [P, 3, B, 3, H1, T])
        KB0H, KB0L = sb("pKB0H", [P, H0, NK], F32R), sb("pKB0L", [P, H0, NK], F32R)
        KB1H, KB1L = (sb(f"pKB1{part}", [P, len(SLOTS1), NK], F32R) for part in "HL")
        V0, V1 = sb("pV0", [P, F]), sb("pV1", [P, len(COMBOS), P])
        A3 = sb("pA3", [P, 3, B, HT])
        VW = sb("pVW", [3 * HT, F], F32R)
        bank = [ctx.enter_context(nc.psum_tensor(f"pbank{i}", [P, HALF], F32)) for i in range(4)]
        loaded, filled, read = sem("pro_loaded"), sem("pro_filled"), sem("pro_read")
        own, weights_hi, blocks_out = sem("pro_dve_done"), sem("pro_weights_hi"), sem("pro_blocks_out")
        blocks = (("KB0H", KB0H), ("KB0L", KB0L), ("KB1H", KB1H), ("KB1L", KB1L), ("V0", V0), ("V1", V1), ("VW", VW),
                  ("CAS", CAS))
        stores = len(blocks) + 1
        MK1 = (3 * D1, 3 * D1, P)
        block = ctx.enter_context(nc.Block())

        @block.sync
        def _(sp):
            for k in raw:
                sp.dma_start(raw[k][:], a[k]).then_inc(loaded, 16)
            for b in range(B):
                sp.wait_ge(read, 15 + 3 * (b + 1))
                for k, src in blocks:
                    sp.dma_start(scr[k][b], src[:] if k in ("V0", "V1") else src[:].bitcast(F32))\
                        .then_inc(blocks_out, 16)
                sp.dma_start(scr["A3"][b], A3[:, :, b, :]).then_inc(blocks_out, 16)
            sp.wait_ge(blocks_out, 16 * stores * B)

        @block.scalar
        def _(act):
            act.wait_ge(loaded, 16 * len(raw))
            for k in ("Wq0", "Wo0", "W1", "W2"):
                nc.scalar.copy(w[k + "H"][:], raw[k][:]).then_inc(weights_hi, 1)
            for k in ("EX", "ones0", "ones1"):
                nc.scalar.copy(w[k][:], raw[k][:])

        @block.tensor
        def _(pe):
            pe.wait_ge(loaded, 16 * len(raw))
            fills = [0]

            def fill(rows, cols, parts):
                n = fills[0]
                if n >= 4:
                    pe.wait_ge(read, n - 3)
                for i, (lhsT, rhs) in enumerate(parts):
                    last = nc.tensor.matmul(bank[n % 4][0:rows, 0:cols], lhsT, rhs, start=(i == 0),
                                            stop=(i == len(parts) - 1))
                last.then_inc(filled, 1)
                fills[0] += 1

            keys = [raw["ctxD"][:, k, :, 0:NK] for k in range(2)]
            toks = [raw["ctxD"][:, k, :, K1:NK] for k in range(2)]
            for t in range(3):
                fill(P, B * NK, [(raw["Wk0"][:, k, P * t:P * t + P], keys[k]) for k in range(2)])
            for t in range(3):
                fill(MK1[t], B * NK, [(raw["Wk1"][:, k, 120 * t:120 * t + MK1[t]], keys[k]) for k in range(2)])
            for name in ("Wkca", "Wvca"):
                for t in range(3):
                    fill(ROWS1[t], B * T, [(raw[name][:, k, 120 * t:120 * t + ROWS1[t]], toks[k]) for k in range(2)])
            pe.wait_ge(read, 12)
            for t in range(3):
                fill(FT[t], B * HT, [(raw["Wq1T"][0:ROWS1[k], k, P * t:P * t + FT[t]],
                                      k3bd[0:ROWS1[k], k].rearrange("p b h t -> p (b h t)")) for k in range(3)])
            for b in range(B):
                for name in ("Wv0", "Wv1"):
                    fill(P, F, [(raw["ctxD"][:, k, b, :], raw[name][:, k, :]) for k in range(2)])
                fill(3 * HT, F, [(v3bd[0:ROWS1[k], k, b].rearrange("p g h t -> p (g h t)"),
                                  raw["W2"][0:ROWS1[k], k, :]) for k in range(3)])

        @block.vector
        def _(dve):
            done = [0]
            fills = [0]

            def link(ins):
                ins.then_inc(own, 1)
                done[0] += 1
                dve.wait_ge(own, done[0])

            def next_fill():
                fills[0] += 1
                dve.wait_ge(filled, fills[0])
                return bank[(fills[0] - 1) % 4]

            for x in (kT0H, kT0L, kT1H, kT1L):
                link(nc.vector.memset(x[:].bitcast(F32), 0.0))
            link(nc.vector.memset(V1[:], 0.0))
            link(nc.vector.memset(A3[:], 0.0))
            dve.wait_ge(loaded, 16 * len(raw))
            for i, k in enumerate(("Wq0", "Wo0", "W1", "W2")):
                dve.wait_ge(weights_hi, i + 1)
                nc.vector.tensor_tensor(w[k + "L"][:], raw[k][:], w[k + "H"][:].bitcast(F32), ALU.subtract)
            for hi, lo, rows in ((kT0H, kT0L, (P, P, P)), (kT1H, kT1L, MK1)):
                for t in range(3):
                    r = rows[t]
                    ps = next_fill()[0:r, 0:B * NK]
                    h = hi[0:r, t].rearrange("p b k -> p (b k)")
                    link(nc.vector.tensor_copy(h, ps))
                    nc.vector.tensor_tensor(lo[0:r, t].rearrange("p b k -> p (b k)"), ps, h.bitcast(F32),
                                            ALU.subtract).then_inc(read, 1)
            for dst in (k3bd, v3bd):
                for t in range(3):
                    r = ROWS1[t]
                    bk = next_fill()[0:r, 0:B * T].rearrange("p (b t) -> p b t", b=B)
                    for d, b in ((d, b) for b in range(B) for d in
                                 ([dst[0:r, t, b]] if dst is k3bd else [dst[0:r, t, b, g] for g in range(3)])):
                        last = nc.vector.tensor_tensor(
                            d, bk[:, b].unsqueeze(1).to_broadcast([r, H1, T]),
                            raw["m8"][0:r, t].unsqueeze(2).to_broadcast([r, H1, T]), ALU.mult)
                    last.then_inc(read, 1)
            for t in range(3):
                r = FT[t]
                ps = next_fill()[0:r, 0:B * HT].rearrange("p (b h) -> p b h", b=B)
                nc.vector.tensor_copy(A3[0:r, t], ps).then_inc(read, 1)
            dve.wait_ge(read, 15)
            for b in range(B):
                if b >= 1:
                    dve.wait_ge(blocks_out, 16 * stores * b)
                link(nc.vector.tensor_copy(CAS[:], raw["car"][:, b]))
                nc.vector.tensor_tensor(CAS[64:96], raw["car"][64:96, b], CAS[64:96].bitcast(F32), ALU.subtract)
                for dst, src in ((KB0H, kT0H), (KB0L, kT0L)):
                    for t in range(3):
                        h = slice(8 * t, min(8 * t + 8, H0))
                        n = h.stop - h.start
                        nc.vector.tensor_tensor(dst[:, h], src[:, t, b].bitcast(F32).unsqueeze(1).to_broadcast([P, n, NK]),
                                                raw["mKB0"][:, h], ALU.mult)
                for dst, src in ((KB1H, kT1H), (KB1L, kT1L)):
                    for t, c in enumerate((slice(0, 4), slice(4, 8), slice(8, 10))):
                        n = c.stop - c.start
                        nc.vector.tensor_tensor(dst[:, c], src[:, t, b].bitcast(F32).unsqueeze(1).to_broadcast([P, n, NK]),
                                                raw["mKB1"][:, c], ALU.mult)
                nc.vector.tensor_tensor(V0[:], next_fill()[:, 0:F], raw["mV0"][:], ALU.mult).then_inc(read, 1)
                bk = next_fill()
                for i, (t, _) in enumerate(COMBOS):
                    n = ROWS1[t]
                    last = nc.vector.tensor_tensor(V1[:, i, 0:n], bk[:, 120 * t:120 * t + n], raw["mV1"][:, i, 0:n],
                                                   ALU.mult)
                last.then_inc(read, 1)
                bk = next_fill()
                link(nc.vector.tensor_copy(VW[:], bk[0:3 * HT, 0:F]))
                lo = slice(2 * HT, 3 * HT)
                nc.vector.tensor_tensor(VW[lo], bk[lo, 0:F], VW[lo].bitcast(F32), ALU.subtract).then_inc(read, 1)


def layers(nc, a, scr, w, out):
    with ExitStack() as ctx:
        def sb(name, shape, dt=F32):
            return ctx.enter_context(nc.sbuf_tensor(name, shape, dt))

        def sem(name):
            return ctx.enter_context(nc.semaphore(name))

        bank = [ctx.enter_context(nc.psum_tensor(f"bank{i}", [P, HALF], F32)) for i in range(8)]
        R0 = Ring(ring0_order(), bank[0:3], [sem(f"l0_bank{i}_full") for i in range(3)],
                  [sem(f"l0_bank{i}_read") for i in range(3)])
        R1 = Ring(ring1_order(), bank[4:7], [sem(f"l1_bank{i}_full") for i in range(3)],
                  [sem(f"l1_bank{i}_read") for i in range(3)])
        sums0, sums1 = bank[3], bank[7]

        WqH, WqL, WoH, WoL, W1H, W1L, W2H, W2L, EX, ones0, ones1 = (
            w[k] for k in ("Wq0H", "Wq0L", "Wo0H", "Wo0L", "W1H", "W1L", "W2H", "W2L", "EX", "ones0", "ones1"))
        bo0, bo1 = sb("bo0_sb", [P, 3]), sb("bo1_sb", [P, 3])
        ident = sb("ident_sb", [P, P])
        OH0, OH1 = sb("OH0_sb", [P, PAIRS0, 32]), sb("OH1_sb", [P, PAIRS1, 32])
        E0, E1 = sb("E0_sb", [P, 3 * P]), sb("E1_sb", [P, 3 * P])
        KB0H, KB0L = sb("KB0H_sb", [P, H0, NK], F32R), sb("KB0L_sb", [P, H0, NK], F32R)
        V0 = sb("V0_sb", [P, F])
        KB1H, KB1L = sb("KB1H_sb", [P, len(SLOTS1), NK], F32R), sb("KB1L_sb", [P, len(SLOTS1), NK], F32R)
        V1 = sb("V1_sb", [P, len(COMBOS), P])
        A3 = sb("A3_sb", [P, 3, HT])
        VW = sb("VW_sb", [96, F], F32R)
        CAS = sb("CAS_sb", [97, HC], F32R)
        X = sb("X_sb", [P, 3, S])
        XH, XL = sb("XH", [P, 3, HALF], F32R), sb("XL", [P, 2, HALF], F32R)
        q0H, q0L = sb("q0H", [P, 3, HALF], F32R), sb("q0L", [P, 2, HALF], F32R)
        o0 = sb("o0", [P, 3, HALF])
        nmax0 = sb("nmax0", [P, QT, H0])
        nmaxT0 = sb("nmaxT0", [H0, HALF], F32R)
        P0 = sb("P0", [P, SLOTS, HALF])
        rec0 = sb("rec0", [P, P])
        x1T = sb("x1T", [P, 3, S])
        X1H, X1L = sb("X1H", [P, 3, HALF], F32R), sb("X1L", [P, 2, HALF], F32R)
        q1H, q1L = sb("q1H", [P, 3, HALF], F32R), sb("q1L", [P, 3, HALF], F32R)
        o1 = sb("o1", [P, 3, HALF])
        nmax1 = sb("nmax1", [P, QT, H1])
        nmaxT1 = sb("nmaxT1", [H1, HALF], F32R)
        P1 = sb("P1", [P, PAIRS1, HALF])
        rec1 = sb("rec1", [P, P])
        GS = sb("GS", [97, S], F32R)
        X1N = sb("X1N", [P, KT, H1, D1 + 1])
        cmax2, cmax = sb("cmax2", [P, HC // P, 2]), sb("cmax", [P, HC // P])
        cmaxT = sb("cmaxT", [HC // P, P], F32R)
        PCA = P1
        CO = sb("CO", [P, PAIRS1, C])
        crec = sb("crec", [CH, 2, H1])
        hs = sb("hs", [CH, 2, H1, D1])
        hsT = o1[:, 0:2, 0:3 * CH].rearrange("p c (t n) -> p c t n", t=3)
        m3, s3, r3 = sb("m3", [CH, 2, H1]), sb("s3", [CH, 2, H1]), sb("r3", [CH, 2, H1])
        d3, e3, p3 = sb("d3", [CH, 2, H1, T]), sb("e3", [CH, 2, H1, T]), sb("p3", [CH, 2, H1, T])
        P3 = sb("P3", [CH, 2, 3, HT], F32R)
        P3S = sb("P3S", [96, 2, HALF], F32R)

        const_here, const_set = sem("const_here"), sem("const_set")
        pack0_here, pack1_here, x_here = sem("pack0_here"), sem("pack1_here"), [sem(f"x_here{s}") for s in range(2)]
        x_hi, x_lo, q0_hi = sem("x_hi"), sem("x_lo"), sem("q0_hi")
        sums0_done, sums0_read, o0_hi, o0_lo = sem("sums0_done"), sem("sums0_read"), sem("o0_hi"), sem("o0_lo")
        x1_here = sem("x1_here")
        x1_hi, x1_lo, q1_hi = sem("x1_hi"), sem("x1_lo"), sem("q1_hi")
        gs_here = sem("gs_here")
        sums1_done, sums1_read = sem("sums1_done"), sem("sums1_read")
        o1_hi, o1_lo = sem("o1_hi"), sem("o1_lo")
        cmax_ready, cas_here, pca_used = sem("cmax_ready"), sem("cas_here"), sem("pca_used")
        dve_ca, act_ca, out_done = sem("dve_ca"), sem("act_ca"), [sem(f"out_done{s}") for s in range(2)]

        consts = [(bo0, "bo0"), (bo1, "bo1"), (ident, "ident"), (OH0, "OH0"), (OH1, "OH1"), (E0, "E0"), (E1, "E1")]
        MQ1 = (3 * D1, 3 * D1, P)
        USES1 = 4 + PAIRS1
        DVE_CA = 2 + 1 + 3 + 3
        ACT_CA = PAIRS1 + 2 + 1
        with nc.Block() as first:
            @first.sync
            def _(sp):
                for x in R0.free + R1.free + [gs_here, sums0_read, sums0_done, sums1_read,
                                                                    pca_used, x1_here] + out_done:
                    sp.sem_inc(x, 1)

        block = ctx.enter_context(nc.Block())

        def tiles_of_part(part):
            n = HC // P // CMAX_PARTS
            return range(n * part, n * part + n)

        def pairs_of_part(part):
            return range(2 * part, 2 * part + 2)

        def pairs_of(t):
            return range(GROUP * t, min(GROUP * t + GROUP, PAIRS0))

        def half(s):
            return slice(s * HALF, (s + 1) * HALF)

        def scratch(k, b):
            return scr[k][bass.ds(b, 1)].squeeze(0)

        def run(eng, steps):
            for name, _, s in PRELUDE:
                if name in steps:
                    steps[name](0, s)
            with eng.Fori(0, B - 1) as b:
                for name, ahead, s in STEADY:
                    if name in steps:
                        steps[name](b + 1 if ahead else b, s)
            for name, ahead, s in STEADY:
                if name in steps and not ahead:
                    steps[name](B - 1, s)

        def wait_last_half(ring, eng, b, s):
            if s:
                ring.wait_read(eng, b, "q", 0, 2)
            else:
                ring.wait_last(eng, b, "q", 1, 2)

        @block.sync
        def _(sp):
            for dst, k in consts:
                sp.dma_start(dst[:], a[k]).then_inc(const_here, 16)

            def load1(b, _):
                R1.wait_before(sp, b, 0)
                for dst, k in ((KB1H, "KB1H"), (KB1L, "KB1L"), (V1, "V1"), (A3, "A3"), (VW, "VW")):
                    d = dst[:] if k in ("V1", "A3") else dst[:].bitcast(F32)
                    sp.dma_start(d, scratch(k, b)).then_inc(pack1_here, 16)
                sp.dma_start(CAS[0:96].bitcast(F32), scratch("CAS", b)).then_inc(pack1_here, 16)

            def project1(b, s):
                R1.wait_read(sp, b, "q", s, 2)
                for seg, src in enumerate((q1H, q1L, q1H)):
                    sp.dma_start(GS[HT * seg:HT * seg + HT, half(s)].bitcast(F32),
                                 src[96:P, 2].bitcast(F32)).then_inc(gs_here, 16)

            def channel_shift(b, _):
                R1.wait_read(sp, b, "cmaxT")
                sp.dma_start(CAS[96:97].bitcast(F32), cmaxT[:].bitcast(F32)).then_inc(cas_here, 16)

            def final(b, s):
                R1.wait_read(sp, b, "fin", s, 2)
                cols = bass.ds(b * S + s * HALF, HALF)
                sp.dma_start(out[:, 0:2, cols], x1T[:, 0:2, half(s)]).then_inc(out_done[s], 16)
                sp.dma_start(out[0:FT[2], 2, cols], x1T[0:FT[2], 2, half(s)]).then_inc(out_done[s], 16)

            run(sp, {"load1": load1, "project1": project1, "channel_shift": channel_shift, "final": final})
            for s in range(2):
                sp.wait_ge(out_done[s], B * 32 + 1)

        @block.gpsimd
        def _(pool):
            nc.gpsimd.memset(GS[96:97].bitcast(F32), 1.0).then_inc(const_set, 1)
            pool.wait_ge(const_set, 1)
            nc.gpsimd.memset(X1N[:], 1.0).then_inc(const_set, 1)
            pool.wait_ge(const_set, 2)
            nc.gpsimd.memset(CO[:], 0.0).then_inc(const_set, 1)
            pool.wait_ge(const_set, 3)
            nc.gpsimd.memset(o1[64:P, 2], 0.0).then_inc(const_set, 1)
            pool.wait_ge(const_set, 4)

            def load_x(b, s):
                if not (isinstance(b, int) and b == 0):
                    pool.wait_ge(x1_here, b * 2 + s)
                    pool.wait_ge(x1_lo, b * 4 + 2 * s - 2)
                pool.dma_start(X[:, :, half(s)], a["xT"][:, :, bass.ds(b * S + s * HALF, HALF)])\
                    .then_inc(x_here[s], 16)

            def load0(b, _):
                R0.wait_before(pool, b, 0)
                for dst, k in ((KB0H, "KB0H"), (KB0L, "KB0L")):
                    pool.dma_start(dst[:].bitcast(F32), scratch(k, b)).then_inc(pack0_here, 16)
                pool.dma_start(V0[:], scratch("V0", b)).then_inc(pack0_here, 16)

            def split0(b, s):
                pool.wait_ge(x_hi, b * 2 + (s + 1))
                if s:
                    pool.wait_ge(x_lo, b * 4 + 2)
                nc.gpsimd.tensor_tensor(XL[:], X[:, 0:2, half(s)], XH[:, 0:2].bitcast(F32), ALU.subtract)\
                    .then_inc(x_lo, 1)
                pool.wait_ge(x_lo, b * 4 + (2 * s + 1))
                nc.gpsimd.tensor_tensor(XH[64:P, 2], X[64:P, 2, half(s)], XH[64:P, 2].bitcast(F32), ALU.subtract)\
                    .then_inc(x_lo, 1)

            run(pool, {"load_x": load_x, "load0": load0, "split0": split0})

        @block.scalar
        def _(act):
            act.wait_ge(const_set, 4)

            def split0(b, s):
                act.wait_ge(x_here[s], b * 16 + 16)
                wait_last_half(R0, act, b, s)
                nc.scalar.copy(XH[:], X[:, :, half(s)]).then_inc(x_hi, 1)

            def project0(b, s):
                R0.wait_before(act, b, s, "wo", 0, 2)
                for t in range(3):
                    R0.wait_full(act, b, "q", s, t)
                    nc.scalar.copy(q0H[:, t], R0.bank("q", s, t)[:]).then_inc(q0_hi, 1)

            def maxima0(b, s):
                R0.wait_full(act, b, "maxT", s)
                R0.read(nc.scalar.copy(nmaxT0[:], R0.bank("maxT", s)[0:H0]), "maxT", s)

            def attend0(b, s):
                u = b * 2 + s
                for t in range(3):
                    act.wait_ge(sums0_done, u * 4 + t + 1)
                    for p in pairs_of(t):
                        R0.wait_full(act, b, "sT", s, p)
                        R0.read(nc.scalar.activation(P0[:, p % SLOTS], R0.bank("sT", s, p)[:], ACT.Exp, scale=SCALE0),
                                "sT", s, p)
                    R0.wait_full(act, b, "pv", s, t)
                    R0.read(nc.scalar.copy(o0[:, t], R0.bank("pv", s, t)[:]), "pv", s, t)

            def normalize0(b, s):
                act.wait_ge(sums0_read, (b * 2 + s) * 2 + 2 + 1)
                for t in range(3):
                    nc.scalar.copy(q0H[:, t], o0[:, t]).then_inc(o0_hi, 1)

            def split1(b, s):
                R0.wait_read(act, b, "wo", s, 2)
                wait_last_half(R1, act, b, s)
                nc.scalar.copy(X1H[:], X[:, :, half(s)]).then_inc(x1_hi, 1)

            def handover(b, s):
                R0.wait_read(act, b, "wo", s, 2)
                act.wait_ge(out_done[s], b * 32 + 1)
                nc.scalar.copy(x1T[:, :, half(s)], X[:, :, half(s)]).then_inc(x1_here, 1)

            def project1(b, s):
                u = b * 2 + s
                R1.wait_before(act, b, s, "wo", 0, 2)
                for t in range(3):
                    R1.wait_full(act, b, "q", s, t)
                    nc.scalar.copy(q1H[0:MQ1[t], t], R1.bank("q", s, t)[0:MQ1[t]]).then_inc(q1_hi, 1)

            def naturals(b, s):
                for qt in range(QT):
                    R1.wait_full(act, b, "xn", s, qt)
                    R1.read(nc.scalar.copy(X1N[:, s * QT + qt, :, 0:D1],
                                           R1.bank("xn", s, qt)[:, 0:F].rearrange("p (h d) -> p h d", h=H1)),
                            "xn", s, qt)

            def maxima1(b, s):
                R1.wait_full(act, b, "maxT", s)
                R1.read(nc.scalar.copy(nmaxT1[:], R1.bank("maxT", s)[0:H1]), "maxT", s)

            def scores1(b, s):
                R1.wait_before(act, b, s, "wo", 0, 2)
                for p in range(PAIRS1):
                    R1.wait_full(act, b, "sT", s, p)
                    R1.read(nc.scalar.activation(P1[:, p], R1.bank("sT", s, p)[:], ACT.Exp, scale=SCALE1), "sT", s, p)

            def values1(b, s):
                for t in range(3):
                    R1.wait_full(act, b, "pv", s, t)
                    R1.read(nc.scalar.copy(o1[0:ROWS1[t], t], R1.bank("pv", s, t)[0:ROWS1[t]]), "pv", s, t)

            def normalize1(b, s):
                act.wait_ge(gs_here, (b * 2 + s) * 48 + 48 + 1)
                act.wait_ge(sums1_read, b * USES1 + (2 * s + 2) + 1)
                for t in range(3):
                    nc.scalar.copy(q1H[0:ROWS1[t], t], o1[0:ROWS1[t], t]).then_inc(o1_hi, 1)

            def channel_shift(b, _):
                R1.wait_full(act, b, "cmaxT")
                R1.read(nc.scalar.copy(cmaxT[:], R1.bank("cmaxT")[0:HC // P, 0:P]), "cmaxT")

            def channel_values(b, part):
                for p in pairs_of_part(part):
                    for kt in range(KT):
                        n = p * KT + kt
                        act.wait_ge(pca_used, b * (PAIRS1 * KT) + max(n - SLOTS + 1, 0) + 1)
                        R1.wait_full(act, b, "csT", p, kt)
                        R1.read(nc.scalar.activation(PCA[:, n % SLOTS, 0:PC], R1.bank("csT", p, kt)[:, 0:PC], ACT.Exp,
                                                     scale=SCALE1), "csT", p, kt)
                    act.wait_ge(pca_used, b * (PAIRS1 * KT) + KT * (p + 1) + 1)
                    nc.scalar.copy(CO[0:D1 + 1, p], sums1[0:D1 + 1, 0:C]).then_inc(act_ca, 1)
                    nc.scalar.copy(CO[64:64 + D1 + 1, p], sums1[64:64 + D1 + 1, 0:C]).then_inc(sums1_read, 1)

            def tokens(b, _):
                for c in range(2):
                    R1.wait_full(act, b, "cnT", c)
                    bk = R1.bank("cnT", c)[:, 0:3 * CH].rearrange("p (t c) -> p t c", t=3)
                    nc.scalar.copy(hsT[:, c, 0:2], bk[:, 0:2]).then_inc(act_ca, 1)
                    R1.read(nc.scalar.copy(hsT[0:FT[2], c, 2], bk[0:FT[2], 2]), "cnT", c)
                R1.wait_read(act, b, "cs3")
                nc.scalar.activation(e3[:], d3[:], ACT.Exp, scale=SCALE1).then_inc(act_ca, 1)

            def spread(b, _):
                for s in range(2):
                    R1.wait_full(act, b, "cexp", s)
                    R1.read(nc.scalar.copy(P3S[:, s], R1.bank("cexp", s)[0:96]), "cexp", s)

            run(act, {"handover": handover, "split0": split0, "split1": split1, "project0": project0, "maxima0": maxima0, "attend0": attend0, "normalize0": normalize0,
                      "project1": project1, "naturals": naturals, "maxima1": maxima1, "scores1": scores1,
                      "values1": values1, "normalize1": normalize1, "channel_shift": channel_shift, "channel_values": channel_values,
                      "tokens": tokens, "spread": spread})

        @block.vector
        def _(dve):
            dve.wait_ge(const_here, 16 * len(consts))
            dve.wait_ge(const_set, 4)

            def project0(b, s):
                u = b * 2 + s
                for t in range(3):
                    dve.wait_ge(q0_hi, u * 3 + (t + 1))
                    r = slice(0, P) if t < 2 else slice(FT[2], P)
                    dst = q0L[:, t] if t < 2 else q0H[r, t]
                    R0.read(nc.vector.tensor_tensor(dst, R0.bank("q", s, t)[r], q0H[r, t].bitcast(F32),
                                                    ALU.subtract), "q", s, t)

            def maxima0(b, s):
                R0.wait_before(dve, b, s, "maxT", 0)
                for qp in range(QT // 2):
                    for i in range(2):
                        for t in range(2):
                            qt = 2 * qp + i
                            R0.wait_full(dve, b, "max", s, qt, t)
                            R0.read(nc.vector.tensor_reduce(
                                nmax0[:, qt, 8 * t:8 * t + 8],
                                R0.bank("max", s, qt, t)[:].rearrange("p (h k) -> p h k", k=NK), axis=AX.X, op=ALU.max,
                                negate=True), "max", s, qt, t)
                    R0.wait_full(dve, b, "max2", s, qp)
                    R0.read(nc.vector.tensor_reduce(
                        nmax0[:, 2 * qp:2 * qp + 2, 16:H0],
                        R0.bank("max2", s, qp)[:].rearrange("p (q h k) -> p q h k", q=2, k=NK), axis=AX.X, op=ALU.max,
                        negate=True), "max2", s, qp)

            def normalize0(b, s):
                u = b * 2 + s
                dve.wait_ge(sums0_done, u * 4 + 3 + 1)
                nc.vector.reciprocal(rec0[:], sums0[:, 0:P]).then_inc(sums0_read, 1)
                R0.wait_read(dve, b, "pv", s, 2)
                for c in range(QT):
                    o = o0[:, :, P * c:P * c + P]
                    if c < QT - 1:
                        R0.wait_full(dve, b, "rec", s, c)
                        rec = R0.bank("rec", s, c)[:, 0:3 * P]
                    else:
                        dve.wait_ge(sums0_done, u * 4 + 4 + 1)
                        rec = sums0[:, P:4 * P]
                    ins = nc.vector.tensor_tensor(o, o, rec.rearrange("p (t c) -> p t c", t=3), ALU.mult)
                    if c < QT - 1:
                        R0.read(ins, "rec", s, c)
                    else:
                        ins.then_inc(sums0_read, 1)
                for t in range(3):
                    dve.wait_ge(o0_hi, u * 3 + (t + 1))
                    dst = q0L[:, t] if t < 2 else q0H[64:P, 2]
                    r = slice(0, P) if t < 2 else slice(64, P)
                    nc.vector.tensor_tensor(dst, o0[r, t], q0H[r, t].bitcast(F32), ALU.subtract).then_inc(o0_lo, 1)

            def output0(b, s):
                for t in range(3):
                    R0.wait_full(dve, b, "wo", s, t)
                    x = X[:, t, half(s)]
                    R0.read(nc.vector.scalar_tensor_tensor(x, R0.bank("wo", s, t)[:], bo0[:, t:t + 1], x, ALU.add,
                                                           ALU.add), "wo", s, t)

            def split1(b, s):
                dve.wait_ge(x1_hi, b * 2 + (s + 1))
                nc.vector.tensor_tensor(X1L[:], X[:, 0:2, half(s)], X1H[:, 0:2].bitcast(F32), ALU.subtract)\
                    .then_inc(x1_lo, 1)
                nc.vector.tensor_tensor(X1H[64:P, 2], X[64:P, 2, half(s)], X1H[64:P, 2].bitcast(F32), ALU.subtract)\
                    .then_inc(x1_lo, 1)

            def project1(b, s):
                u = b * 2 + s
                for t in range(3):
                    dve.wait_ge(q1_hi, u * 3 + (t + 1))
                    r = MQ1[t]
                    R1.read(nc.vector.tensor_tensor(q1L[0:r, t], R1.bank("q", s, t)[0:r], q1H[0:r, t].bitcast(F32),
                                                    ALU.subtract), "q", s, t)

            def maxima1(b, s):
                R1.wait_before(dve, b, s, "maxT", 0)
                for qt in range(QT):
                    R1.wait_full(dve, b, "max", s, qt)
                    R1.read(nc.vector.tensor_reduce(
                        nmax1[:, qt], R1.bank("max", s, qt)[:].rearrange("p (h k) -> p h k", k=NK)[:, :, 0:K1],
                        axis=AX.X, op=ALU.max, negate=True), "max", s, qt)

            def normalize1(b, s):
                u = b * 2 + s
                dve.wait_ge(sums1_done, u * 2 + 1)
                nc.vector.reciprocal(rec1[:], sums1[:, 0:P]).then_inc(sums1_read, 1)
                R1.wait_read(dve, b, "pv", s, 2)
                r = ROWS1[0]
                for c in range(QT):
                    o = o1[0:r, :, P * c:P * c + P]
                    if c < QT - 1:
                        R1.wait_full(dve, b, "rec", s, c)
                        rec = R1.bank("rec", s, c)[0:r, 0:3 * P]
                    else:
                        dve.wait_ge(sums1_done, u * 2 + 2)
                        rec = sums1[0:r, P:4 * P]
                    ins = nc.vector.tensor_tensor(o, o, rec.rearrange("p (t c) -> p t c", t=3), ALU.mult)
                    if c < QT - 1:
                        R1.read(ins, "rec", s, c)
                    else:
                        ins.then_inc(sums1_read, 1)
                for t in range(3):
                    r = ROWS1[t]
                    dve.wait_ge(o1_hi, u * 3 + (t + 1))
                    nc.vector.tensor_tensor(q1L[0:r, t], o1[0:r, t], q1H[0:r, t].bitcast(F32), ALU.subtract)\
                        .then_inc(o1_lo, 1)

            def output1(b, s):
                for t in range(3):
                    r = FT[t]
                    R1.wait_full(dve, b, "wo", s, t)
                    x = x1T[0:r, t, half(s)]
                    R1.read(nc.vector.scalar_tensor_tensor(x, R1.bank("wo", s, t)[0:r], bo1[0:r, t:t + 1], x, ALU.add,
                                                           ALU.add), "wo", s, t)

            def channel_maxima(b, part):
                for m in tiles_of_part(part):
                    for s in range(2):
                        R1.wait_full(dve, b, "cmax", m, s)
                        R1.read(nc.vector.tensor_reduce(cmax2[:, m, s:s + 1], R1.bank("cmax", m, s)[:], axis=AX.X,
                                                        op=ALU.max), "cmax", m, s)

            def channel_shift(b, _):
                R1.wait_read(dve, b, "cmax", HC // P - 1, 1)
                nc.vector.tensor_reduce(cmax[:], cmax2[:], axis=AX.X, op=ALU.max, negate=True).then_inc(cmax_ready, 1)

            def tokens(b, _):
                done = [0]

                def link(ins):
                    ins.then_inc(dve_ca, 1)
                    done[0] += 1
                    dve.wait_ge(dve_ca, b * DVE_CA + done[0])

                for c in range(2):
                    R1.wait_full(dve, b, "cnat", c)
                    bk = R1.bank("cnat", c)[0:CH].rearrange("p (h d) -> p h d", h=H1)
                    link(nc.vector.reciprocal(crec[:, c].unsqueeze(2), bk[:, :, D1:D1 + 1]))
                    R1.read(nc.vector.tensor_tensor(hs[:, c], bk[:, :, 0:D1],
                                                    crec[:, c].unsqueeze(2).to_broadcast([CH, H1, D1]), ALU.mult),
                            "cnat", c)
                R1.wait_full(dve, b, "cs3")
                sc = R1.bank("cs3")[0:CH, 0:2 * HT].rearrange("p (c h t) -> p c h t", c=2, t=T)
                link(nc.vector.tensor_reduce(m3[:], sc, axis=AX.X, op=ALU.max))
                R1.read(nc.vector.tensor_tensor(d3[:], sc, m3[:].unsqueeze(3).to_broadcast([CH, 2, H1, T]),
                                                ALU.subtract), "cs3")
                dve.wait_ge(act_ca, b * ACT_CA + ACT_CA)
                link(nc.vector.tensor_reduce(s3[:], e3[:], axis=AX.X, op=ALU.add))
                link(nc.vector.reciprocal(r3[:], s3[:]))
                link(nc.vector.tensor_tensor(p3[:], e3[:], r3[:].unsqueeze(3).to_broadcast([CH, 2, H1, T]), ALU.mult))
                pf = p3[:].rearrange("p c h t -> p c (h t)")
                link(nc.vector.tensor_copy(P3[:, :, 0], pf))
                link(nc.vector.tensor_copy(P3[:, :, 2], pf))
                link(nc.vector.tensor_tensor(P3[:, :, 1], pf, P3[:, :, 0].bitcast(F32), ALU.subtract))
                assert done[0] == DVE_CA

            def final(b, s):
                for t in range(3):
                    r = FT[t]
                    x = x1T[0:r, t, half(s)]
                    R1.wait_full(dve, b, "fin", s, t)
                    R1.read(nc.vector.tensor_tensor(x, R1.bank("fin", s, t)[0:r], x, ALU.add), "fin", s, t)

            run(dve, {"split1": split1, "project0": project0, "maxima0": maxima0, "normalize0": normalize0, "output0": output0,
                      "project1": project1, "maxima1": maxima1, "normalize1": normalize1, "output1": output1,
                      "channel_maxima": channel_maxima, "channel_shift": channel_shift, "tokens": tokens, "final": final})

        @block.tensor
        def _(pe):
            pe.wait_ge(const_here, 16 * len(consts))
            pe.wait_ge(const_set, 4)

            def products(ring, b, name, rows, parts, cols=HALF):
                ring.wait_free(pe, b, *name)
                for i, (lhsT, rhs) in enumerate(parts):
                    last = nc.tensor.matmul(ring.bank(*name)[0:rows, 0:cols], lhsT, rhs, start=(i == 0),
                                            stop=(i == len(parts) - 1))
                ring.filled(last, *name)

            def split_parts(WH, WL, XH, XL, m):
                return ([(WH[:, k, m], XH[:, k]) for k in range(3)] + [(WH[:, k, m], XL[:, k]) for k in range(2)]
                        + [(WL[:, k, m], XH[:, k]) for k in range(2)] + [(WL[0:64, 2, m], XH[0:64, 2])])

            def project0(b, s):
                u = b * 2 + s
                pe.wait_ge(x_lo, u * 2 + 2)
                for t in range(3):
                    products(R0, b, ("q", s, t), P, split_parts(WqH, WqL, XH, XL, slice(P * t, P * t + P)))

            def maxima0(b, s):
                u = b * 2 + s
                pe.wait_ge(q0_hi, u * 3 + 3)
                pe.wait_ge(pack0_here, b * 48 + 48)
                for qp in range(QT // 2):
                    for i in range(2):
                        qt = 2 * qp + i
                        for t in range(2):
                            products(R0, b, ("max", s, qt, t), P,
                                     [(q0H[:, t, P * qt:P * qt + P], KB0H[:, 8 * t:8 * t + 8].rearrange("p h k -> p (h k)"))])
                    R0.wait_free(pe, b, "max2", s, qp)
                    for i in range(2):
                        qt = 2 * qp + i
                        last = nc.tensor.matmul(R0.bank("max2", s, qp)[:, 256 * i:256 * i + 256],
                                                q0H[0:64, 2, P * qt:P * qt + P],
                                                KB0H[0:64, 16:H0].rearrange("p h k -> p (h k)"), start=True, stop=True)
                    R0.filled(last, "max2", s, qp)
                R0.wait_read(pe, b, "max2", s, QT // 2 - 1)
                R0.wait_free(pe, b, "maxT", s)
                for qt in range(QT):
                    last = nc.tensor.transpose(R0.bank("maxT", s)[0:H0, P * qt:P * qt + P], nmax0[:, qt], ident[:])
                R0.filled(last, "maxT", s)

            def attend0(b, s):
                u = b * 2 + s
                pe.wait_ge(sums0_read, u * 2 + 1)
                R0.wait_read(pe, b, "maxT", s)
                for t in range(3):
                    for p in pairs_of(t):
                        kh = KB0H[:, 2 * p:2 * p + 2].rearrange("p h k -> p (h k)")
                        kl = KB0L[:, 2 * p:2 * p + 2].rearrange("p h k -> p (h k)")
                        parts = ([(kh, q0H[:, t]), (kh, q0L[:, t]), (kl, q0H[:, t])] if t < 2 else
                                 [(kh, q0H[:, t]), (kl[0:FT[2]], q0H[0:FT[2], t])])
                        products(R0, b, ("sT", s, p), P, parts + [(ones0[:, p], nmaxT0[:])])
                    for p in pairs_of(t):
                        R0.wait_read(pe, b, "sT", s, p)
                    R0.wait_free(pe, b, "pv", s, t)
                    for j in range(GROUP):
                        p = GROUP * t + j % len(pairs_of(t))
                        last = nc.tensor.matmul(R0.bank("pv", s, t)[32 * j:32 * j + 32], V0[:, 32 * p:32 * p + 32],
                                                P0[:, p % SLOTS], start=True, stop=True)
                    R0.filled(last, "pv", s, t)
                    for p in pairs_of(t):
                        for c in range(QT):
                            last = nc.tensor.matmul(sums0[32 * c:32 * c + 32, 0:P], OH0[:, p],
                                                    P0[:, p % SLOTS, P * c:P * c + P], start=(p == 0),
                                                    stop=(p == PAIRS0 - 1))
                    last.then_inc(sums0_done, 1)

            def normalize0(b, s):
                u = b * 2 + s
                pe.wait_ge(sums0_read, u * 2 + 1 + 1)
                for c in range(QT):
                    if c < QT - 1:
                        R0.wait_free(pe, b, "rec", s, c)
                        dst = R0.bank("rec", s, c)[:, 0:3 * P]
                    else:
                        dst = sums0[:, P:4 * P]
                    for t in range(3):
                        last = nc.tensor.matmul(dst[:, P * t:P * t + P], E0[32 * c:32 * c + H0, P * t:P * t + P],
                                                rec0[32 * c:32 * c + H0], start=True, stop=True)
                    if c < QT - 1:
                        R0.filled(last, "rec", s, c)
                    else:
                        last.then_inc(sums0_done, 1)

            def output0(b, s):
                u = b * 2 + s
                pe.wait_ge(o0_lo, u * 3 + 3)
                for t in range(3):
                    products(R0, b, ("wo", s, t), P, split_parts(WoH, WoL, q0H, q0L, slice(P * t, P * t + P)))

            def project1(b, s):
                u = b * 2 + s
                pe.wait_ge(x1_lo, u * 2 + 2)
                for t in range(3):
                    products(R1, b, ("q", s, t), MQ1[t],
                             split_parts(W1H, W1L, X1H, X1L, slice(120 * t, 120 * t + MQ1[t])))

            def naturals(b, s):
                pe.wait_ge(x1_here, b * 2 + (s + 2))
                for qt in range(QT):
                    R1.wait_free(pe, b, "xn", s, qt)
                    for t in range(3):
                        r = FT[t]
                        last = nc.tensor.transpose(R1.bank("xn", s, qt)[:, P * t:P * t + r],
                                                   x1T[0:r, t, s * HALF + P * qt:s * HALF + P * qt + P], ident[0:r, 0:r])
                    R1.filled(last, "xn", s, qt)

            def maxima1(b, s):
                u = b * 2 + s
                pe.wait_ge(q1_hi, u * 3 + 3)
                pe.wait_ge(pack1_here, b * 96 + 96)
                for qt in range(QT):
                    R1.wait_free(pe, b, "max", s, qt)
                    for t in range(3):
                        n, r = HEADS1[t] * NK, MQ1[t]
                        first = SLOTS1.index((t, HEAD1[t]))
                        last = nc.tensor.matmul(R1.bank("max", s, qt)[:, 192 * t:192 * t + n],
                                                q1H[0:r, t, P * qt:P * qt + P],
                                                KB1H[0:r, first:first + HEADS1[t]].rearrange("p h k -> p (h k)"), start=True,
                                                stop=True)
                    R1.filled(last, "max", s, qt)
                R1.wait_read(pe, b, "max", s, QT - 1)
                R1.wait_free(pe, b, "maxT", s)
                for qt in range(QT):
                    last = nc.tensor.transpose(R1.bank("maxT", s)[0:H1, P * qt:P * qt + P], nmax1[:, qt], ident[:])
                R1.filled(last, "maxT", s)

            def scores1(b, s):
                R1.wait_read(pe, b, "maxT", s)
                for p in range(PAIRS1):
                    parts = []
                    for i, (t, pp) in enumerate(COMBOS):
                        if pp == p:
                            r = ROWS1[t]
                            kh = KB1H[0:r, 2 * i:2 * i + 2].rearrange("p h k -> p (h k)")
                            kl = KB1L[0:r, 2 * i:2 * i + 2].rearrange("p h k -> p (h k)")
                            parts += [(kh, q1H[0:r, t]), (kh, q1L[0:r, t]), (kl, q1H[0:r, t])]
                    products(R1, b, ("sT", s, p), P, parts + [(ones1[:, p], nmaxT1[:])])

            def values1(b, s):
                for p in range(PAIRS1):
                    R1.wait_read(pe, b, "sT", s, p)
                for t in range(3):
                    r = ROWS1[t]
                    products(R1, b, ("pv", s, t), r, [(V1[:, i, 0:r], P1[:, p]) for i, (tt, p) in enumerate(COMBOS)
                                                      if tt == t])
                pe.wait_ge(sums1_read, b * USES1 + 2 * s + 1)
                for p in range(PAIRS1):
                    for c in range(QT):
                        last = nc.tensor.matmul(sums1[32 * c:32 * c + 32, 0:P], OH1[:, p], P1[:, p, P * c:P * c + P],
                                                start=(p == 0), stop=(p == PAIRS1 - 1))
                last.then_inc(sums1_done, 1)

            def normalize1(b, s):
                pe.wait_ge(sums1_read, b * USES1 + (2 * s + 1) + 1)
                r = ROWS1[0]
                for c in range(QT):
                    if c < QT - 1:
                        R1.wait_free(pe, b, "rec", s, c)
                        dst = R1.bank("rec", s, c)[0:r, 0:3 * P]
                    else:
                        dst = sums1[0:r, P:4 * P]
                    for t in range(3):
                        last = nc.tensor.matmul(dst[:, P * t:P * t + P], E1[32 * c:32 * c + H1, P * t:P * t + r],
                                                rec1[32 * c:32 * c + H1], start=True, stop=True)
                    if c < QT - 1:
                        R1.filled(last, "rec", s, c)
                    else:
                        last.then_inc(sums1_done, 1)

            def output1(b, s):
                u = b * 2 + s
                pe.wait_ge(o1_lo, u * 3 + 3)
                for t in range(3):
                    m = slice(P * t, P * t + FT[t])
                    parts = [(W[0:ROWS1[k], k, m], X[0:ROWS1[k], k]) for W, X in
                             ((W2H, q1H), (W2H, q1L), (W2L, q1H)) for k in range(3)]
                    products(R1, b, ("wo", s, t), FT[t], parts)

            def channel_maxima(b, part):
                pe.wait_ge(gs_here, b * 96 + 96 + 1)
                for m in tiles_of_part(part):
                    for s in range(2):
                        products(R1, b, ("cmax", m, s), P, [(CAS[0:HT, P * m:P * m + P], GS[0:HT, half(s)])])

            def channel_shift(b, _):
                pe.wait_ge(cmax_ready, b + 1)
                R1.wait_free(pe, b, "cmaxT")
                R1.filled(nc.tensor.transpose(R1.bank("cmaxT")[0:HC // P, 0:P], cmax[:], ident[:]), "cmaxT")

            def channel_values(b, part):
                pe.wait_ge(cas_here, b * 16 + 16)

                def values(p, kt):
                    n = p * KT + kt
                    if kt == 0:
                        pe.wait_ge(sums1_read, b * USES1 + (4 + p) + 1)
                    R1.wait_read(pe, b, "csT", p, kt)
                    for i in range(2):
                        last = nc.tensor.matmul(sums1[64 * i:64 * i + D1 + 1, 0:C], X1N[:, kt, 2 * p + i],
                                                PCA[:, n % SLOTS, C * i:C * i + C], start=(kt == 0),
                                                stop=(kt == KT - 1))
                    last.then_inc(pca_used, 1)

                steps = [(p, kt) for p in pairs_of_part(part) for kt in range(KT)]
                for n, (p, kt) in enumerate(steps):
                    products(R1, b, ("csT", p, kt), P, [(GS[:, P * kt:P * kt + P], CAS[:, PC * p:PC * p + PC])], PC)
                    if n >= 2:
                        values(*steps[n - 2])
                values(*steps[-2])
                values(*steps[-1])

            def tokens(b, _):
                pe.wait_ge(sums1_read, b * USES1 + USES1 + 1)
                for c in range(2):
                    R1.wait_free(pe, b, "cnat", c)
                    for p in range(PAIRS1):
                        last = nc.tensor.transpose(R1.bank("cnat", c)[0:CH, P * p:P * p + P],
                                                   CO[:, p, CH0[c]:CH0[c] + CH], ident[:])
                    R1.filled(last, "cnat", c)
                for c in range(2):
                    R1.wait_read(pe, b, "cnat", c)
                    R1.wait_free(pe, b, "cnT", c)
                    for t in range(3):
                        r = FT[t]
                        last = nc.tensor.transpose(R1.bank("cnT", c)[0:r, CH * t:CH * t + CH],
                                                   hs[:, c].rearrange("p h d -> p (h d)")[:, P * t:P * t + r],
                                                   ident[0:CH, 0:CH])
                    R1.filled(last, "cnT", c)
                R1.wait_free(pe, b, "cs3")
                for c in range(2):
                    R1.wait_read(pe, b, "cnT", c)
                    for t in range(3):
                        r = FT[t]
                        last = nc.tensor.matmul(R1.bank("cs3")[0:CH, HT * c:HT * c + HT], hsT[0:r, c, t], A3[0:r, t],
                                                start=(t == 0), stop=(t == 2))
                R1.filled(last, "cs3")

            def spread(b, _):
                pe.wait_ge(dve_ca, b * DVE_CA + DVE_CA)
                for s in range(2):
                    products(R1, b, ("cexp", s), 96, [(P3[:, s].rearrange("p g k -> p (g k)"), EX[:, s])])

            def final(b, s):
                R1.wait_read(pe, b, "cexp", s)
                for t in range(3):
                    products(R1, b, ("fin", s, t), FT[t], [(VW[:, P * t:P * t + FT[t]], P3S[:, s])])

            run(pe, {"project0": project0, "maxima0": maxima0, "attend0": attend0, "normalize0": normalize0,
                     "output0": output0, "project1": project1, "naturals": naturals, "maxima1": maxima1, "scores1": scores1,
                     "values1": values1, "normalize1": normalize1, "output1": output1,
                     "channel_maxima": channel_maxima, "channel_shift": channel_shift,
                     "channel_values": channel_values, "tokens": tokens, "spread": spread, "final": final})


def program(nc, a, out):
    shapes = {"KB0H": [P, H0, NK], "KB0L": [P, H0, NK], "V0": [P, F], "KB1H": [P, len(SLOTS1), NK],
              "KB1L": [P, len(SLOTS1), NK], "V1": [P, len(COMBOS), P], "A3": [P, 3, HT], "VW": [96, F], "CAS": [96, HC]}
    scr = {k: nc.dram_tensor(f"scratch_{k}", [B] + s, F32, kind="Internal").ap() for k, s in shapes.items()}
    with ExitStack() as ctx:
        w = {}
        for k, n in (("Wq0", 3 * P), ("Wo0", 3 * P), ("W1", 368), ("W2", F)):
            for part in "HL":
                w[k + part] = ctx.enter_context(nc.sbuf_tensor(f"{k}{part}", [P, 3, n], F32R))
        w["EX"] = ctx.enter_context(nc.sbuf_tensor("EX_split", [CH, 2, HALF], F32R))
        w["ones0"] = ctx.enter_context(nc.sbuf_tensor("ones0_sb", [H0, PAIRS0, P], F32R))
        w["ones1"] = ctx.enter_context(nc.sbuf_tensor("ones1_sb", [H1, PAIRS1, P], F32R))
        prologue(nc, a, scr, w)
        layers(nc, a, scr, w, out)



def tiles(x, sizes, rows=P, at=None):
    import numpy as np
    out = np.zeros((rows, len(sizes)) + x.shape[1:], np.float32)
    r = 0
    for t, n in enumerate(sizes):
        out[0:n, t] = x[r:r + n]
        r += n
    return out


def doubled(x):
    import numpy as np
    return tiles(np.concatenate([x, x[2 * P:]], 0), [P, P, P])


def shape_constants():
    import numpy as np
    f = np.float32
    c = {}
    part = np.arange(P)
    c["ident"] = np.eye(P, dtype=f)
    head = np.arange(H0)
    row = np.where(head[None] < 16, part[:, None], part[:, None] % FT[2]) // D0
    c["mKB0"] = np.repeat((row == head[None] % 8).astype(f)[:, :, None], NK, 2)
    k1 = np.zeros((P, len(SLOTS1), NK), f)
    m8 = np.zeros((P, 3, H1), f)
    for t in range(3):
        for j in range(HEADS1[t]):
            k1[D1 * j:D1 * j + D1, SLOTS1.index((t, HEAD1[t] + j)), 0:K1] = 1
            m8[D1 * j:D1 * j + D1, t, 3 * t + j] = 1
    c["mKB1"], c["m8"] = k1, m8
    feat = np.arange(F)
    c["mV0"] = ((feat[None] // D0) % 2 == part[:, None] // NK).astype(f)
    v1 = np.zeros((P, len(COMBOS), P), f)
    for i, (t, p) in enumerate(COMBOS):
        for m in range(ROWS1[t]):
            h = 3 * t + m // D1
            if h // 2 == p:
                v1[NK * (h % 2):NK * (h % 2) + K1, i, m] = 1
    c["mV1"] = v1
    ones0 = np.zeros((H0, PAIRS0, 2, NK), f)
    for h in range(H0):
        ones0[h, h // 2, h % 2] = 1
    c["ones0"] = ones0.reshape(H0, PAIRS0, P)
    ones1 = np.zeros((H1, PAIRS1, 2, NK), f)
    for h in range(H1):
        ones1[h, h // 2, h % 2, 0:K1] = 1
    c["ones1"] = ones1.reshape(H1, PAIRS1, P)
    oh0 = np.ones((P, PAIRS0, 32), f)
    oh0[:, :, 0:H0] = 0
    oh1 = np.ones((P, PAIRS1, 32), f)
    oh1[:, :, 0:H1] = 0
    for i in range(2):
        for p in range(PAIRS0):
            oh0[NK * i:NK * i + NK, p, 2 * p + i] = 1
        for p in range(PAIRS1):
            oh1[NK * i:NK * i + K1, p, 2 * p + i] = 1
    c["OH0"], c["OH1"] = oh0, oh1
    e0, e1 = np.zeros((P, 3 * P), f), np.zeros((P, 3 * P), f)
    doubled_feature = np.concatenate([feat, feat[2 * P:]])
    for q in range(QT):
        for m, ft in enumerate(doubled_feature):
            e0[32 * q + ft // D0, m] = 1
        for t in range(3):
            for m in range(ROWS1[t]):
                e1[32 * q + HEAD1[t] + m // D1, P * t + m] = 1
    c["E0"], c["E1"] = e0, e1
    channel = np.linspace(0, C - 1, S).astype(np.int64)
    ex = np.zeros((CH, 2, HALF), f)
    for i in range(S):
        ex[channel[i] - CH0[i // HALF], i // HALF, i % HALF] = 1
    c["EX"] = ex
    return c


def kernel(x, ctx_768, L0_xattn_Wq, L0_xattn_Wk, L0_xattn_Wv, L0_xattn_Wo, L0_xattn_bo, L1_xattn_Wq, L1_xattn_Wk,
           L1_xattn_Wv, L1_xattn_Wq_ca, L1_xattn_Wk_ca, L1_xattn_Wv_ca, L1_xattn_Wout, L1_xattn_b_out):
    import numpy as np
    import concourse.bacc as bacc
    from concourse.bass_utils import run_bass_kernel_spmd

    def host(v):
        return np.asarray(v)

    x, ctx = host(x), host(ctx_768)
    Wq1 = host(L1_xattn_Wq)
    arrays = shape_constants()
    arrays["xT"] = doubled(x.reshape(B * S, F).T)
    ctxT = ctx.transpose(2, 0, 1).reshape(2, KC, B, NK).transpose(1, 0, 2, 3)
    arrays["ctxD"] = np.concatenate([ctxT, ctxT], 3)

    def context_rows(w):
        return w.reshape(2, KC, w.shape[1]).transpose(1, 0, 2)

    def wide(w):
        return np.concatenate([w, w[:, 2 * P:]], 1)

    arrays["Wk0"] = context_rows(wide(host(L0_xattn_Wk)))
    wk1 = np.zeros((C, 368), np.float32)
    wk1[:, 0:F] = host(L1_xattn_Wk)
    arrays["Wk1"] = context_rows(wk1)
    arrays["Wv0"], arrays["Wv1"] = context_rows(host(L0_xattn_Wv)), context_rows(host(L1_xattn_Wv))
    arrays["Wkca"], arrays["Wvca"] = context_rows(host(L1_xattn_Wk_ca)), context_rows(host(L1_xattn_Wv_ca))
    arrays["Wq0"] = doubled(wide(host(L0_xattn_Wq)))
    arrays["Wo0"] = doubled(wide(host(L0_xattn_Wo)))
    w1 = np.zeros((F, 368), np.float32)
    w1[:, 0:F] = Wq1
    wca = host(L1_xattn_Wq_ca)
    for h in range(H1):
        for t in range(T):
            w1[D1 * h:D1 * h + D1, 336 + T * h + t] = wca[t, D1 * h:D1 * h + D1]
    arrays["W1"] = doubled(w1)
    arrays["Wq1T"] = tiles(Wq1.T, ROWS1)
    arrays["W2"] = tiles(host(L1_xattn_Wout), ROWS1)
    car = np.zeros((3, H1, T, B, H1, C), np.float32)
    for h in range(H1):
        car[:, h, :, :, h] = ctx[:, K1:].transpose(1, 0, 2)
    arrays["car"] = car.reshape(3 * HT, B, HC)
    for name, bias in (("bo0", L0_xattn_bo), ("bo1", L1_xattn_b_out)):
        arrays[name] = doubled(host(bias).reshape(F, 1))[:, :, 0]

    nc = bacc.Bacc("TRN2", target_bir_lowering=False, num_devices=1)
    arrays = {k: np.ascontiguousarray(v) for k, v in arrays.items()}
    a = {k: nc.dram_tensor(f"in_{k}", v.shape, mybir.dt.from_np(v.dtype), kind="ExternalInput").ap()
         for k, v in arrays.items()}
    out = nc.dram_tensor("out_T", (P, 3, B * S), F32, kind="ExternalOutput").ap()
    program(nc, a, out)
    r = run_bass_kernel_spmd(nc, [{f"in_{k}": v for k, v in arrays.items()}], core_ids=[0])
    y = r.results[0]["out_T"].reshape(P, 3, B * S)
    y = np.concatenate([y[:, 0], y[:, 1], y[0:FT[2], 2]], 0)
    return np.ascontiguousarray(y.T).reshape(B, S, F)
```

```python
from contextlib import ExitStack

import concourse.bass as bass
from concourse import mybir

F32 = mybir.dt.float32
F32R = mybir.dt.float32r
ALU = mybir.AluOpType
ACT = mybir.ActivationFunctionType
AX = mybir.AxisListType

B, S, F, C, NK = 4, 1024, 320, 192, 64
P = 128
HALF = 512
H0, D0 = 20, 16
H1, D1 = 8, 40
T = 4
K1 = NK - T
PAIRS0, PAIRS1 = H0 // 2, H1 // 2
GROUP = 4
QT = HALF // P
KT = S // P
SCALE0 = float(D0) ** -0.5
SCALE1 = float(D1) ** -0.5
KC = C // 2
HC = H1 * C
PC = 2 * C
HT = H1 * T
CH = C // 2 + 1
CH0 = [0, C - CH]
TILE1 = 3 * D1
ROWS1 = [3 * D1, 3 * D1, 2 * D1]
HEADS1 = [3, 3, 2]
COMBOS = [(0, 0), (0, 1), (1, 1), (1, 2), (2, 3)]
HEAD1 = [0, 3, 6]
SLOTS1 = [(t, 2 * p + i if 2 * p + i in range(HEAD1[t], HEAD1[t] + HEADS1[t]) else None) for t, p in COMBOS
          for i in range(2)]
FT = [P, P, F - 2 * P]
SLOTS = 4
XW = D1 + 1


class Ring:

    def __init__(self, names, banks, full, free):
        self.banks, self.full, self.free = banks, full, free
        self.names = list(names)
        assert len(self.names) % len(banks) == 0, len(self.names)
        self.per = len(self.names) // len(banks)
        self.at = {n: i for i, n in enumerate(self.names)}

    def bank(self, *name):
        return self.banks[self.at[name] % len(self.banks)]

    def wait_free(self, eng, b, *name):
        i = self.at[name]
        eng.wait_ge(self.free[i % len(self.banks)], b * self.per + (i // len(self.banks) + 1))

    def filled(self, ins, *name):
        ins.then_inc(self.full[self.at[name] % len(self.banks)], 1)

    def wait_full(self, eng, b, *name):
        i = self.at[name]
        eng.wait_ge(self.full[i % len(self.banks)], b * self.per + (i // len(self.banks) + 1))

    def read(self, ins, *name):
        ins.then_inc(self.free[self.at[name] % len(self.banks)], 1)

    def wait_read(self, eng, b, *name):
        i = self.at[name]
        eng.wait_ge(self.free[i % len(self.banks)], b * self.per + (i // len(self.banks) + 2))

    def wait_last(self, eng, b, *name):
        i = self.at[name]
        if isinstance(b, int) and b == 0:
            return
        eng.wait_ge(self.free[i % len(self.banks)], b * self.per + (i // len(self.banks) + 2 - self.per))

    def wait_before(self, eng, b, s, *name):
        if s:
            self.wait_read(eng, b, *name)
        else:
            eng.wait_ge(self.free[(len(self.names) - 1) % len(self.banks)], b * self.per + 1)


ATTEND0 = ([("sT", 0), ("sT", 1), ("sT", 2), ("sT", 3)], [("sT", 4), ("sT", 5), ("pv", 0)],
           [("sT", 6), ("sT", 7)], [("sT", 8), ("sT", 9), ("pv", 1)], [("pv", 2)])


def ring0_order():
    for s in range(2):
        yield from (("q", s, t) for t in range(3))
        for qp in range(QT // 2):
            yield from (("max", s, 2 * qp + i, t) for i in range(2) for t in range(2))
            yield ("max2", s, qp)
        yield ("maxT", s)
        yield from ((what, s, i) for part in ATTEND0 for what, i in part)
        yield from (("rec", s, t) for t in range(3))
        yield from (("wo", s, t) for t in range(3))


def ring1_order():
    for s in range(2):
        yield from (("q", s, t) for t in range(3))
        yield from (("xn", s, qt) for qt in range(QT))
        yield from (("max", s, qt) for qt in range(QT))
        yield ("maxT", s)
        names = {"values1": "pv", "normalize1": "rec"}
        for name, _, *which in STEADY:
            if name in ("scores1", "output1") and which[0] == s:
                yield ("sT" if name == "scores1" else "wo", s, which[1])
            elif name in names and which[0] == s:
                yield from ((names[name], s, i) for i in range(3))
            elif name == "channel_maxima" and s == 1:
                n = HC // P // CMAX_PARTS
                yield from (("cmax", m, i) for m in range(n * which[0], n * which[0] + n) for i in range(2))
    yield ("cmaxT",)
    yield from (("csT", p, kt) for p in range(PAIRS1) for kt in range(KT))
    yield from (("cnat", c) for c in range(2))
    yield from (("cnT", c) for c in range(2))
    yield ("cs3",)
    yield from (("cexp", s) for s in range(2))
    yield from (("fin", s, t) for s in range(2) for t in range(3))


PRELUDE = [("load0", 0), ("split0", 0, 0), ("blocks0", 0), ("project0", 0, 0, 0), ("project0", 0, 0, 1),
           ("project0", 0, 0, 2), ("load1", 0), ("maxima0", 0, 0, 0), ("split0", 0, 1), ("maxima0", 0, 0, 1),
           ("maxima0", 0, 0, 2), ("maxima0", 0, 0, 3), ("shift0", 0, 0), ("attend0", 0, 0, 0), ("blocks1", 0),
           ("attend0", 0, 0, 1), ("attend0", 0, 0, 2), ("attend0", 0, 0, 3), ("attend0", 0, 0, 4),
           ("reciprocals0", 0, 0), ("normalize0", 0, 0), ("split_o0", 0, 0), ("output0", 0, 0, 0),
           ("output0", 0, 0, 1), ("output0", 0, 0, 2), ("split1", 0, 0), ("project0", 0, 1, 0), ("project0", 0, 1, 1),
           ("project0", 0, 1, 2), ("handover", 0, 0), ("project1", 0, 0, 0), ("maxima0", 0, 1, 0),
           ("project1", 0, 0, 1), ("maxima0", 0, 1, 1), ("project1", 0, 0, 2), ("maxima0", 0, 1, 2),
           ("maxima0", 0, 1, 3), ("naturals", 0, 0, 0), ("naturals", 0, 0, 1), ("naturals", 0, 0, 2),
           ("naturals", 0, 0, 3), ("shift0", 0, 1), ("maxima1", 0, 0, 0), ("maxima1", 0, 0, 1), ("maxima1", 0, 0, 2),
           ("maxima1", 0, 0, 3), ("attend0", 0, 1, 0), ("shift1", 0, 0), ("attend0", 0, 1, 1), ("scores1", 0, 0, 0),
           ("scores1", 0, 0, 1), ("attend0", 0, 1, 2), ("scores1", 0, 0, 2), ("scores1", 0, 0, 3),
           ("attend0", 0, 1, 3), ("values1", 0, 0), ("reciprocals1", 0, 0), ("attend0", 0, 1, 4),
           ("reciprocals0", 0, 1), ("normalize0", 0, 1), ("split_o0", 0, 1), ("normalize1", 0, 0), ("split_o1", 0, 0),
           ("output0", 0, 1, 0), ("output0", 0, 1, 1), ("output0", 0, 1, 2), ("split1", 0, 1), ("output1", 0, 0, 0),
           ("output1", 0, 0, 1), ("output1", 0, 0, 2)]
STEADY = [("handover", 0, 1), ("load_x", 1, 0), ("load0", 1), ("blocks0", 1), ("project1", 0, 1, 0),
          ("project1", 0, 1, 1), ("split0", 1, 0), ("project1", 0, 1, 2), ("naturals", 0, 1, 0),
          ("naturals", 0, 1, 1), ("naturals", 0, 1, 2), ("naturals", 0, 1, 3), ("maxima1", 0, 1, 0), ("load_x", 1, 1),
          ("maxima1", 0, 1, 1), ("maxima1", 0, 1, 2), ("project0", 1, 0, 0), ("project0", 1, 0, 1),
          ("maxima1", 0, 1, 3), ("project0", 1, 0, 2), ("shift1", 0, 1), ("scores1", 0, 1, 0), ("scores1", 0, 1, 1),
          ("scores1", 0, 1, 2), ("scores1", 0, 1, 3), ("maxima0", 1, 0, 0), ("maxima0", 1, 0, 1),
          ("maxima0", 1, 0, 2), ("channel_maxima", 0, 0), ("maxima0", 1, 0, 3), ("channel_maxima", 0, 1),
          ("values1", 0, 1), ("reciprocals1", 0, 1), ("channel_maxima", 0, 2), ("shift0", 1, 0), ("normalize1", 0, 1),
          ("split_o1", 0, 1), ("channel_maxima", 0, 3), ("attend0", 1, 0, 0), ("output1", 0, 1, 0),
          ("output1", 0, 1, 1), ("output1", 0, 1, 2), ("channel_maxima", 0, 4), ("attend0", 1, 0, 1),
          ("channel_maxima", 0, 5), ("channel_maxima", 0, 6), ("channel_maxima", 0, 7), ("attend0", 1, 0, 2),
          ("channel_maxima", 0, 8), ("channel_maxima", 0, 9), ("attend0", 1, 0, 3), ("channel_maxima", 0, 10),
          ("channel_maxima", 0, 11), ("split0", 1, 1), ("attend0", 1, 0, 4), ("channel_shift", 0),
          ("reciprocals0", 1, 0), ("normalize0", 1, 0), ("channel_values", 0, 0, 0), ("channel_values", 0, 0, 1),
          ("split_o0", 1, 0), ("channel_values", 0, 0, 2), ("channel_values", 0, 0, 3), ("output0", 1, 0, 0),
          ("output0", 1, 0, 1), ("channel_values", 0, 1, 0), ("channel_values", 0, 1, 1), ("channel_values", 0, 1, 2),
          ("output0", 1, 0, 2), ("project0", 1, 1, 0), ("channel_values", 0, 1, 3), ("split1", 1, 0),
          ("project0", 1, 1, 1), ("channel_values", 0, 2, 0), ("channel_values", 0, 2, 1),
          ("channel_values", 0, 2, 2), ("project0", 1, 1, 2), ("maxima0", 1, 1, 0), ("channel_values", 0, 2, 3),
          ("channel_values", 0, 3, 0), ("maxima0", 1, 1, 1), ("channel_values", 0, 3, 1), ("channel_values", 0, 3, 2),
          ("channel_values", 0, 3, 3), ("channel_end", 0), ("tokens", 0), ("tokens_back", 0), ("maxima0", 1, 1, 2),
          ("maxima0", 1, 1, 3), ("token_scores", 0), ("shift0", 1, 1), ("token_softmax", 0), ("attend0", 1, 1, 0),
          ("spread", 0), ("final", 0, 0), ("attend0", 1, 1, 1), ("final", 0, 1), ("project1", 1, 0, 0),
          ("project1", 1, 0, 1), ("attend0", 1, 1, 2), ("handover", 1, 0), ("load1", 1), ("attend0", 1, 1, 3),
          ("project1", 1, 0, 2), ("naturals", 1, 0, 0), ("attend0", 1, 1, 4), ("naturals", 1, 0, 1),
          ("reciprocals0", 1, 1), ("naturals", 1, 0, 2), ("naturals", 1, 0, 3), ("maxima1", 1, 0, 0),
          ("maxima1", 1, 0, 1), ("maxima1", 1, 0, 2), ("blocks1", 1), ("maxima1", 1, 0, 3), ("normalize0", 1, 1),
          ("split_o0", 1, 1), ("shift1", 1, 0), ("output0", 1, 1, 0), ("scores1", 1, 0, 0), ("output0", 1, 1, 1),
          ("scores1", 1, 0, 1), ("scores1", 1, 0, 2), ("scores1", 1, 0, 3), ("values1", 1, 0), ("reciprocals1", 1, 0),
          ("normalize1", 1, 0), ("split_o1", 1, 0), ("output0", 1, 1, 2), ("split1", 1, 1), ("output1", 1, 0, 0),
          ("output1", 1, 0, 1), ("output1", 1, 0, 2)]
CMAX_PARTS = 12
CONSTS = ("bo0", "bo1", "ident", "OH0", "OH1", "E0", "E1", "mKB0", "mKB1", "mCAS")


def prologue(nc, a, scr, w, early, early_here, x_here):
    with ExitStack() as ctx:
        def sb(name, shape, dt=F32):
            return ctx.enter_context(nc.sbuf_tensor(name, shape, dt))

        def sem(name):
            return ctx.enter_context(nc.semaphore(name))

        groups = (("ctxD", "Wk0", "Wk1", "Wkca", "Wvca", "m8"), ("Wq1T", "W2", "Wv0", "Wv1", "mV0", "mV1", "tok"),
                  ("Wq0", "Wo0", "W1", "EX", "ones0", "ones1"))
        raw = {k: sb(f"pro_{k}", list(a[k].shape)) for group in groups for k in group}
        kT = [[sb(f"kT{layer}{part}", [P, 3, B, NK], F32R) for part in "HL"] for layer in range(2)]
        tok = sb("tok_split", [3 * HT, B, C], F32R)
        k3bd, v3bd = sb("k3bd", [P, 3, B, H1, T]), sb("v3bd", [P, 3, B, 3, H1, T])
        V0, V1 = sb("pV0", [P, B, F]), sb("pV1", [P, B, len(COMBOS), P])
        A3 = sb("pA3", [P, 3, B, HT])
        VW = sb("pVW", [3 * HT, B, F], F32R)
        bank = [ctx.enter_context(nc.psum_tensor(f"pbank{i}", [P, HALF], F32)) for i in range(4)]
        loaded = [sem(f"pro_loaded{i}") for i in range(len(groups))]
        filled, read, own = sem("pro_filled"), sem("pro_read"), sem("pro_dve_done")
        weights_hi, tok_ready, stored = sem("pro_weights_hi"), sem("pro_tok_ready"), sem("pro_stored")
        v1_zero, weights_lo = sem("pro_v1_zero"), sem("pro_weights_lo")
        KEY_FILLS, ALL_FILLS = 6, 15 + 3 * B
        block = ctx.enter_context(nc.Block())

        @block.sync
        def _(sp):
            for i, group in enumerate(groups):
                for k in group:
                    sp.dma_start(raw[k][:], a[k]).then_inc(loaded[i], 16)
            sp.wait_ge(read, KEY_FILLS)
            for layer in range(2):
                for part in range(2):
                    for b in range(B):
                        sp.dma_start(scr["KT"][b, layer, :, part], kT[layer][part][:, :, b].bitcast(F32))\
                            .then_inc(stored, 16)
            sp.wait_ge(tok_ready, 2)
            sp.dma_start(scr["TOK"].rearrange("b p c -> p b c"), tok[:].bitcast(F32)).then_inc(stored, 16)
            sp.wait_ge(read, ALL_FILLS)
            sp.dma_start(scr["V0"].rearrange("b p f -> p b f"), V0[:]).then_inc(stored, 16)
            sp.dma_start(scr["VW"].rearrange("b p f -> p b f"), VW[:].bitcast(F32)).then_inc(stored, 16)
            sp.dma_start(scr["V1"].rearrange("b p i f -> p b (i f)"), V1[:].rearrange("p b i f -> p b (i f)"))\
                .then_inc(stored, 16)
            for b in range(B):
                sp.dma_start(scr["A3"][b], A3[:, :, b]).then_inc(stored, 16)
            sp.wait_ge(stored, 16 * (4 * B + 4 + B))

        @block.gpsimd
        def _(pool):
            nc.gpsimd.memset(V1[:], 0.0).then_inc(v1_zero, 1)
            pool.wait_ge(loaded[0], 16 * len(groups[0]))
            for s in range(2):
                pool.dma_start(early["X"][:, :, s * HALF:(s + 1) * HALF], a["xT"][:, :, s * HALF:(s + 1) * HALF])\
                    .then_inc(x_here[s], 16)
            for k in CONSTS:
                pool.dma_start(early[k][:], a[k]).then_inc(early_here, 16)
            pool.wait_ge(v1_zero, 1)
            for i, tile in enumerate((early["GS"][96:97].bitcast(F32), early["X1N"][:])):
                nc.gpsimd.memset(tile, 1.0).then_inc(v1_zero, 1)
                pool.wait_ge(v1_zero, i + 2)
            for i, k in enumerate(("W2", "Wq0", "Wo0", "W1")):
                pool.wait_ge(weights_hi, i + 1)
                nc.gpsimd.tensor_tensor(w[k + "L"][:], raw[k][:], w[k + "H"][:].bitcast(F32), ALU.subtract)\
                    .then_inc(weights_lo, 1)
                pool.wait_ge(weights_lo, i + 1)

        @block.scalar
        def _(act):
            act.wait_ge(loaded[1], 16 * len(groups[1]))
            nc.scalar.copy(tok[:], raw["tok"][:]).then_inc(tok_ready, 1)
            nc.scalar.copy(w["W2H"][:], raw["W2"][:]).then_inc(weights_hi, 1)
            act.wait_ge(loaded[2], 16 * len(groups[2]))
            for k in ("Wq0", "Wo0", "W1"):
                nc.scalar.copy(w[k + "H"][:], raw[k][:]).then_inc(weights_hi, 1)
            for k in ("EX", "ones0", "ones1"):
                nc.scalar.copy(w[k][:], raw[k][:])

        @block.tensor
        def _(pe):
            pe.wait_ge(loaded[0], 16 * len(groups[0]))
            fills = [0]

            def fill(rows, cols, parts):
                n = fills[0]
                if n >= 4:
                    pe.wait_ge(read, n - 3)
                for i, (lhsT, rhs) in enumerate(parts):
                    last = nc.tensor.matmul(bank[n % 4][0:rows, 0:cols], lhsT, rhs, start=(i == 0),
                                            stop=(i == len(parts) - 1))
                last.then_inc(filled, 1)
                fills[0] += 1

            keys = [raw["ctxD"][:, k, :, 0:NK] for k in range(2)]
            toks = [raw["ctxD"][:, k, :, K1:NK] for k in range(2)]
            for name, width in (("Wk0", P), ("Wk1", TILE1)):
                for t in range(3):
                    fill(P, B * NK, [(raw[name][:, k, width * t:width * t + P], keys[k]) for k in range(2)])
            for name in ("Wkca", "Wvca"):
                for t in range(3):
                    fill(ROWS1[t], B * T, [(raw[name][:, k, TILE1 * t:TILE1 * t + ROWS1[t]], toks[k])
                                           for k in range(2)])
            pe.wait_ge(loaded[1], 16 * len(groups[1]))
            pe.wait_ge(read, 12)
            for t in range(3):
                fill(FT[t], B * HT, [(raw["Wq1T"][0:ROWS1[k], k, P * t:P * t + FT[t]],
                                      k3bd[0:ROWS1[k], k].rearrange("p b h t -> p (b h t)")) for k in range(3)])
            for b in range(B):
                for name in ("Wv0", "Wv1"):
                    fill(P, F, [(raw["ctxD"][:, k, b, :], raw[name][:, k, :]) for k in range(2)])
                fill(3 * HT, F, [(v3bd[0:ROWS1[k], k, b].rearrange("p g h t -> p (g h t)"),
                                  raw["W2"][0:ROWS1[k], k, :]) for k in range(3)])

        @block.vector
        def _(dve):
            done = [0]
            fills = [0]

            def link(ins):
                ins.then_inc(own, 1)
                done[0] += 1
                dve.wait_ge(own, done[0])

            def next_fill():
                fills[0] += 1
                dve.wait_ge(filled, fills[0])
                return bank[(fills[0] - 1) % 4]

            link(nc.vector.memset(A3[:], 0.0))
            for x in kT[1]:
                link(nc.vector.memset(x[:, :, :, K1:NK].bitcast(F32), 0.0))
            dve.wait_ge(loaded[0], 16 * len(groups[0]))
            for (hi, lo), n in zip(kT, (NK, K1)):
                for t in range(3):
                    ps = next_fill()[:, 0:B * NK].rearrange("p (b k) -> p b k", b=B)[:, :, 0:n]
                    link(nc.vector.tensor_copy(hi[:, t, :, 0:n], ps))
                    nc.vector.tensor_tensor(lo[:, t, :, 0:n], ps, hi[:, t, :, 0:n].bitcast(F32), ALU.subtract)\
                        .then_inc(read, 1)
            for dst in (k3bd, v3bd):
                for t in range(3):
                    r = ROWS1[t]
                    bk = next_fill()[0:r, 0:B * T].rearrange("p (b t) -> p b t", b=B)
                    for b in range(B):
                        x, m = bk[:, b].unsqueeze(1), raw["m8"][0:r, t].unsqueeze(2)
                        shape = [r, H1, T]
                        if dst is v3bd:
                            x, m, shape = x.unsqueeze(1), m.unsqueeze(1), [r, 3, H1, T]
                        last = nc.vector.tensor_tensor(dst[0:r, t, b], x.to_broadcast(shape), m.to_broadcast(shape),
                                                       ALU.mult)
                    last.then_inc(read, 1)
            dve.wait_ge(v1_zero, 1)
            dve.wait_ge(loaded[1], 16 * len(groups[1]))
            for t in range(3):
                r = FT[t]
                ps = next_fill()[0:r, 0:B * HT].rearrange("p (b h) -> p b h", b=B)
                nc.vector.tensor_copy(A3[0:r, t], ps).then_inc(read, 1)
            dve.wait_ge(tok_ready, 1)
            lo = slice(2 * HT, 3 * HT)
            nc.vector.tensor_tensor(tok[lo], raw["tok"][lo], tok[lo].bitcast(F32), ALU.subtract).then_inc(tok_ready, 1)
            for b in range(B):
                nc.vector.tensor_tensor(V0[:, b], next_fill()[:, 0:F], raw["mV0"][:], ALU.mult).then_inc(read, 1)
                bk = next_fill()
                for i, (t, _) in enumerate(COMBOS):
                    n = ROWS1[t]
                    last = nc.vector.tensor_tensor(V1[:, b, i, 0:n], bk[:, TILE1 * t:TILE1 * t + n],
                                                   raw["mV1"][:, i, 0:n], ALU.mult)
                last.then_inc(read, 1)
                bk = next_fill()
                link(nc.vector.tensor_copy(VW[:, b], bk[0:3 * HT, 0:F]))
                nc.vector.tensor_tensor(VW[lo, b], bk[lo, 0:F], VW[lo, b].bitcast(F32), ALU.subtract).then_inc(read, 1)


def layers(nc, a, scr, w, early, early_here, x_here, out):
    with ExitStack() as ctx:
        def sb(name, shape, dt=F32):
            return ctx.enter_context(nc.sbuf_tensor(name, shape, dt))

        def sem(name):
            return ctx.enter_context(nc.semaphore(name))

        bank = [ctx.enter_context(nc.psum_tensor(f"bank{i}", [P, HALF], F32)) for i in range(8)]
        R0 = Ring(ring0_order(), bank[0:3], [sem(f"l0_bank{i}_full") for i in range(3)],
                  [sem(f"l0_bank{i}_read") for i in range(3)])
        R1 = Ring(ring1_order(), bank[4:7], [sem(f"l1_bank{i}_full") for i in range(3)],
                  [sem(f"l1_bank{i}_read") for i in range(3)])
        sums0, sums1 = bank[3], bank[7]

        WqH, WqL, WoH, WoL, W1H, W1L, W2H, W2L, EX, ones0, ones1 = (
            w[k] for k in ("Wq0H", "Wq0L", "Wo0H", "Wo0L", "W1H", "W1L", "W2H", "W2L", "EX", "ones0", "ones1"))
        bo0, bo1, ident, OH0, OH1, E0, E1, mKB0, mKB1, mCAS = (early[k] for k in CONSTS)
        X, GS, X1N, CO = (early[k] for k in ("X", "GS", "X1N", "CO"))
        KT0, KT1, TOK = sb("KT0", [P, 2, 3, NK]), sb("KT1", [P, 2, 3, NK]), sb("TOK_sb", [3 * HT, C])
        KB0H, KB0L = sb("KB0H_sb", [P, H0, NK], F32R), sb("KB0L_sb", [P, H0, NK], F32R)
        V0 = sb("V0_sb", [P, F])
        KB1H, KB1L = sb("KB1H_sb", [P, len(SLOTS1), NK], F32R), sb("KB1L_sb", [P, len(SLOTS1), NK], F32R)
        V1 = sb("V1_sb", [P, len(COMBOS), P])
        A3 = sb("A3_sb", [P, 3, HT])
        VW = sb("VW_sb", [96, F], F32R)
        CAS = sb("CAS_sb", [97, HC], F32R)
        XH, XL = sb("XH", [P, 3, HALF], F32R), sb("XL", [P, 2, HALF], F32R)
        q0H, q0L = sb("q0H", [P, 3, HALF], F32R), sb("q0L", [P, 2, HALF], F32R)
        o0 = sb("o0", [P, 3, HALF])
        nmax0 = sb("nmax0", [P, QT, H0])
        nmaxT0 = sb("nmaxT0", [H0, HALF], F32R)
        P0 = sb("P0", [P, SLOTS, HALF])
        rec0 = sb("rec0", [P, P])
        x1T = sb("x1T", [P, 3, S])
        X1H, X1L = sb("X1H", [P, 3, HALF], F32R), sb("X1L", [P, 2, HALF], F32R)
        q1H, q1L = sb("q1H", [P, 3, HALF], F32R), sb("q1L", [P, 3, HALF], F32R)
        o1 = sb("o1", [P, 3, HALF])
        nmax1 = sb("nmax1", [P, QT, H1])
        nmaxT1 = sb("nmaxT1", [H1, HALF], F32R)
        P1 = sb("P1", [P, PAIRS1, HALF])
        rec1 = sb("rec1", [P, P])
        cmax2, cmax = sb("cmax2", [P, HC // P, 2]), sb("cmax", [P, HC // P])
        cmaxT = sb("cmaxT", [HC // P, P], F32R)
        PCA = P1
        crec = sb("crec", [CH, 2, H1])
        hs = sb("hs", [CH, 2, H1, D1])
        hsT = o1[:, 0:2, 0:3 * CH].rearrange("p c (t n) -> p c t n", t=3)
        m3, s3, r3 = sb("m3", [CH, 2, H1]), sb("s3", [CH, 2, H1]), sb("r3", [CH, 2, H1])
        d3, e3, p3 = sb("d3", [CH, 2, H1, T]), sb("e3", [CH, 2, H1, T]), sb("p3", [CH, 2, H1, T])
        P3 = sb("P3", [CH, 2, 3, HT], F32R)
        P3S = sb("P3S", [96, 2, HALF], F32R)

        pack0_here, pack1_here, blocks0_ready, blocks1_ready = (
            sem(k) for k in ("pack0_here", "pack1_here", "blocks0_ready", "blocks1_ready"))
        x_hi, x_lo, q0_hi = sem("x_hi"), sem("x_lo"), sem("q0_hi")
        sums0_done, sums0_read, o0_hi, o0_lo = sem("sums0_done"), sem("sums0_read"), sem("o0_hi"), sem("o0_lo")
        x1_here = sem("x1_here")
        x1_hi, x1_lo, q1_hi = sem("x1_hi"), sem("x1_lo"), sem("q1_hi")
        gs_here = sem("gs_here")
        sums1_done, sums1_read = sem("sums1_done"), sem("sums1_read")
        o1_hi, o1_lo = sem("o1_hi"), sem("o1_lo")
        cmax_ready, cas_here, pca_used = sem("cmax_ready"), sem("cas_here"), sem("pca_used")
        dve_ca, act_ca, out_done = sem("dve_ca"), sem("act_ca"), [sem(f"out_done{s}") for s in range(2)]

        USES1 = 4 + PAIRS1
        DVE_CA = 9
        ACT_CA = 2 + 1
        block = ctx.enter_context(nc.Block())

        def kts_of(quarter):
            return range(KT // 4 * quarter, KT // 4 * quarter + KT // 4)

        def tiles_of_part(part):
            n = HC // P // CMAX_PARTS
            return range(n * part, n * part + n)

        def pairs_of(t):
            return range(GROUP * t, min(GROUP * t + GROUP, PAIRS0))

        def half(s):
            return slice(s * HALF, (s + 1) * HALF)

        def scratch(k, b):
            return scr[k][bass.ds(b, 1)].squeeze(0)

        def keys_of(b, layer):
            return scr["KT"][bass.ds(b, 1), layer].squeeze(0)

        def run(eng, steps):
            for name, _, *which in PRELUDE:
                if name in steps:
                    steps[name](0, *which)
            with eng.Fori(0, B - 1) as b:
                for name, ahead, *which in STEADY:
                    if name in steps:
                        steps[name](b + 1 if ahead else b, *which)
            for name, ahead, *which in STEADY:
                if name in steps and not ahead:
                    steps[name](B - 1, *which)

        def wait_last_half(ring, eng, b, s):
            if s:
                ring.wait_read(eng, b, "q", 0, 2)
            else:
                ring.wait_last(eng, b, "q", 1, 2)

        @block.sync
        def _(sp):
            for x in R0.free + R1.free + [gs_here, sums0_read, sums0_done, sums1_read, pca_used, x1_here] + out_done:
                sp.sem_inc(x, 1)

            def load1(b):
                R1.wait_before(sp, b, 0)
                sp.dma_start(KT1[:], keys_of(b, 1)).then_inc(pack1_here, 16)
                sp.dma_start(TOK[:], scratch("TOK", b)).then_inc(pack1_here, 16)
                sp.dma_start(V1[:], scratch("V1", b)).then_inc(pack1_here, 16)
                sp.dma_start(A3[:], scratch("A3", b)).then_inc(pack1_here, 16)
                sp.dma_start(VW[:].bitcast(F32), scratch("VW", b)).then_inc(pack1_here, 16)

            def project1(b, s, t):
                if t < 2:
                    return
                R1.wait_read(sp, b, "q", s, 2)
                for seg, src in enumerate((q1H, q1L, q1H)):
                    sp.dma_start(GS[HT * seg:HT * seg + HT, half(s)].bitcast(F32),
                                 src[96:P, 2].bitcast(F32)).then_inc(gs_here, 16)

            def channel_shift(b):
                R1.wait_read(sp, b, "cmaxT")
                sp.dma_start(CAS[96:97].bitcast(F32), cmaxT[:].bitcast(F32)).then_inc(cas_here, 16)

            def final(b, s):
                R1.wait_read(sp, b, "fin", s, 2)
                cols = bass.ds(b * S + s * HALF, HALF)
                sp.dma_start(out[:, 0:2, cols], x1T[:, 0:2, half(s)]).then_inc(out_done[s], 16)
                sp.dma_start(out[0:FT[2], 2, cols], x1T[0:FT[2], 2, half(s)]).then_inc(out_done[s], 16)

            run(sp, {"load1": load1, "project1": project1, "channel_shift": channel_shift, "final": final})
            for s in range(2):
                sp.wait_ge(out_done[s], B * 32 + 1)

        @block.gpsimd
        def _(pool):
            pool.wait_ge(early_here, 16 * len(CONSTS))

            def load_x(b, s):
                pool.wait_ge(x1_here, b * 2 + s)
                pool.wait_ge(x1_lo, b * 4 + 2 * s - 2)
                pool.dma_start(X[:, :, half(s)], a["xT"][:, :, bass.ds(b * S + s * HALF, HALF)])\
                    .then_inc(x_here[s], 16)

            def load0(b):
                R0.wait_before(pool, b, 0)
                pool.dma_start(KT0[:], keys_of(b, 0)).then_inc(pack0_here, 16)
                pool.dma_start(V0[:], scratch("V0", b)).then_inc(pack0_here, 16)

            def build(ready, b, products):
                for i, (dst, x, y) in enumerate(products):
                    if i:
                        pool.wait_ge(ready, b * len(products) + i)
                    nc.gpsimd.tensor_tensor(dst, x, y, ALU.mult).then_inc(ready, 1)
                pool.wait_ge(ready, b * len(products) + len(products))

            def key_blocks(dst, src, mask, tiles):
                return [(dst[:, c], src[:, t].unsqueeze(1).to_broadcast([P, c.stop - c.start, NK]),
                         mask[:, c].unsqueeze(2).to_broadcast([P, c.stop - c.start, NK])) for t, c in enumerate(tiles)]

            def blocks0(b):
                pool.wait_ge(pack0_here, b * 32 + 32)
                tiles0 = (slice(0, 8), slice(8, 16), slice(16, H0))
                build(blocks0_ready, b, key_blocks(KB0H, KT0[:, 0], mKB0, tiles0)
                      + key_blocks(KB0L, KT0[:, 1], mKB0, tiles0))

            def blocks1(b):
                pool.wait_ge(pack1_here, b * 80 + 80)
                tiles1 = (slice(0, 4), slice(4, 8), slice(8, 10))
                build(blocks1_ready, b, key_blocks(KB1H, KT1[:, 0], mKB1, tiles1)
                      + key_blocks(KB1L, KT1[:, 1], mKB1, tiles1)
                      + [(CAS[0:3 * HT].rearrange("p (h c) -> p h c", h=H1),
                          TOK[:].unsqueeze(1).to_broadcast([3 * HT, H1, C]),
                          mCAS[:].unsqueeze(2).to_broadcast([3 * HT, H1, C]))])

            def split0(b, s):
                pool.wait_ge(x_hi, b * 2 + (s + 1))
                nc.gpsimd.tensor_tensor(XL[:], X[:, 0:2, half(s)], XH[:, 0:2].bitcast(F32), ALU.subtract)\
                    .then_inc(x_lo, 1)
                pool.wait_ge(x_lo, b * 4 + (2 * s + 1))
                nc.gpsimd.tensor_tensor(XH[64:P, 2], X[64:P, 2, half(s)], XH[64:P, 2].bitcast(F32), ALU.subtract)\
                    .then_inc(x_lo, 1)
                pool.wait_ge(x_lo, b * 4 + (2 * s + 2))

            run(pool, {"load_x": load_x, "load0": load0, "blocks0": blocks0, "blocks1": blocks1, "split0": split0})

        @block.scalar
        def _(act):

            def split0(b, s):
                act.wait_ge(x_here[s], b * 16 + 16)
                wait_last_half(R0, act, b, s)
                nc.scalar.copy(XH[:], X[:, :, half(s)]).then_inc(x_hi, 1)

            def project0(b, s, t):
                if t == 0:
                    R0.wait_before(act, b, s, "wo", 0, 2)
                R0.wait_full(act, b, "q", s, t)
                nc.scalar.copy(q0H[:, t], R0.bank("q", s, t)[:]).then_inc(q0_hi, 1)

            def shift0(b, s):
                R0.wait_full(act, b, "maxT", s)
                R0.read(nc.scalar.copy(nmaxT0[:], R0.bank("maxT", s)[0:H0]), "maxT", s)

            def attend0(b, s, part):
                u = b * 2 + s
                for what, i in ATTEND0[part]:
                    R0.wait_full(act, b, what, s, i)
                    if what == "pv":
                        R0.read(nc.scalar.copy(o0[:, i], R0.bank("pv", s, i)[:]), "pv", s, i)
                    else:
                        if i % GROUP == 0:
                            act.wait_ge(sums0_done, u * 4 + (i // GROUP + 1))
                        R0.read(nc.scalar.activation(P0[:, i % SLOTS], R0.bank("sT", s, i)[:], ACT.Exp, scale=SCALE0),
                                "sT", s, i)

            def split_o0(b, s):
                act.wait_ge(sums0_read, (b * 2 + s) * 2 + 2 + 1)
                for t in range(3):
                    nc.scalar.copy(q0H[:, t], o0[:, t]).then_inc(o0_hi, 1)

            def split1(b, s):
                R0.wait_read(act, b, "wo", s, 2)
                wait_last_half(R1, act, b, s)
                nc.scalar.copy(X1H[:], X[:, :, half(s)]).then_inc(x1_hi, 1)

            def handover(b, s):
                R0.wait_read(act, b, "wo", s, 2)
                act.wait_ge(out_done[s], b * 32 + 1)
                nc.scalar.copy(x1T[:, :, half(s)], X[:, :, half(s)]).then_inc(x1_here, 1)

            def project1(b, s, t):
                if t == 0:
                    R1.wait_before(act, b, s, "wo", 0, 2)
                R1.wait_full(act, b, "q", s, t)
                nc.scalar.copy(q1H[:, t], R1.bank("q", s, t)[:]).then_inc(q1_hi, 1)

            def naturals(b, s, qt):
                R1.wait_full(act, b, "xn", s, qt)
                R1.read(nc.scalar.copy(X1N[:, s * QT + qt, 0:H1 * XW].rearrange("p (h d) -> p h d", h=H1)[:, :, 0:D1],
                                       R1.bank("xn", s, qt)[:, 0:F].rearrange("p (h d) -> p h d", h=H1)),
                        "xn", s, qt)

            def shift1(b, s):
                R1.wait_full(act, b, "maxT", s)
                R1.read(nc.scalar.copy(nmaxT1[:], R1.bank("maxT", s)[0:H1]), "maxT", s)

            def scores1(b, s, p):
                if p == 0:
                    R1.wait_before(act, b, s, "wo", 0, 2)
                R1.wait_full(act, b, "sT", s, p)
                R1.read(nc.scalar.activation(P1[:, p], R1.bank("sT", s, p)[:], ACT.Exp, scale=SCALE1), "sT", s, p)

            def values1(b, s):
                for t in range(3):
                    R1.wait_full(act, b, "pv", s, t)
                    R1.read(nc.scalar.copy(o1[:, t], R1.bank("pv", s, t)[:]), "pv", s, t)

            def split_o1(b, s):
                act.wait_ge(gs_here, (b * 2 + s) * 48 + 48 + 1)
                act.wait_ge(sums1_read, b * USES1 + (2 * s + 2) + 1)
                for t in range(3):
                    nc.scalar.copy(q1H[:, t], o1[:, t]).then_inc(o1_hi, 1)

            def channel_shift(b):
                R1.wait_full(act, b, "cmaxT")
                R1.read(nc.scalar.copy(cmaxT[:], R1.bank("cmaxT")[0:HC // P, 0:P]), "cmaxT")

            def keep(b, p):
                act.wait_ge(pca_used, b * (PAIRS1 * KT) + KT * (p + 1) + 1)
                nc.scalar.copy(CO[:, p], sums1[:, 0:C]).then_inc(sums1_read, 1)

            def channel_values(b, p, quarter):
                for kt in kts_of(quarter):
                    if kt == 2 and p:
                        keep(b, p - 1)
                    n = p * KT + kt
                    act.wait_ge(pca_used, b * (PAIRS1 * KT) + max(n - SLOTS + 1, 0) + 1)
                    R1.wait_full(act, b, "csT", p, kt)
                    R1.read(nc.scalar.activation(PCA[:, n % SLOTS, 0:PC], R1.bank("csT", p, kt)[:, 0:PC], ACT.Exp,
                                                 scale=SCALE1), "csT", p, kt)

            def channel_end(b):
                keep(b, PAIRS1 - 1)

            def tokens_back(b):
                for c in range(2):
                    R1.wait_full(act, b, "cnT", c)
                    bk = R1.bank("cnT", c)[:, 0:3 * CH].rearrange("p (t c) -> p t c", t=3)
                    nc.scalar.copy(hsT[:, c, 0:2], bk[:, 0:2]).then_inc(act_ca, 1)
                    R1.read(nc.scalar.copy(hsT[0:FT[2], c, 2], bk[0:FT[2], 2]), "cnT", c)

            def token_softmax(b):
                R1.wait_read(act, b, "cs3")
                nc.scalar.activation(e3[:], d3[:], ACT.Exp, scale=SCALE1).then_inc(act_ca, 1)

            def spread(b):
                for s in range(2):
                    R1.wait_full(act, b, "cexp", s)
                    R1.read(nc.scalar.copy(P3S[:, s], R1.bank("cexp", s)[0:96]), "cexp", s)

            run(act, {"handover": handover, "split0": split0, "split1": split1, "project0": project0, "shift0": shift0,
                      "attend0": attend0, "split_o0": split_o0, "project1": project1, "naturals": naturals,
                      "shift1": shift1, "scores1": scores1, "values1": values1, "split_o1": split_o1,
                      "channel_shift": channel_shift, "channel_values": channel_values, "channel_end": channel_end,
                      "tokens_back": tokens_back, "token_softmax": token_softmax, "spread": spread})

        @block.vector
        def _(dve):
            dve.wait_ge(early_here, 16 * len(CONSTS))

            def project0(b, s, t):
                dve.wait_ge(q0_hi, (b * 2 + s) * 3 + (t + 1))
                r = slice(0, P) if t < 2 else slice(FT[2], P)
                dst = q0L[:, t] if t < 2 else q0H[r, t]
                R0.read(nc.vector.tensor_tensor(dst, R0.bank("q", s, t)[r], q0H[r, t].bitcast(F32), ALU.subtract),
                        "q", s, t)

            def maxima0(b, s, qt):
                if qt == 0:
                    R0.wait_before(dve, b, s, "maxT", 0)
                for t in range(2):
                    R0.wait_full(dve, b, "max", s, qt, t)
                    R0.read(nc.vector.tensor_reduce(
                        nmax0[:, qt, 8 * t:8 * t + 8],
                        R0.bank("max", s, qt, t)[:].rearrange("p (h k) -> p h k", k=NK), axis=AX.X, op=ALU.max,
                        negate=True), "max", s, qt, t)
                if qt % 2 == 0:
                    return
                qp = qt // 2
                R0.wait_full(dve, b, "max2", s, qp)
                R0.read(nc.vector.tensor_reduce(
                    nmax0[:, 2 * qp:2 * qp + 2, 16:H0],
                    R0.bank("max2", s, qp)[:].rearrange("p (q h k) -> p q h k", q=2, k=NK), axis=AX.X, op=ALU.max,
                    negate=True), "max2", s, qp)

            def reciprocals0(b, s):
                dve.wait_ge(sums0_done, (b * 2 + s) * 4 + 3 + 1)
                nc.vector.reciprocal(rec0[:], sums0[:, 0:P]).then_inc(sums0_read, 1)

            def normalize0(b, s):
                u = b * 2 + s
                R0.wait_read(dve, b, "pv", s, 2)
                for c in range(QT):
                    o = o0[:, :, P * c:P * c + P]
                    if c < QT - 1:
                        R0.wait_full(dve, b, "rec", s, c)
                        rec = R0.bank("rec", s, c)[:, 0:3 * P]
                    else:
                        dve.wait_ge(sums0_done, u * 4 + 4 + 1)
                        rec = sums0[:, P:4 * P]
                    ins = nc.vector.tensor_tensor(o, o, rec.rearrange("p (t c) -> p t c", t=3), ALU.mult)
                    if c < QT - 1:
                        R0.read(ins, "rec", s, c)
                    else:
                        ins.then_inc(sums0_read, 1)

            def split_o0(b, s):
                u = b * 2 + s
                for t in range(3):
                    dve.wait_ge(o0_hi, u * 3 + (t + 1))
                    dst = q0L[:, t] if t < 2 else q0H[64:P, 2]
                    r = slice(0, P) if t < 2 else slice(64, P)
                    nc.vector.tensor_tensor(dst, o0[r, t], q0H[r, t].bitcast(F32), ALU.subtract).then_inc(o0_lo, 1)

            def output0(b, s, t):
                R0.wait_full(dve, b, "wo", s, t)
                x = X[:, t, half(s)]
                R0.read(nc.vector.scalar_tensor_tensor(x, R0.bank("wo", s, t)[:], bo0[:, t:t + 1], x, ALU.add, ALU.add),
                        "wo", s, t)

            def split1(b, s):
                dve.wait_ge(x1_hi, b * 2 + (s + 1))
                nc.vector.tensor_tensor(X1L[:], X[:, 0:2, half(s)], X1H[:, 0:2].bitcast(F32), ALU.subtract)\
                    .then_inc(x1_lo, 1)
                nc.vector.tensor_tensor(X1H[64:P, 2], X[64:P, 2, half(s)], X1H[64:P, 2].bitcast(F32), ALU.subtract)\
                    .then_inc(x1_lo, 1)

            def project1(b, s, t):
                dve.wait_ge(q1_hi, (b * 2 + s) * 3 + (t + 1))
                R1.read(nc.vector.tensor_tensor(q1L[:, t], R1.bank("q", s, t)[:], q1H[:, t].bitcast(F32),
                                                ALU.subtract), "q", s, t)

            def maxima1(b, s, qt):
                if qt == 0:
                    R1.wait_before(dve, b, s, "maxT", 0)
                R1.wait_full(dve, b, "max", s, qt)
                R1.read(nc.vector.tensor_reduce(
                    nmax1[:, qt], R1.bank("max", s, qt)[:].rearrange("p (h k) -> p h k", k=NK)[:, :, 0:K1],
                    axis=AX.X, op=ALU.max, negate=True), "max", s, qt)

            def reciprocals1(b, s):
                dve.wait_ge(sums1_done, (b * 2 + s) * 2 + 1)
                nc.vector.reciprocal(rec1[:], sums1[:, 0:P]).then_inc(sums1_read, 1)

            def normalize1(b, s):
                u = b * 2 + s
                R1.wait_read(dve, b, "pv", s, 2)
                for c in range(QT):
                    o = o1[:, :, P * c:P * c + P]
                    if c < QT - 1:
                        R1.wait_full(dve, b, "rec", s, c)
                        rec = R1.bank("rec", s, c)[:, 0:3 * P]
                    else:
                        dve.wait_ge(sums1_done, u * 2 + 2)
                        rec = sums1[:, P:4 * P]
                    ins = nc.vector.tensor_tensor(o, o, rec.rearrange("p (t c) -> p t c", t=3), ALU.mult)
                    if c < QT - 1:
                        R1.read(ins, "rec", s, c)
                    else:
                        ins.then_inc(sums1_read, 1)

            def split_o1(b, s):
                u = b * 2 + s
                for t in range(3):
                    dve.wait_ge(o1_hi, u * 3 + (t + 1))
                    nc.vector.tensor_tensor(q1L[:, t], o1[:, t], q1H[:, t].bitcast(F32), ALU.subtract)\
                        .then_inc(o1_lo, 1)

            def output1(b, s, t):
                r = FT[t]
                R1.wait_full(dve, b, "wo", s, t)
                x = x1T[0:r, t, half(s)]
                R1.read(nc.vector.scalar_tensor_tensor(x, R1.bank("wo", s, t)[0:r], bo1[0:r, t:t + 1], x, ALU.add,
                                                       ALU.add), "wo", s, t)

            def channel_maxima(b, part):
                for m in tiles_of_part(part):
                    for s in range(2):
                        R1.wait_full(dve, b, "cmax", m, s)
                        R1.read(nc.vector.tensor_reduce(cmax2[:, m, s:s + 1], R1.bank("cmax", m, s)[:], axis=AX.X,
                                                        op=ALU.max), "cmax", m, s)

            def channel_shift(b):
                R1.wait_read(dve, b, "cmax", HC // P - 1, 1)
                nc.vector.tensor_reduce(cmax[:], cmax2[:], axis=AX.X, op=ALU.max, negate=True).then_inc(cmax_ready, 1)

            def link(ins, b, k):
                ins.then_inc(dve_ca, 1)
                dve.wait_ge(dve_ca, b * DVE_CA + k)

            def tokens(b):
                for c in range(2):
                    R1.wait_full(dve, b, "cnat", c)
                    bk = R1.bank("cnat", c)[0:CH].rearrange("p (h d) -> p h d", h=H1)
                    link(nc.vector.reciprocal(crec[:, c].unsqueeze(2), bk[:, :, D1:D1 + 1]), b, c + 1)
                    R1.read(nc.vector.tensor_tensor(hs[:, c], bk[:, :, 0:D1],
                                                    crec[:, c].unsqueeze(2).to_broadcast([CH, H1, D1]), ALU.mult),
                            "cnat", c)

            def token_scores(b):
                R1.wait_full(dve, b, "cs3")
                sc = R1.bank("cs3")[0:CH, 0:2 * HT].rearrange("p (c h t) -> p c h t", c=2, t=T)
                link(nc.vector.tensor_reduce(m3[:], sc, axis=AX.X, op=ALU.max), b, 3)
                R1.read(nc.vector.tensor_tensor(d3[:], sc, m3[:].unsqueeze(3).to_broadcast([CH, 2, H1, T]),
                                                ALU.subtract), "cs3")

            def token_softmax(b):
                dve.wait_ge(act_ca, b * ACT_CA + ACT_CA)
                link(nc.vector.tensor_reduce(s3[:], e3[:], axis=AX.X, op=ALU.add), b, 4)
                link(nc.vector.reciprocal(r3[:], s3[:]), b, 5)
                link(nc.vector.tensor_tensor(p3[:], e3[:], r3[:].unsqueeze(3).to_broadcast([CH, 2, H1, T]), ALU.mult),
                     b, 6)
                pf = p3[:].rearrange("p c h t -> p c (h t)")
                link(nc.vector.tensor_copy(P3[:, :, 0], pf), b, 7)
                link(nc.vector.tensor_copy(P3[:, :, 2], pf), b, 8)
                link(nc.vector.tensor_tensor(P3[:, :, 1], pf, P3[:, :, 0].bitcast(F32), ALU.subtract), b, 9)

            def final(b, s):
                for t in range(3):
                    r = FT[t]
                    x = x1T[0:r, t, half(s)]
                    R1.wait_full(dve, b, "fin", s, t)
                    R1.read(nc.vector.tensor_tensor(x, R1.bank("fin", s, t)[0:r], x, ALU.add), "fin", s, t)

            run(dve, {"reciprocals0": reciprocals0, "reciprocals1": reciprocals1, "split_o0": split_o0,
                      "split_o1": split_o1, "split1": split1, "project0": project0, "maxima0": maxima0,
                      "normalize0": normalize0, "output0": output0, "project1": project1, "maxima1": maxima1,
                      "normalize1": normalize1, "output1": output1, "channel_maxima": channel_maxima,
                      "channel_shift": channel_shift, "tokens": tokens, "token_scores": token_scores,
                      "token_softmax": token_softmax, "final": final})

        @block.tensor
        def _(pe):
            pe.wait_ge(early_here, 16 * len(CONSTS))

            def products(ring, b, name, rows, parts, cols=HALF, lo=None):
                ring.wait_free(pe, b, *name)
                for i, (lhsT, rhs) in enumerate(parts):
                    if lo and i == lo[0]:
                        pe.wait_ge(lo[1], lo[2])
                    last = nc.tensor.matmul(ring.bank(*name)[0:rows, 0:cols], lhsT, rhs, start=(i == 0),
                                            stop=(i == len(parts) - 1))
                ring.filled(last, *name)

            def split_parts(WH, WL, XH, XL, m):
                return ([(W[:, k, m], XH[:, k]) for W in (WH, WL) for k in range(2)] + [(WL[0:64, 2, m], XH[0:64, 2])]
                        + [(WH[:, 2, m], XH[:, 2])] + [(WH[:, k, m], XL[:, k]) for k in range(2)])

            def project0(b, s, t):
                u = b * 2 + s
                if t == 0:
                    pe.wait_ge(x_hi, u + 1)
                products(R0, b, ("q", s, t), P, split_parts(WqH, WqL, XH, XL, slice(P * t, P * t + P)),
                         lo=None if t else (5, x_lo, u * 2 + 2))

            def maxima0(b, s, qt):
                if qt == 0:
                    pe.wait_ge(q0_hi, (b * 2 + s) * 3 + 3)
                    pe.wait_ge(pack0_here, b * 32 + 32)
                    pe.wait_ge(blocks0_ready, b * 6 + 6)
                for t in range(2):
                    products(R0, b, ("max", s, qt, t), P,
                             [(q0H[:, t, P * qt:P * qt + P], KB0H[:, 8 * t:8 * t + 8].rearrange("p h k -> p (h k)"))])
                if qt % 2 == 0:
                    return
                qp = qt // 2
                R0.wait_free(pe, b, "max2", s, qp)
                for i in range(2):
                    qt = 2 * qp + i
                    last = nc.tensor.matmul(R0.bank("max2", s, qp)[:, 256 * i:256 * i + 256],
                                            q0H[0:64, 2, P * qt:P * qt + P],
                                            KB0H[0:64, 16:H0].rearrange("p h k -> p (h k)"), start=True, stop=True)
                R0.filled(last, "max2", s, qp)

            def shift0(b, s):
                R0.wait_read(pe, b, "max2", s, QT // 2 - 1)
                R0.wait_free(pe, b, "maxT", s)
                for qt in range(QT):
                    last = nc.tensor.transpose(R0.bank("maxT", s)[0:H0, P * qt:P * qt + P], nmax0[:, qt], ident[:])
                R0.filled(last, "maxT", s)

            def attend0(b, s, part):
                u = b * 2 + s
                if part == 0:
                    pe.wait_ge(sums0_read, u * 2 + 1)
                    R0.wait_read(pe, b, "maxT", s)

                def scores(p):
                    t = p // GROUP
                    kh = KB0H[:, 2 * p:2 * p + 2].rearrange("p h k -> p (h k)")
                    kl = KB0L[:, 2 * p:2 * p + 2].rearrange("p h k -> p (h k)")
                    parts = ([(kh, q0H[:, t]), (kh, q0L[:, t]), (kl, q0H[:, t])] if t < 2 else
                             [(kh, q0H[:, t]), (kl[0:FT[2]], q0H[0:FT[2], t])])
                    products(R0, b, ("sT", s, p), P, parts + [(ones0[:, p], nmaxT0[:])])

                def values(t):
                    R0.wait_read(pe, b, "sT", s, pairs_of(t)[-1])
                    R0.wait_free(pe, b, "pv", s, t)
                    for j in range(GROUP):
                        p = GROUP * t + j % len(pairs_of(t))
                        last = nc.tensor.matmul(R0.bank("pv", s, t)[32 * j:32 * j + 32], V0[:, 32 * p:32 * p + 32],
                                                P0[:, p % SLOTS], start=True, stop=True)
                    R0.filled(last, "pv", s, t)
                    for p in pairs_of(t):
                        for c in range(QT):
                            last = nc.tensor.matmul(sums0[32 * c:32 * c + 32, 0:P], OH0[:, p],
                                                    P0[:, p % SLOTS, P * c:P * c + P], start=(p == 0),
                                                    stop=(p == PAIRS0 - 1))
                    last.then_inc(sums0_done, 1)

                for what, i in ATTEND0[part]:
                    if what == "pv":
                        values(i)
                    else:
                        scores(i)

            def normalize0(b, s):
                u = b * 2 + s
                pe.wait_ge(sums0_read, u * 2 + 1 + 1)
                for c in range(QT):
                    if c < QT - 1:
                        R0.wait_free(pe, b, "rec", s, c)
                        dst = R0.bank("rec", s, c)[:, 0:3 * P]
                    else:
                        dst = sums0[:, P:4 * P]
                    for t in range(3):
                        last = nc.tensor.matmul(dst[:, P * t:P * t + P], E0[32 * c:32 * c + 32, P * t:P * t + P],
                                                rec0[32 * c:32 * c + 32], start=True, stop=True)
                    if c < QT - 1:
                        R0.filled(last, "rec", s, c)
                    else:
                        last.then_inc(sums0_done, 1)

            def output0(b, s, t):
                u = b * 2 + s
                if t == 0:
                    pe.wait_ge(o0_hi, u * 3 + 3)
                products(R0, b, ("wo", s, t), P, split_parts(WoH, WoL, q0H, q0L, slice(P * t, P * t + P)),
                         lo=None if t else (5, o0_lo, u * 3 + 3))

            def project1(b, s, t):
                u = b * 2 + s
                if t == 0:
                    pe.wait_ge(x1_hi, u + 1)
                products(R1, b, ("q", s, t), P, split_parts(W1H, W1L, X1H, X1L, slice(TILE1 * t, TILE1 * t + P)),
                         lo=None if t else (5, x1_lo, u * 2 + 2))

            def naturals(b, s, qt):
                if qt == 0:
                    pe.wait_ge(x1_here, b * 2 + (s + 2))
                R1.wait_free(pe, b, "xn", s, qt)
                for t in range(3):
                    r = FT[t]
                    last = nc.tensor.transpose(R1.bank("xn", s, qt)[:, P * t:P * t + r],
                                               x1T[0:r, t, s * HALF + P * qt:s * HALF + P * qt + P], ident[0:r, 0:r])
                R1.filled(last, "xn", s, qt)

            def maxima1(b, s, qt):
                if qt == 0:
                    pe.wait_ge(q1_hi, (b * 2 + s) * 3 + 3)
                    pe.wait_ge(pack1_here, b * 80 + 80)
                    pe.wait_ge(blocks1_ready, b * 7 + 7)
                R1.wait_free(pe, b, "max", s, qt)
                for t in range(3):
                    n = HEADS1[t] * NK
                    first = SLOTS1.index((t, HEAD1[t]))
                    last = nc.tensor.matmul(R1.bank("max", s, qt)[:, 192 * t:192 * t + n],
                                            q1H[:, t, P * qt:P * qt + P],
                                            KB1H[:, first:first + HEADS1[t]].rearrange("p h k -> p (h k)"), start=True,
                                            stop=True)
                R1.filled(last, "max", s, qt)

            def shift1(b, s):
                R1.wait_read(pe, b, "max", s, QT - 1)
                R1.wait_free(pe, b, "maxT", s)
                for qt in range(QT):
                    last = nc.tensor.transpose(R1.bank("maxT", s)[0:H1, P * qt:P * qt + P], nmax1[:, qt], ident[:])
                R1.filled(last, "maxT", s)

            def scores1(b, s, p):
                if p == 0:
                    R1.wait_read(pe, b, "maxT", s)
                parts = []
                for i, (t, pair) in enumerate(COMBOS):
                    if pair == p:
                        kh = KB1H[:, 2 * i:2 * i + 2].rearrange("p h k -> p (h k)")
                        kl = KB1L[:, 2 * i:2 * i + 2].rearrange("p h k -> p (h k)")
                        parts += [(kh, q1H[:, t]), (kh, q1L[:, t]), (kl, q1H[:, t])]
                products(R1, b, ("sT", s, p), P, parts + [(ones1[:, p], nmaxT1[:])])

            def values1(b, s):
                R1.wait_read(pe, b, "sT", s, PAIRS1 - 1)
                for t in range(3):
                    products(R1, b, ("pv", s, t), P, [(V1[:, i], P1[:, p]) for i, (tt, p) in enumerate(COMBOS)
                                                      if tt == t])
                pe.wait_ge(sums1_read, b * USES1 + 2 * s + 1)
                for p in range(PAIRS1):
                    for c in range(QT):
                        last = nc.tensor.matmul(sums1[32 * c:32 * c + 32, 0:P], OH1[:, p], P1[:, p, P * c:P * c + P],
                                                start=(p == 0), stop=(p == PAIRS1 - 1))
                last.then_inc(sums1_done, 1)

            def normalize1(b, s):
                pe.wait_ge(sums1_read, b * USES1 + (2 * s + 1) + 1)
                for c in range(QT):
                    if c < QT - 1:
                        R1.wait_free(pe, b, "rec", s, c)
                        dst = R1.bank("rec", s, c)[:, 0:3 * P]
                    else:
                        dst = sums1[:, P:4 * P]
                    for t in range(3):
                        last = nc.tensor.matmul(dst[:, P * t:P * t + P], E1[32 * c:32 * c + 32, P * t:P * t + P],
                                                rec1[32 * c:32 * c + 32], start=True, stop=True)
                    if c < QT - 1:
                        R1.filled(last, "rec", s, c)
                    else:
                        last.then_inc(sums1_done, 1)

            def output1(b, s, t):
                u = b * 2 + s
                if t == 0:
                    pe.wait_ge(o1_hi, u * 3 + 3)
                m = slice(P * t, P * t + FT[t])
                parts = [(W[:, k, m], o[:, k]) for W, o in ((W2H, q1H), (W2L, q1H), (W2H, q1L)) for k in range(3)]
                products(R1, b, ("wo", s, t), FT[t], parts, lo=None if t else (6, o1_lo, u * 3 + 3))

            def channel_maxima(b, part):
                pe.wait_ge(gs_here, b * 96 + 96 + 1)
                for m in tiles_of_part(part):
                    for s in range(2):
                        products(R1, b, ("cmax", m, s), P, [(CAS[0:3 * HT, P * m:P * m + P], GS[0:3 * HT, half(s)])])

            def channel_shift(b):
                pe.wait_ge(cmax_ready, b + 1)
                R1.wait_free(pe, b, "cmaxT")
                R1.filled(nc.tensor.transpose(R1.bank("cmaxT")[0:HC // P, 0:P], cmax[:], ident[:]), "cmaxT")

            def used(b, n):
                p, kt = n // KT, n % KT
                if kt == 0:
                    pe.wait_ge(sums1_read, b * USES1 + (4 + p) + 1)
                R1.wait_read(pe, b, "csT", p, kt)
                for i in range(2):
                    head = XW * (2 * p + i)
                    last = nc.tensor.matmul(sums1[64 * i:64 * i + 64, 0:C], X1N[:, kt, head:head + 64],
                                            PCA[:, n % SLOTS, C * i:C * i + C], start=(kt == 0), stop=(kt == KT - 1))
                last.then_inc(pca_used, 1)

            def channel_values(b, p, quarter):
                if p == 0 and quarter == 0:
                    pe.wait_ge(cas_here, b * 16 + 16)
                for kt in kts_of(quarter):
                    n = p * KT + kt
                    products(R1, b, ("csT", p, kt), P, [(GS[:, P * kt:P * kt + P], CAS[:, PC * p:PC * p + PC])], PC)
                    if n >= 2:
                        used(b, n - 2)

            def channel_end(b):
                used(b, PAIRS1 * KT - 2)
                used(b, PAIRS1 * KT - 1)

            def tokens(b):
                pe.wait_ge(sums1_read, b * USES1 + USES1 + 1)
                for c in range(2):
                    R1.wait_free(pe, b, "cnat", c)
                    for p in range(PAIRS1):
                        last = nc.tensor.transpose(R1.bank("cnat", c)[0:CH, P * p:P * p + P],
                                                   CO[:, p, CH0[c]:CH0[c] + CH], ident[:])
                    R1.filled(last, "cnat", c)

            def tokens_back(b):
                for c in range(2):
                    R1.wait_read(pe, b, "cnat", c)
                    R1.wait_free(pe, b, "cnT", c)
                    for t in range(3):
                        r = FT[t]
                        last = nc.tensor.transpose(R1.bank("cnT", c)[0:r, CH * t:CH * t + CH],
                                                   hs[:, c].rearrange("p h d -> p (h d)")[:, P * t:P * t + r],
                                                   ident[0:CH, 0:CH])
                    R1.filled(last, "cnT", c)

            def token_scores(b):
                R1.wait_free(pe, b, "cs3")
                for c in range(2):
                    R1.wait_read(pe, b, "cnT", c)
                    for t in range(3):
                        r = FT[t]
                        last = nc.tensor.matmul(R1.bank("cs3")[0:CH, HT * c:HT * c + HT], hsT[0:r, c, t], A3[0:r, t],
                                                start=(t == 0), stop=(t == 2))
                R1.filled(last, "cs3")

            def spread(b):
                pe.wait_ge(dve_ca, b * DVE_CA + DVE_CA)
                for s in range(2):
                    products(R1, b, ("cexp", s), 96, [(P3[:, s].rearrange("p g k -> p (g k)"), EX[:, s])])

            def final(b, s):
                R1.wait_read(pe, b, "cexp", s)
                for t in range(3):
                    products(R1, b, ("fin", s, t), FT[t], [(VW[:, P * t:P * t + FT[t]], P3S[:, s])])

            run(pe, {"project0": project0, "maxima0": maxima0, "shift0": shift0, "attend0": attend0,
                     "normalize0": normalize0, "output0": output0, "project1": project1, "naturals": naturals,
                     "maxima1": maxima1, "shift1": shift1, "scores1": scores1, "values1": values1,
                     "normalize1": normalize1, "output1": output1, "channel_maxima": channel_maxima,
                     "channel_shift": channel_shift, "channel_values": channel_values, "channel_end": channel_end,
                     "tokens": tokens, "tokens_back": tokens_back, "token_scores": token_scores, "spread": spread,
                     "final": final})


def program(nc, a, out):
    shapes = {"KT": [2, P, 2, 3, NK], "TOK": [3 * HT, C], "V0": [P, F], "V1": [P, len(COMBOS), P], "A3": [P, 3, HT],
              "VW": [3 * HT, F]}
    scr = {k: nc.dram_tensor(f"scratch_{k}", [B] + s, F32, kind="Internal").ap() for k, s in shapes.items()}
    with ExitStack() as ctx:
        w = {}
        for k, n in (("Wq0", 3 * P), ("Wo0", 3 * P), ("W1", 368), ("W2", F)):
            for part in "HL":
                w[k + part] = ctx.enter_context(nc.sbuf_tensor(f"{k}{part}", [P, 3, n], F32R))
        w["EX"] = ctx.enter_context(nc.sbuf_tensor("EX_split", [CH, 2, HALF], F32R))
        w["ones0"] = ctx.enter_context(nc.sbuf_tensor("ones0_sb", [H0, PAIRS0, P], F32R))
        w["ones1"] = ctx.enter_context(nc.sbuf_tensor("ones1_sb", [H1, PAIRS1, P], F32R))
        early = {k: ctx.enter_context(nc.sbuf_tensor(f"{k}_sb", list(a[k].shape), F32)) for k in CONSTS}
        early["X"] = ctx.enter_context(nc.sbuf_tensor("X_sb", [P, 3, S], F32))
        early["GS"] = ctx.enter_context(nc.sbuf_tensor("GS_sb", [97, S], F32R))
        early["X1N"] = ctx.enter_context(nc.sbuf_tensor("X1N_sb", [P, KT, H1 * XW + 64 - XW], F32))
        early["CO"] = ctx.enter_context(nc.sbuf_tensor("CO_sb", [P, PAIRS1, C], F32))
        early_here = ctx.enter_context(nc.semaphore("early_here"))
        x_here = [ctx.enter_context(nc.semaphore(f"x_here{s}")) for s in range(2)]
        prologue(nc, a, scr, w, early, early_here, x_here)
        layers(nc, a, scr, w, early, early_here, x_here, out)



def tiles(x, sizes, rows=P, at=None):
    import numpy as np
    out = np.zeros((rows, len(sizes)) + x.shape[1:], np.float32)
    r = 0
    for t, n in enumerate(sizes):
        out[0:n, t] = x[r:r + n]
        r += n
    return out


def doubled(x):
    import numpy as np
    return tiles(np.concatenate([x, x[2 * P:]], 0), [P, P, P])


def shape_constants():
    import numpy as np
    f = np.float32
    c = {}
    part = np.arange(P)
    c["ident"] = np.eye(P, dtype=f)
    head = np.arange(H0)
    row = np.where(head[None] < 16, part[:, None], part[:, None] % FT[2]) // D0
    c["mKB0"] = (row == head[None] % 8).astype(f)
    k1 = np.zeros((P, len(SLOTS1)), f)
    m8 = np.zeros((P, 3, H1), f)
    for t in range(3):
        for j in range(HEADS1[t]):
            k1[D1 * j:D1 * j + D1, SLOTS1.index((t, HEAD1[t] + j))] = 1
            m8[D1 * j:D1 * j + D1, t, 3 * t + j] = 1
    c["mKB1"], c["m8"] = k1, m8
    c["mCAS"] = ((np.arange(3 * HT)[:, None] % HT) // T == np.arange(H1)[None]).astype(f)
    feat = np.arange(F)
    c["mV0"] = ((feat[None] // D0) % 2 == part[:, None] // NK).astype(f)
    v1 = np.zeros((P, len(COMBOS), P), f)
    for i, (t, p) in enumerate(COMBOS):
        for m in range(ROWS1[t]):
            h = 3 * t + m // D1
            if h // 2 == p:
                v1[NK * (h % 2):NK * (h % 2) + K1, i, m] = 1
    c["mV1"] = v1
    ones0 = np.zeros((H0, PAIRS0, 2, NK), f)
    for h in range(H0):
        ones0[h, h // 2, h % 2] = 1
    c["ones0"] = ones0.reshape(H0, PAIRS0, P)
    ones1 = np.zeros((H1, PAIRS1, 2, NK), f)
    for h in range(H1):
        ones1[h, h // 2, h % 2, 0:K1] = 1
    c["ones1"] = ones1.reshape(H1, PAIRS1, P)
    oh0 = np.ones((P, PAIRS0, 32), f)
    oh0[:, :, 0:H0] = 0
    oh1 = np.ones((P, PAIRS1, 32), f)
    oh1[:, :, 0:H1] = 0
    for i in range(2):
        for p in range(PAIRS0):
            oh0[NK * i:NK * i + NK, p, 2 * p + i] = 1
        for p in range(PAIRS1):
            oh1[NK * i:NK * i + K1, p, 2 * p + i] = 1
    c["OH0"], c["OH1"] = oh0, oh1
    e0, e1 = np.zeros((P, 3 * P), f), np.zeros((P, 3 * P), f)
    doubled_feature = np.concatenate([feat, feat[2 * P:]])
    for q in range(QT):
        for m, ft in enumerate(doubled_feature):
            e0[32 * q + ft // D0, m] = 1
        for t in range(3):
            for m in range(ROWS1[t]):
                e1[32 * q + HEAD1[t] + m // D1, P * t + m] = 1
    c["E0"], c["E1"] = e0, e1
    channel = np.linspace(0, C - 1, S).astype(np.int64)
    ex = np.zeros((CH, 2, HALF), f)
    for i in range(S):
        ex[channel[i] - CH0[i // HALF], i // HALF, i % HALF] = 1
    c["EX"] = ex
    return c


def kernel(x, ctx_768, L0_xattn_Wq, L0_xattn_Wk, L0_xattn_Wv, L0_xattn_Wo, L0_xattn_bo, L1_xattn_Wq, L1_xattn_Wk,
           L1_xattn_Wv, L1_xattn_Wq_ca, L1_xattn_Wk_ca, L1_xattn_Wv_ca, L1_xattn_Wout, L1_xattn_b_out):
    import numpy as np
    import concourse.bacc as bacc
    from concourse.bass_utils import run_bass_kernel_spmd

    def host(v):
        return np.asarray(v)

    x, ctx = host(x), host(ctx_768)
    Wq1 = host(L1_xattn_Wq)
    arrays = shape_constants()
    arrays["xT"] = doubled(x.reshape(B * S, F).T)
    ctxT = ctx.transpose(2, 0, 1).reshape(2, KC, B, NK).transpose(1, 0, 2, 3)
    arrays["ctxD"] = np.concatenate([ctxT, ctxT], 3)

    def context_rows(w):
        return w.reshape(2, KC, w.shape[1]).transpose(1, 0, 2)

    def wide(w):
        return np.concatenate([w, w[:, 2 * P:]], 1)

    arrays["Wk0"] = context_rows(wide(host(L0_xattn_Wk)))
    wk1 = np.zeros((C, 368), np.float32)
    wk1[:, 0:F] = host(L1_xattn_Wk)
    arrays["Wk1"] = context_rows(wk1)
    arrays["Wv0"], arrays["Wv1"] = context_rows(host(L0_xattn_Wv)), context_rows(host(L1_xattn_Wv))
    arrays["Wkca"], arrays["Wvca"] = context_rows(host(L1_xattn_Wk_ca)), context_rows(host(L1_xattn_Wv_ca))
    arrays["Wq0"] = doubled(wide(host(L0_xattn_Wq)))
    arrays["Wo0"] = doubled(wide(host(L0_xattn_Wo)))
    w1 = np.zeros((F, 368), np.float32)
    w1[:, 0:F] = Wq1
    wca = host(L1_xattn_Wq_ca)
    for h in range(H1):
        for t in range(T):
            w1[D1 * h:D1 * h + D1, 336 + T * h + t] = wca[t, D1 * h:D1 * h + D1]
    arrays["W1"] = doubled(w1)
    arrays["Wq1T"] = tiles(Wq1.T, ROWS1)
    arrays["W2"] = tiles(host(L1_xattn_Wout), ROWS1)
    arrays["tok"] = np.tile(ctx[:, K1:].transpose(1, 0, 2), (3 * H1, 1, 1))
    for name, bias in (("bo0", L0_xattn_bo), ("bo1", L1_xattn_b_out)):
        arrays[name] = doubled(host(bias).reshape(F, 1))[:, :, 0]

    nc = bacc.Bacc("TRN2", target_bir_lowering=False, num_devices=1)
    arrays = {k: np.ascontiguousarray(v) for k, v in arrays.items()}
    a = {k: nc.dram_tensor(f"in_{k}", v.shape, mybir.dt.from_np(v.dtype), kind="ExternalInput").ap()
         for k, v in arrays.items()}
    out = nc.dram_tensor("out_T", (P, 3, B * S), F32, kind="ExternalOutput").ap()
    program(nc, a, out)
    r = run_bass_kernel_spmd(nc, [{f"in_{k}": v for k, v in arrays.items()}], core_ids=[0])
    y = r.results[0]["out_T"].reshape(P, 3, B * S)
    y = np.concatenate([y[:, 0], y[:, 1], y[0:FT[2], 2]], 0)
    return np.ascontiguousarray(y.T).reshape(B, S, F)
```
